# Optimizing a Trainium2 kernel written in Bass

```python
import numpy as np
import jax
import jax.numpy as jnp

def _softmax(x, axis=-1):
    return jax.nn.softmax(x, axis=axis)

def _gelu(x):
    return jax.nn.gelu(x, approximate=True)

def _silu(x):
    return jax.nn.silu(x)

def _sigmoid(x):
    return jax.nn.sigmoid(x)

def _layernorm(x, axis=-1, eps=1e-05):
    m = jnp.mean(x, axis=axis, keepdims=True)
    v = jnp.var(x, axis=axis, keepdims=True)
    return (x - m) / jnp.sqrt(v + eps)

def _scatter_add(tgt, idx, src, axis=0):
    return tgt.at[idx].add(src)

def _segment_sum(src, seg, n):
    return jax.ops.segment_sum(src, seg, n)
kernel_name = 'mk_vit_tower_cls_d2_tok_img256_r4_586269'

def setup_inputs(seed: int=0):
    np.random.seed(seed)
    _w = jnp.asarray

    def _rec_inputs():
        import jax
        import jax.numpy as jnp
        _rk = jax.random.key(seed)
        x = -0.000596345 + 1.00056 * jax.random.normal(jax.random.fold_in(_rk, 1), (128, 64, 64, 3), jnp.float32)
        cls_tok = 0.02 * jax.random.normal(jax.random.fold_in(_rk, 5), (1, 1, 64), jnp.float32)
        return (x, cls_tok)
    x, cls_tok = _rec_inputs()

    def _L0_tok_setup():
        import jax, jax.numpy as jnp
        import numpy as np
        B, H, W = (16, 64, 64)
        WIDTH, LAYERS, M1, M2 = (32, 4, 12, 12)
        EPS = 1e-05

        def layer_norm(x, g, b):
            mu = jnp.mean(x, axis=-1, keepdims=True)
            var = jnp.mean((x - mu) ** 2, axis=-1, keepdims=True)
            return (x - mu) * jax.lax.rsqrt(var + EPS) * g + b

        def gelu(x):
            return jax.nn.gelu(x, approximate=False)

        def spectral_conv(x, w1, w2):
            b, c, h, w = x.shape
            x_ft = jnp.fft.rfft2(x)
            out_ft = jnp.zeros((b, w1.shape[1], h, w // 2 + 1), dtype=x_ft.dtype)
            out_ft = out_ft.at[:, :, :M1, :M2].set(jnp.einsum('bixy,ioxy->boxy', x_ft[:, :, :M1, :M2], w1))
            out_ft = out_ft.at[:, :, -M1:, :M2].set(jnp.einsum('bixy,ioxy->boxy', x_ft[:, :, -M1:, :M2], w2))
            return jnp.fft.irfft2(out_ft, s=(h, w))
        key = jax.random.key(seed)
        ks = jax.random.split(key, 16)
        scale = 1.0 / (WIDTH * WIDTH)
        d = {'x': jax.random.normal(ks[0], (B, H, W, 3), jnp.float32), 'fc0_w': jax.random.normal(ks[1], (3, WIDTH), jnp.float32) * 0.5, 'fc0_b': jnp.zeros((WIDTH,), jnp.float32), 'ln0_g': jnp.ones((WIDTH,), jnp.float32), 'ln0_b': jnp.zeros((WIDTH,), jnp.float32), 'w1r': jax.random.uniform(ks[2], (LAYERS, WIDTH, WIDTH, M1, M2), jnp.float32) * scale, 'w1i': jax.random.uniform(ks[3], (LAYERS, WIDTH, WIDTH, M1, M2), jnp.float32) * scale, 'w2r': jax.random.uniform(ks[4], (LAYERS, WIDTH, WIDTH, M1, M2), jnp.float32) * scale, 'w2i': jax.random.uniform(ks[5], (LAYERS, WIDTH, WIDTH, M1, M2), jnp.float32) * scale, 'conv_w': jax.random.normal(ks[6], (LAYERS, WIDTH, WIDTH), jnp.float32) * (1.0 / np.sqrt(WIDTH)), 'conv_b': jnp.zeros((LAYERS, WIDTH), jnp.float32), 'ln_g': jnp.ones((LAYERS, WIDTH), jnp.float32), 'ln_b': jnp.zeros((LAYERS, WIDTH), jnp.float32), 'fc1_w': jax.random.normal(ks[7], (WIDTH, 128), jnp.float32) * (1.0 / np.sqrt(WIDTH)), 'fc1_b': jnp.zeros((128,), jnp.float32), 'fc2_w': jax.random.normal(ks[8], (128, 64), jnp.float32) * (1.0 / np.sqrt(128)), 'fc2_b': jnp.zeros((64,), jnp.float32), 'fc3_w': jax.random.normal(ks[9], (64, 1), jnp.float32) * (1.0 / np.sqrt(64)), 'fc3_b': jnp.zeros((1,), jnp.float32)}
        return d
    _L0_tok_all = _L0_tok_setup()
    _L0_tok_in = {k: v for k, v in _L0_tok_all.items() if k in ('fc0_w', 'fc0_b', 'ln0_g', 'ln0_b', 'w1r', 'w1i', 'w2r', 'w2i', 'conv_w', 'conv_b', 'ln_g', 'ln_b', 'fc1_w', 'fc1_b', 'fc2_w', 'fc2_b', 'fc3_w', 'fc3_b')}
    del _L0_tok_all

    def _L0_attn_setup():
        import jax, jax.numpy as jnp
        import numpy as np
        DIM = 64
        WS = 64
        H = 8
        HD = DIM // H
        SCALE = HD ** (-0.5)
        key = jax.random.key(seed)
        k1, k2, k3, k4 = jax.random.split(key, 4)
        B, L = (8, 4096)
        x = jax.random.normal(k1, (B, L, DIM), dtype=jnp.float32)
        w_qkv = jax.random.normal(k2, (3 * DIM, DIM), dtype=jnp.float32) * DIM ** (-0.5)
        w_proj = jax.random.normal(k3, (DIM, DIM), dtype=jnp.float32) * DIM ** (-0.5)
        b_proj = jnp.zeros((DIM,), dtype=jnp.float32)
        rel_bias = jax.random.normal(k4, (2 * WS - 1,), dtype=jnp.float32) * 0.02
        return {'x': x, 'w_qkv': w_qkv, 'w_proj': w_proj, 'b_proj': b_proj, 'rel_bias': rel_bias}
    _L0_attn_all = _L0_attn_setup()
    _L0_attn_in = {k: v for k, v in _L0_attn_all.items() if k in ('w_qkv', 'w_proj', 'b_proj', 'rel_bias')}
    del _L0_attn_all

    def _L0_ffn_setup():
        import jax, jax.numpy as jnp
        import numpy as np
        E = 8
        K = 2
        D = 64
        H = 128
        DOUT = 64
        EPS = 1e-05
        key = jax.random.key(seed)
        ks = jax.random.split(key, 9)
        s = 0.02
        return {'x': jax.random.normal(ks[0], (4, 2048, D), jnp.float32), 'gamma': 1.0 + 0.05 * jax.random.normal(ks[1], (D,), jnp.float32), 'beta': 0.05 * jax.random.normal(ks[2], (D,), jnp.float32), 'Wr': 0.01 * jax.random.normal(ks[3], (D, E), jnp.float32), 'br': jnp.zeros((E,), jnp.float32), 'W1': s * jax.random.normal(ks[4], (E, D, H), jnp.float32), 'b1': s * jax.random.normal(ks[5], (E, H), jnp.float32), 'W2': s * jax.random.normal(ks[6], (E, H, DOUT), jnp.float32), 'b2': s * jax.random.normal(ks[7], (E, DOUT), jnp.float32)}
    _L0_ffn_all = _L0_ffn_setup()
    _L0_ffn_in = {k: v for k, v in _L0_ffn_all.items() if k in ('gamma', 'beta', 'Wr', 'br', 'W1', 'b1', 'W2', 'b2')}
    del _L0_ffn_all

    def _L1_attn_setup():
        import jax, jax.numpy as jnp
        import numpy as np
        DIM = 64
        HEADS = 4
        DIM_HEAD = 32
        NUM_MEM = 4
        HIDDEN = HEADS * DIM_HEAD
        SCALE = DIM_HEAD ** (-0.5)

        def rmsnorm(x, g):
            n = jnp.linalg.norm(x, axis=-1, keepdims=True)
            return x / jnp.maximum(n, 1e-12) * g * x.shape[-1] ** 0.5
        key = jax.random.key(seed)
        ks = jax.random.split(key, 8)
        B, N = (4, 4096)
        return {'x': jax.random.normal(ks[0], (B, N, DIM), jnp.float32), 't': jax.random.normal(ks[1], (B,), jnp.float32), 'w_qkv': jax.random.normal(ks[2], (DIM, 3 * HIDDEN), jnp.float32) * 0.02, 'mem_kv': jax.random.normal(ks[3], (2, HEADS, DIM_HEAD, NUM_MEM), jnp.float32), 'w_out': jax.random.normal(ks[4], (HIDDEN, DIM), jnp.float32) * 0.02, 'b_out': jnp.zeros((DIM,), jnp.float32), 'g_out': jnp.ones((DIM,), jnp.float32), 'g_pre': jnp.ones((DIM,), jnp.float32)}
    _L1_attn_all = _L1_attn_setup()
    _L1_attn_in = {k: v for k, v in _L1_attn_all.items() if k in ('t', 'w_qkv', 'mem_kv', 'w_out', 'b_out', 'g_out', 'g_pre')}
    del _L1_attn_all

    def _L1_ffn_setup():
        import jax, jax.numpy as jnp
        import numpy as np
        C = 64
        HID = 256
        E = 8
        TEMP = 1.0
        key = jax.random.key(seed)
        ks = jax.random.split(key, 7)
        x = jax.random.normal(ks[0], (8, 4096, C), dtype=jnp.float32)
        W1 = jax.random.normal(ks[1], (C, HID), dtype=jnp.float32) * 0.02
        b1 = jnp.zeros((HID,), dtype=jnp.float32)
        Wg = jax.random.normal(ks[2], (HID, E), dtype=jnp.float32) * 0.02
        bg = jnp.zeros((E,), dtype=jnp.float32)
        Wd = jax.random.normal(ks[3], (E, HID, C), dtype=jnp.float32) * 0.02
        bd = jnp.zeros((E, C), dtype=jnp.float32)
        return {'x': x, 'W1': W1, 'b1': b1, 'Wg': Wg, 'bg': bg, 'Wd': Wd, 'bd': bd}
    _L1_ffn_all = _L1_ffn_setup()
    _L1_ffn_in = {k: v for k, v in _L1_ffn_all.items() if k in ('W1', 'b1', 'Wg', 'bg', 'Wd', 'bd')}
    del _L1_ffn_all
    return {'x': x, 'cls_tok': cls_tok, 'L0_tok_fc0_w': _L0_tok_in['fc0_w'], 'L0_tok_fc0_b': _L0_tok_in['fc0_b'], 'L0_tok_ln0_g': _L0_tok_in['ln0_g'], 'L0_tok_ln0_b': _L0_tok_in['ln0_b'], 'L0_tok_w1r': _L0_tok_in['w1r'], 'L0_tok_w1i': _L0_tok_in['w1i'], 'L0_tok_w2r': _L0_tok_in['w2r'], 'L0_tok_w2i': _L0_tok_in['w2i'], 'L0_tok_conv_w': _L0_tok_in['conv_w'], 'L0_tok_conv_b': _L0_tok_in['conv_b'], 'L0_tok_ln_g': _L0_tok_in['ln_g'], 'L0_tok_ln_b': _L0_tok_in['ln_b'], 'L0_tok_fc1_w': _L0_tok_in['fc1_w'], 'L0_tok_fc1_b': _L0_tok_in['fc1_b'], 'L0_tok_fc2_w': _L0_tok_in['fc2_w'], 'L0_tok_fc2_b': _L0_tok_in['fc2_b'], 'L0_tok_fc3_w': _L0_tok_in['fc3_w'], 'L0_tok_fc3_b': _L0_tok_in['fc3_b'], 'L0_attn_w_qkv': _L0_attn_in['w_qkv'], 'L0_attn_w_proj': _L0_attn_in['w_proj'], 'L0_attn_b_proj': _L0_attn_in['b_proj'], 'L0_attn_rel_bias': _L0_attn_in['rel_bias'], 'L0_ffn_gamma': _L0_ffn_in['gamma'], 'L0_ffn_beta': _L0_ffn_in['beta'], 'L0_ffn_Wr': _L0_ffn_in['Wr'], 'L0_ffn_br': _L0_ffn_in['br'], 'L0_ffn_W1': _L0_ffn_in['W1'], 'L0_ffn_b1': _L0_ffn_in['b1'], 'L0_ffn_W2': _L0_ffn_in['W2'], 'L0_ffn_b2': _L0_ffn_in['b2'], 'L1_attn_t': _L1_attn_in['t'], 'L1_attn_w_qkv': _L1_attn_in['w_qkv'], 'L1_attn_mem_kv': _L1_attn_in['mem_kv'], 'L1_attn_w_out': _L1_attn_in['w_out'], 'L1_attn_b_out': _L1_attn_in['b_out'], 'L1_attn_g_out': _L1_attn_in['g_out'], 'L1_attn_g_pre': _L1_attn_in['g_pre'], 'L1_ffn_W1': _L1_ffn_in['W1'], 'L1_ffn_b1': _L1_ffn_in['b1'], 'L1_ffn_Wg': _L1_ffn_in['Wg'], 'L1_ffn_bg': _L1_ffn_in['bg'], 'L1_ffn_Wd': _L1_ffn_in['Wd'], 'L1_ffn_bd': _L1_ffn_in['bd']}

def reference(x, cls_tok, L0_tok_fc0_w, L0_tok_fc0_b, L0_tok_ln0_g, L0_tok_ln0_b, L0_tok_w1r, L0_tok_w1i, L0_tok_w2r, L0_tok_w2i, L0_tok_conv_w, L0_tok_conv_b, L0_tok_ln_g, L0_tok_ln_b, L0_tok_fc1_w, L0_tok_fc1_b, L0_tok_fc2_w, L0_tok_fc2_b, L0_tok_fc3_w, L0_tok_fc3_b, L0_attn_w_qkv, L0_attn_w_proj, L0_attn_b_proj, L0_attn_rel_bias, L0_ffn_gamma, L0_ffn_beta, L0_ffn_Wr, L0_ffn_br, L0_ffn_W1, L0_ffn_b1, L0_ffn_W2, L0_ffn_b2, L1_attn_t, L1_attn_w_qkv, L1_attn_mem_kv, L1_attn_w_out, L1_attn_b_out, L1_attn_g_out, L1_attn_g_pre, L1_ffn_W1, L1_ffn_b1, L1_ffn_Wg, L1_ffn_bg, L1_ffn_Wd, L1_ffn_bd):
    import jax
    import jax.numpy as jnp

    def _L0_tok_ref(x, fc0_w, fc0_b, ln0_g, ln0_b, w1r, w1i, w2r, w2i, conv_w, conv_b, ln_g, ln_b, fc1_w, fc1_b, fc2_w, fc2_b, fc3_w, fc3_b):
        import jax, jax.numpy as jnp
        import numpy as np
        B, H, W = (16, 64, 64)
        WIDTH, LAYERS, M1, M2 = (32, 4, 12, 12)
        EPS = 1e-05

        def layer_norm(x, g, b):
            mu = jnp.mean(x, axis=-1, keepdims=True)
            var = jnp.mean((x - mu) ** 2, axis=-1, keepdims=True)
            return (x - mu) * jax.lax.rsqrt(var + EPS) * g + b

        def gelu(x):
            return jax.nn.gelu(x, approximate=False)

        def spectral_conv(x, w1, w2):
            b, c, h, w = x.shape
            x_ft = jnp.fft.rfft2(x)
            out_ft = jnp.zeros((b, w1.shape[1], h, w // 2 + 1), dtype=x_ft.dtype)
            out_ft = out_ft.at[:, :, :M1, :M2].set(jnp.einsum('bixy,ioxy->boxy', x_ft[:, :, :M1, :M2], w1))
            out_ft = out_ft.at[:, :, -M1:, :M2].set(jnp.einsum('bixy,ioxy->boxy', x_ft[:, :, -M1:, :M2], w2))
            return jnp.fft.irfft2(out_ft, s=(h, w))
        h = layer_norm(x @ fc0_w + fc0_b, ln0_g, ln0_b)
        h = jnp.transpose(h, (0, 3, 1, 2))
        for i in range(LAYERS):
            w1 = w1r[i] + 1j * w1i[i]
            w2 = w2r[i] + 1j * w2i[i]
            x1 = spectral_conv(h, w1, w2)
            x2 = jnp.einsum('bchw,oc->bohw', h, conv_w[i]) + conv_b[i][None, :, None, None]
            h = x1 + x2
            h = jnp.transpose(h, (0, 2, 3, 1))
            h = layer_norm(h, ln_g[i], ln_b[i])
            if i < LAYERS - 1:
                h = gelu(h)
            h = jnp.transpose(h, (0, 3, 1, 2))
        h = jnp.transpose(h, (0, 2, 3, 1))
        h = gelu(h @ fc1_w + fc1_b)
        h = gelu(h @ fc2_w + fc2_b)
        h = h @ fc3_w + fc3_b
        return h[..., 0]

    def _L0_attn_ref(x, w_qkv, w_proj, b_proj, rel_bias):
        import jax, jax.numpy as jnp
        import numpy as np
        DIM = 64
        WS = 64
        H = 8
        HD = DIM // H
        SCALE = HD ** (-0.5)
        B, L, C = x.shape
        pad_len = (WS - L % WS) % WS
        if pad_len > 0:
            x = jnp.pad(x, ((0, 0), (0, pad_len), (0, 0)))
        padded_L = x.shape[1]
        nw = padded_L // WS
        xw = x.reshape(B, nw, WS, C)
        qkv = jnp.einsum('bnwc,oc->bnwo', xw, w_qkv)
        qkv = qkv.reshape(B, nw, WS, 3, H, HD)
        q = jnp.transpose(qkv[..., 0, :, :], (0, 1, 3, 2, 4))
        k = jnp.transpose(qkv[..., 1, :, :], (0, 1, 3, 2, 4))
        v = jnp.transpose(qkv[..., 2, :, :], (0, 1, 3, 2, 4))
        attn = jnp.einsum('bnhqd,bnhkd->bnhqk', q, k) * SCALE
        pos = jnp.arange(WS)
        rel_idx = pos[None, :] - pos[:, None] + WS - 1
        attn = attn + rel_bias[rel_idx]
        attn = jax.nn.softmax(attn, axis=-1)
        out = jnp.einsum('bnhqk,bnhkd->bnhqd', attn, v)
        out = jnp.transpose(out, (0, 1, 3, 2, 4)).reshape(B, nw, WS, C)
        out = jnp.einsum('bnwc,oc->bnwo', out, w_proj) + b_proj
        out = out.reshape(B, padded_L, C)
        if pad_len > 0:
            out = out[:, :L, :]
        return out

    def _L0_ffn_ref(x, gamma, beta, Wr, br, W1, b1, W2, b2):
        import jax, jax.numpy as jnp
        import numpy as np
        E = 8
        K = 2
        D = 64
        H = 128
        DOUT = 64
        EPS = 1e-05
        mu = jnp.mean(x, axis=-1, keepdims=True)
        var = jnp.mean(jnp.square(x - mu), axis=-1, keepdims=True)
        xn = (x - mu) * jax.lax.rsqrt(var + EPS) * gamma + beta
        logits = jnp.einsum('bsd,de->bse', xn, Wr) + br
        top_vals, top_idx = jax.lax.top_k(logits, K)
        w = jax.nn.softmax(top_vals, axis=-1)
        w_full = jnp.einsum('bsk,bske->bse', w, jax.nn.one_hot(top_idx, E, dtype=w.dtype))
        y = jnp.zeros(x.shape[:-1] + (DOUT,), x.dtype)
        for e in range(E):
            h = jax.nn.gelu(jnp.einsum('bsd,dh->bsh', xn, W1[e]) + b1[e], approximate=False)
            y_e = jnp.einsum('bsh,hd->bsd', h, W2[e]) + b2[e]
            y = y + y_e * w_full[..., e, None]
        return y

    def _L1_attn_ref(x, t, w_qkv, mem_kv, w_out, b_out, g_out, g_pre):
        import jax, jax.numpy as jnp
        import numpy as np
        DIM = 64
        HEADS = 4
        DIM_HEAD = 32
        NUM_MEM = 4
        HIDDEN = HEADS * DIM_HEAD
        SCALE = DIM_HEAD ** (-0.5)

        def rmsnorm(x, g):
            n = jnp.linalg.norm(x, axis=-1, keepdims=True)
            return x / jnp.maximum(n, 1e-12) * g * x.shape[-1] ** 0.5
        b, n, c = x.shape
        xn = rmsnorm(x, g_pre)
        qkv = xn @ w_qkv
        q, k, v = jnp.split(qkv, 3, axis=-1)

        def to_heads(z):
            return z.reshape(b, n, HEADS, DIM_HEAD).transpose(0, 2, 3, 1)
        q, k, v = map(to_heads, (q, k, v))
        mk = jnp.broadcast_to(mem_kv[0], (b, HEADS, DIM_HEAD, NUM_MEM))
        mv = jnp.broadcast_to(mem_kv[1], (b, HEADS, DIM_HEAD, NUM_MEM))
        k = jnp.concatenate([mk, k], axis=-1)
        v = jnp.concatenate([mv, v], axis=-1)
        q = jax.nn.softmax(q, axis=-2) * SCALE
        k = jax.nn.softmax(k, axis=-1)
        context = jnp.einsum('bhdn,bhen->bhde', k, v)
        out = jnp.einsum('bhde,bhdn->bhen', context, q)
        out = out.transpose(0, 3, 1, 2).reshape(b, n, HIDDEN)
        out = rmsnorm(out @ w_out + b_out, g_out)
        return out + x

    def _L1_ffn_ref(x, W1, b1, Wg, bg, Wd, bd):
        import jax, jax.numpy as jnp
        import numpy as np
        C = 64
        HID = 256
        E = 8
        TEMP = 1.0
        orig_shape = x.shape
        xf = x.reshape(-1, orig_shape[-1])
        H = jax.nn.gelu(xf @ W1 + b1, approximate=False)
        probs = jax.nn.softmax((H @ Wg + bg) / TEMP, axis=-1)
        assign = jnp.argmax(probs, axis=-1)
        out = jnp.zeros_like(xf)
        for e in range(Wd.shape[0]):
            y = H @ Wd[e] + bd[e]
            sel = (assign == e)[:, None]
            out = out + jnp.where(sel, probs[:, e:e + 1] * y, 0.0)
        return out.reshape(orig_shape)
    h = _L0_tok_ref(x, L0_tok_fc0_w, L0_tok_fc0_b, L0_tok_ln0_g, L0_tok_ln0_b, L0_tok_w1r, L0_tok_w1i, L0_tok_w2r, L0_tok_w2i, L0_tok_conv_w, L0_tok_conv_b, L0_tok_ln_g, L0_tok_ln_b, L0_tok_fc1_w, L0_tok_fc1_b, L0_tok_fc2_w, L0_tok_fc2_b, L0_tok_fc3_w, L0_tok_fc3_b)
    h = jnp.concatenate([jnp.broadcast_to(cls_tok, (h.shape[0], 1, h.shape[2])), h], axis=1)
    h = h + _L0_attn_ref(_layernorm(h, axis=-1), L0_attn_w_qkv, L0_attn_w_proj, L0_attn_b_proj, L0_attn_rel_bias)
    h = h + _L0_ffn_ref(_layernorm(h, axis=-1), L0_ffn_gamma, L0_ffn_beta, L0_ffn_Wr, L0_ffn_br, L0_ffn_W1, L0_ffn_b1, L0_ffn_W2, L0_ffn_b2)
    h = h + _L1_attn_ref(_layernorm(h, axis=-1), L1_attn_t, L1_attn_w_qkv, L1_attn_mem_kv, L1_attn_w_out, L1_attn_b_out, L1_attn_g_out, L1_attn_g_pre)
    h = h + _L1_ffn_ref(_layernorm(h, axis=-1), L1_ffn_W1, L1_ffn_b1, L1_ffn_Wg, L1_ffn_bg, L1_ffn_Wd, L1_ffn_bd)
    return h

_drawn_inputs = setup_inputs


def setup_inputs(seed=0):
    import zlib

    import numpy as np

    out = dict(_drawn_inputs(seed))
    spreads = {'L0_tok_fc0_b': (0.0, 0.1),
     'L0_tok_ln0_g': (1.0, 0.2),
     'L0_tok_ln0_b': (0.0, 0.1),
     'L0_tok_conv_b': (0.0, 0.1),
     'L0_tok_ln_g': (1.0, 0.2),
     'L0_tok_ln_b': (0.0, 0.1),
     'L0_tok_fc1_b': (0.0, 0.1),
     'L0_tok_fc2_b': (0.0, 0.1),
     'L0_attn_b_proj': (0.0, 0.1),
     'L0_ffn_br': (0.0, 0.1),
     'L1_attn_b_out': (0.0, 0.1),
     'L1_attn_g_out': (1.0, 0.2),
     'L1_attn_g_pre': (1.0, 0.6),
     'L1_ffn_b1': (0.0, 0.8),
     'L1_ffn_bg': (0.0, 0.8),
     'L1_ffn_bd': (0.0, 0.8)}
    factors = {'L0_tok_w1r': 8.0,
     'L0_tok_w1i': 8.0,
     'L0_tok_w2r': 8.0,
     'L0_tok_w2i': 8.0,
     'L0_attn_rel_bias': 8.0,
     'L0_ffn_gamma': 8.0,
     'L0_ffn_beta': 8.0,
     'L0_ffn_Wr': 3.334,
     'L0_ffn_b1': 8.0,
     'L1_attn_w_qkv': 3.894,
     'L1_attn_mem_kv': 6.234,
     'L1_attn_w_out': 3.163,
     'L1_ffn_W1': 8.0,
     'L1_ffn_Wg': 8.0,
     'L1_ffn_Wd': 8.0}
    for name, (base, spread) in spreads.items():
        noise = np.random.default_rng([zlib.crc32(name.encode()), seed]).standard_normal(out[name].shape)
        drawn = base * np.exp(spread * noise) if base else spread * noise
        out[name] = jnp.asarray(drawn.astype(out[name].dtype))
    for name, factor in factors.items():
        out[name] = (out[name] * factor).astype(out[name].dtype)
    return out
```

```python
from contextlib import ExitStack

import numpy as np

import concourse.bass as bass
from concourse import mybir

ALU = mybir.AluOpType
ACT = mybir.ActivationFunctionType
AX = mybir.AxisListType
F32 = mybir.dt.float32
BF16 = mybir.dt.bfloat16

SIDE = 64
CH = 32
LAYERS = 4
KY = 12
KX = 13
WQ = 4
WJ = SIDE // WQ
QI = 4
CHUNK = 512
QCOLS = WJ * QI * SIDE
NCH = QCOLS // CHUNK
EPS = 1e-5
SK = 2 * KX
RK = 2 * KY
MODES = KY * KX
VCOLS = CH // 4 * 2 * KX * QI
D_FILLS, A_FILLS, B_FILLS = 4, 4, 2
B_SETS = (range(0, 7), range(7, 13))


def constants():
    y = np.arange(SIDE)
    ky, kx = np.arange(KY), np.arange(KX)
    th = 2 * np.pi * np.outer(y, kx) / SIDE
    ph = 2 * np.pi * np.outer(y, ky) / SIDE
    fy = np.concatenate([np.cos(th), np.sin(th)], 1)
    fw = np.concatenate([np.cos(ph), np.sin(ph)], 1)
    two = np.eye(2)
    weight = np.where(ky == 0, 1.0, 2.0)[:, None] / SIDE ** 2
    iw = np.concatenate([weight * np.cos(ph.T), -weight * np.sin(ph.T)], 0)
    iy = fy.T
    c = {
        "fwd_y": np.kron(two, fy),
        "fwd_w": np.kron(two, fw),
        "inv_w": np.einsum("rw,ab->rabw", iw, np.eye(4)).reshape(RK * 4, 4 * SIDE),
        "inv_y": np.einsum("sy,ab->saby", iy, np.eye(QI)).reshape(SK * QI, QI * SIDE),
        "ident": np.eye(128),
        "center": np.eye(128) - np.kron(np.eye(4), np.full((CH, CH), 1.0 / CH)),
    }
    c["mean_sel"] = np.kron(np.eye(WQ), np.full((CH, 1), 1.0 / CH))
    back = np.zeros((96, NCH, 128))
    for part in range(3):
        for q in range(WQ):
            for t in range(NCH):
                back[part * 32 + t * WQ + q, t, q * CH:(q + 1) * CH] = 1.0
    c["spread_sel"] = back.reshape(96, NCH * 128)
    pos = np.array([[1, 1, 1, -1], [1, -1, -1, -1], [-1, 1, 1, 1], [1, 1, 1, -1]], float).T
    neg = np.array([[1, -1, 1, 1], [1, 1, -1, 1], [1, 1, -1, 1], [-1, 1, -1, -1]], float).T
    signs = np.stack([pos, neg], 2).reshape(4, 8)
    c["sign"] = np.repeat(np.concatenate([signs, np.full((4, 1), 1.0 / CH)], 1), CH, 0)
    return {k: np.ascontiguousarray(v.astype(np.float32)) for k, v in c.items()}


def token_tower(nc, io, nq, bank, sem, sb, dram, tok):
    ni = nq * QI

    h_dram = dram("h_dram", [nq, 128, QCOLS], F32)
    mix_dram = dram("mix_dram", [LAYERS * KY, 128, KX * 128], F32)
    spec_dram = dram("spec_dram", [nq, RK, 4 * VCOLS], F32)

    fwd_y = sb("fwd_y", [128, 2 * SK], F32)
    fwd_w = sb("fwd_w", [128, 2 * RK], F32)
    inv_w = sb("inv_w", [96, 4 * SIDE], F32)
    inv_y = sb("inv_y", [SK * QI, QI * SIDE], F32)
    ident = sb("ident", [128, 128], F32)
    center = sb("center", [128, 128], F32)
    mean_sel = sb("mean_sel", [128, WQ], F32)
    ident_b = sb("ident_b", [128, 128], BF16)
    spread_f = sb("spread_f", [96, NCH * 128], F32)
    spread_sel = sb("spread_sel", [96, NCH * 128], BF16)
    sign = sb("sign", [128, 9], F32)
    fc0_w = sb("fc0_w", [12, 128], F32)
    conv_w = sb("conv_w", [128, LAYERS * 128], F32)
    col_sum = sb("col_sum", [128, LAYERS * 4], F32)
    bias_in = sb("bias_in", [128, LAYERS + 1], F32)
    bias = sb("bias", [128, LAYERS + 1], F32)
    gain = sb("gain", [128, LAYERS + 1], F32)
    shift = sb("shift", [128, LAYERS + 1], F32)
    fc1_w = sb("fc1_w", [128, 128], F32)
    fc1_b = sb("fc1_b", [128, 1], F32)
    fc2_w = sb("fc2_w", [128, 64], F32)
    fc2_b = sb("fc2_b", [128, 1], F32)
    fc3_sel = sb("fc3_sel", [128, 16 * 32], F32)
    fc3_b = sb("fc3_b", [32, 1], F32)

    h_in = sb("h_in", [128, QCOLS], F32)
    h_out = sb("h_out", [128, QCOLS], F32)
    dev = sb("dev", [128, QCOLS], F32)
    rows = sb("rows", [128, QCOLS], F32)
    squares = sb("squares", [128, 2 * CHUNK], F32)
    spec_y = sb("spec_y", [128, CH * 2 * SK], F32)
    half_inv = sb("half_inv", [SK * QI, CH * SIDE], F32)
    mixed = sb("mixed", [96, VCOLS], F32)
    spec = sb("spec", [128, MODES * ni], F32)
    var_eps = sb("var_eps", [128, 128], F32)
    seed = sb("seed", [128, 128], mybir.dt.int32)
    rstd = sb("rstd", [128, 128], F32)
    newton = sb("newton", [128, 128], F32)
    rest = sb("rest", [128, 128], F32)
    split = sb("split", [128, 4 * 96], BF16)
    parts = sb("parts", [96, CHUNK], BF16)
    prep_in = sb("prep_in", [128, 4 * KX * CH], F32)
    prep_fold = sb("prep_fold", [128, 4 * KX * CH // 2], F32)
    prep_tmp = sb("prep_tmp", [128, KX * CH], F32)
    prep_out = sb("prep_out", [128, KX * 128], F32)
    logits = sb("logits", [128, CHUNK], F32)
    tok_rows = sb("tok_rows", [128, 2 * SIDE], F32)
    stage_cols = nq * KX * QI
    hidden1 = [rows[:, b * CHUNK:(b + 1) * CHUNK] for b in range(2)]
    hidden2 = [rows[:, (2 + b) * CHUNK:(3 + b) * CHUNK] for b in range(2)]

    turn_ps, inv_ps, conv_ps = (bank[0], bank[1]), (bank[2], bank[3]), (bank[4], bank[5])
    var_ps, logit_ps = bank[6], bank[7]

    names = ("consts_in consts_ready h_loaded mixed_loaded h_stored spec_stored0 spec_stored1 mix_loaded0 mix_loaded1 prep_loaded "
             "prep_stored tok_stored prep_step prep_done "
             "inv_half_ps inv_half conv_done dev_ready square_ready var_added split_ready parts_turned rstd_step "
             "fold_step cls_stored parts_ready spread_done normed h_ready turned turn_dve turn_act fy_done fy_taken "
             "fw_done fw_taken mix_done mix_act mix_dve bias_ps "
             "fc1_done fc1_act fc2_done fc2_act fc3_done logit_taken tok_turned tok_ready")
    s = {n: sem(n) for n in names.split()}

    v_mix_w = [h_out[:, b * KX * 128:(b + 1) * KX * 128] for b in range(2)]
    v_stage = [dev[:, b * stage_cols:(b + 1) * stage_cols] for b in range(2)]
    spec_v = spec[:].rearrange("p (q k n) -> p q k n", q=KY, k=KX)

    loads = [(fwd_y, "fwd_y"), (fwd_w, "fwd_w"), (inv_w, "inv_w"), (inv_y, "inv_y"), (ident, "ident"),
             (center, "center"), (mean_sel, "mean_sel"), (spread_f, "spread_sel"), (sign, "sign"),
             (fc0_w, "fc0_w"), (conv_w, "conv_w"), (bias_in, "bias_in"), (gain, "gain"),
             (shift, "shift"), (fc1_w, "fc1_w"), (fc1_b, "fc1_b"), (fc2_w, "fc2_w"),
             (fc2_b, "fc2_b"), (fc3_sel, "fc3_sel"), (fc3_b, "fc3_b")]
    N_CONST = 16 * len(loads)
    MIX_SETS = (range(0, 4), range(4, 8), range(8, 12), range(12, 13))

    def quads(eng, first, last, body):
        if last - first == 1:
            body(first)
        elif last > first:
            with eng.Fori(first, last) as i:
                body(i)

    def pipeline(eng, P, front, back):
        front(0, None)
        peeled = 2 if P in (0, LAYERS) else 1
        if peeled == 2:
            front(1, back)
        quads(eng, peeled, nq, lambda i: front(i, back))
        back(nq - 1)

    def sp_program(sp):
        for t, name in loads:
            sp.dma_start(t[:], io[name]).then_inc(s["consts_in"], 16)
        for P in range(LAYERS + 1):
            if P > 0:
                sp.wait_ge(s["h_stored"], 16 * P * nq)
                sp.wait_ge(s["turned"], 8 * P * nq)
                sp.wait_ge(s["conv_done"], 8 * P * nq)
                sp.dma_start(h_in[:], h_dram[0]).then_inc(s["h_loaded"], 16)
                for ky in range(KY + 2):
                    n = (P - 1) * KY + ky
                    if ky >= 2:
                        sp.wait_ge(s["mix_act"], 2 * (n - 1))
                        sp.wait_ge(s["mix_dve"], 2 * (n - 1))
                        dst = spec_dram.rearrange("a (r q) (o s m) -> r s q o a m", r=2, o=CH, s=2)
                        src = v_stage[ky % 2].rearrange("p (a m) -> p a m", a=nq)
                        for sr in range(4):
                            sp.dma_start(dst[sr % 2, sr // 2, ky - 2], src[32 * sr:32 * sr + 32]
                                         ).then_inc(s[f"spec_stored{ky % 2}"], 16)
                    if ky < KY:
                        sp.wait_ge(s["prep_stored"], 16 * (n + 1))
                        if ky >= 2:
                            sp.wait_ge(s["mix_done"], 4 * (n - 1))
                        sp.dma_start(v_mix_w[ky % 2], mix_dram[n]).then_inc(s[f"mix_loaded{ky % 2}"], 16)

            def one(i, P=P):
                g = P * nq + i
                if not isinstance(i, int) or i > 0:
                    sp.wait_ge(s["conv_done"], 8 * g)
                if P == 0:
                    sp.dma_start(h_in[0:12, :], io["x"][i]).then_inc(s["h_loaded"], 16)
                else:
                    if not isinstance(i, int) or i > 0:
                        sp.dma_start(h_in[:], h_dram[i]).then_inc(s["h_loaded"], 16)
                    else:
                        sp.wait_ge(s["spec_stored0"], 32 * KY * P)
                        sp.wait_ge(s["spec_stored1"], 32 * KY * P)
                    if P > 1 or not isinstance(i, int) or i > 0:
                        sp.wait_ge(s["inv_half_ps"], D_FILLS * (g - nq))
                    sp.dma_start(mixed[:], spec_dram[i].rearrange("r (a c) -> (r a) c", a=4)
                                 ).then_inc(s["mixed_loaded"], 16)

            one(0)
            quads(sp, 1, nq, one)
        sp.wait_ge(s["tok_stored"], 32 * nq)

    def pe_program(pe):
        pe.wait_ge(s["consts_in"], N_CONST)
        nc.tensor.matmul(logit_ps[:, 0:LAYERS + 1], center[:], bias_in[:], start=True, stop=True
                         ).then_inc(s["bias_ps"], 1)
        pe.wait_ge(s["consts_ready"], 6)
        for P in range(LAYERS + 1):
            if P > 0:
                pe.wait_ge(s["fw_taken"], B_FILLS * P * nq)
                for ky in range(KY):
                    n = (P - 1) * KY + ky
                    pe.wait_ge(s[f"mix_loaded{ky % 2}"], 16 * (n // 2 + 1))
                    for f, ks in enumerate(MIX_SETS):
                        ps = (turn_ps + inv_ps)[f]
                        if n > 0:
                            pe.wait_ge(s["mix_act" if f % 2 == 0 else "mix_dve"], 2 * (n - 1) + f // 2 + 1)
                        for j, k in enumerate(ks):
                            mm = nc.tensor.matmul(ps[:, j * ni:(j + 1) * ni],
                                                  v_mix_w[ky % 2][:, k * 128:(k + 1) * 128],
                                                  spec_v[:, ky, k, :], start=True, stop=True)
                        mm.then_inc(s["mix_done"], 1)
                pe.wait_ge(s["mix_act"], 2 * P * KY)
                pe.wait_ge(s["mix_dve"], 2 * P * KY)

            def front(i, back, P=P):
                g = P * nq + i
                start = P == 0 and isinstance(i, int) and i == 0
                inner = not (isinstance(i, int) and i == 0)
                gd = g - nq
                if P > 0:
                    pe.wait_ge(s["mixed_loaded"], 16 * (gd + 1))
                    mv = mixed[:].rearrange("p (o m) -> p o m", o=8)
                    for f in range(D_FILLS):
                        if f < 2:
                            if inner:
                                if P < LAYERS:
                                    pe.wait_ge(s["fw_taken"], B_FILLS * (g - 1))
                                pe.wait_ge(s["inv_half"], D_FILLS * gd)
                        else:
                            pe.wait_ge(s["inv_half"], D_FILLS * gd + f - 1)
                        for j in range(2):
                            mm = nc.tensor.matmul(inv_ps[f % 2][0:SK * QI, j * 256:(j + 1) * 256],
                                                  mv[:, 2 * f + j, :], inv_w[:], start=True, stop=True)
                        mm.then_inc(s["inv_half_ps"], 1)
                    pe.wait_ge(s["inv_half"], D_FILLS * (gd + 1))
                pe.wait_ge(s["h_loaded"], 16 * (g + 1))

                def add_var(t):
                    pe.wait_ge(s["square_ready"], 8 * g + t + 1)
                    if t == 0 and not start:
                        pe.wait_ge(s["parts_ready"], g)
                    for j in range(4):
                        c = (t % 2) * CHUNK + j * 128
                        o = j * 32 + t * WQ
                        mm = nc.tensor.matmul(var_ps[:, o:o + WQ], squares[:, c:c + 128], mean_sel[:],
                                              start=True, stop=True)
                    mm.then_inc(s["var_added"], 1)

                hv = half_inv[:].rearrange("p (w o) -> p w o", w=SIDE)
                for t in range(NCH):
                    if t >= 2:
                        pe.wait_ge(s["dev_ready"], 8 * g + t - 1)
                    elif not start:
                        pe.wait_ge(s["normed"], 8 * g - 1 + t)
                    cols = slice(t * CHUNK, (t + 1) * CHUNK)
                    if P == 0:
                        mm = nc.tensor.matmul(conv_ps[t % 2][:], fc0_w[:], h_in[0:12, cols],
                                              start=True, stop=True)
                    else:
                        nc.tensor.matmul(conv_ps[t % 2][:], conv_w[:, (P - 1) * 128:P * 128],
                                         h_in[:, cols], start=True, stop=False)
                        for j in range(2):
                            wj = 2 * t + j
                            mm = nc.tensor.matmul(conv_ps[t % 2][:, j * 256:(j + 1) * 256],
                                                  hv[:, wj * WQ:(wj + 1) * WQ, :], inv_y[:],
                                                  start=False, stop=(j == 1))
                    mm.then_inc(s["conv_done"], 1)
                    if t >= 2:
                        add_var(t - 2)
                add_var(NCH - 2)
                add_var(NCH - 1)
                if back is not None:
                    back(i - 1)
                pe.wait_ge(s["split_ready"], g + 1)
                for j in range(4):
                    mm = nc.tensor.matmul(var_ps[0:96, j * 128:(j + 1) * 128],
                                          split[:, j * 96:(j + 1) * 96], ident_b[:], start=True, stop=True)
                mm.then_inc(s["parts_turned"], 1)
                pe.wait_ge(s["parts_ready"], g + 1)
                for t in range(NCH):
                    if t < 2:
                        pe.wait_ge(s["dev_ready"], 8 * g + 7 + t)
                    else:
                        pe.wait_ge(s["normed"], 8 * g + t - 1)
                    nc.tensor.matmul(conv_ps[t % 2][:], spread_sel[:, t * 128:(t + 1) * 128], parts[:],
                                     start=True, stop=True).then_inc(s["spread_done"], 1)

            def forward(i, P=P):
                g = P * nq + i
                start = P == 0 and isinstance(i, int) and i == 0
                for t in range(NCH):
                    pe.wait_ge(s["h_ready"], 8 * g + t + 1)
                    if t >= 2 or not start:
                        pe.wait_ge(s["turn_dve" if t % 2 == 0 else "turn_act"], 4 * g + t // 2)
                    for j in range(4):
                        c = t * CHUNK + j * 128
                        mm = nc.tensor.transpose(turn_ps[t % 2][:, j * 128:(j + 1) * 128],
                                                 h_out[:, c:c + 128], ident[:])
                    mm.then_inc(s["turned"], 1)
                pe.wait_ge(s["turn_dve"], 4 * (g + 1))
                pe.wait_ge(s["turn_act"], 4 * (g + 1))
                rv = rows[:].rearrange("p (a w c) -> p a w c", a=2, w=SIDE)
                for f in range(A_FILLS):
                    if f < 2:
                        if not start:
                            pe.wait_ge(s["fw_taken"], B_FILLS * g)
                    else:
                        pe.wait_ge(s["fy_taken"], A_FILLS * g + f - 1)
                    for j in range(8):
                        mm = nc.tensor.matmul(inv_ps[f % 2][:, j * 2 * SK:(j + 1) * 2 * SK],
                                              rv[:, :, :, 8 * f + j], fwd_y[:], start=True, stop=True)
                    mm.then_inc(s["fy_done"], 1)
                pe.wait_ge(s["fy_taken"], A_FILLS * (g + 1))
                yv = spec_y[:].rearrange("p (k m) -> p k m", k=KX)
                for f, ks in enumerate(B_SETS):
                    for j, k in enumerate(ks):
                        mm = nc.tensor.matmul(inv_ps[f % 2][:, j * 2 * RK:(j + 1) * 2 * RK],
                                              yv[:, k, :], fwd_w[:], start=True, stop=True)
                    mm.then_inc(s["fw_done"], 1)

            def head(i):
                def fc1(u):
                    t, q = divmod(u, WQ)
                    if q == 0:
                        pe.wait_ge(s["h_ready"], 8 * (LAYERS * nq + i) + t + 1)
                    if u >= 2 or not (isinstance(i, int) and i == 0):
                        pe.wait_ge(s["fc1_act"], 32 * i + u - 1)
                    r = slice(q * CH, (q + 1) * CH)
                    nc.tensor.matmul(turn_ps[u % 2][:], fc1_w[r, :], h_out[r, t * CHUNK:(t + 1) * CHUNK],
                                     start=True, stop=True).then_inc(s["fc1_done"], 1)

                def fc2(u):
                    pr = u // 2
                    pe.wait_ge(s["fc1_act"], 32 * i + u + 1)
                    if u % 2 == 0:
                        if pr >= 2:
                            pe.wait_ge(s["fc2_act"], 16 * i + pr - 1)
                        else:
                            if not (isinstance(i, int) and i == 0):
                                pe.wait_ge(s["fc2_act"], 16 * i)
                    half = slice(64 * (u % 2), 64 * (u % 2) + 64)
                    nc.tensor.matmul(inv_ps[pr % 2][half, :], fc2_w[:], hidden1[u % 2],
                                     start=True, stop=True).then_inc(s["fc2_done"], 1)

                def fc3(pr):
                    pe.wait_ge(s["fc2_act"], 16 * i + pr + 1)
                    if pr == 0 and not (isinstance(i, int) and i == 0):
                        pe.wait_ge(s["tok_ready"], i)
                    nc.tensor.matmul(logit_ps[0:32, :], fc3_sel[:, pr * 32:(pr + 1) * 32], hidden2[pr % 2],
                                     start=(pr == 0), stop=(pr == 15)).then_inc(s["fc3_done"], 1)

                for u in range(32 + 5):
                    if u < 32:
                        fc1(u)
                    if 1 <= u < 33:
                        fc2(u - 1)
                    if u >= 4 and u % 2 == 0 and (u - 4) // 2 < 16:
                        fc3((u - 4) // 2)
                pe.wait_ge(s["logit_taken"], i + 1)
                for a in range(2):
                    for j in range(2):
                        c = j * 256 + a * 128
                        o = (a * 2 + j) * 128
                        mm = nc.tensor.transpose(logit_ps[:, o:o + 128], logits[:, c:c + 128], ident[:])
                mm.then_inc(s["tok_turned"], 1)

            pipeline(pe, P, front, forward if P < LAYERS else head)

    def act_program(act):
        act.wait_ge(s["consts_ready"], 6)
        for P in range(LAYERS + 1):
            if P > 0:
                act.wait_ge(s["h_ready"], 8 * P * nq)
                for ky in range(KY):
                    n = (P - 1) * KY + ky
                    stage = v_stage[ky % 2].rearrange("p (a k n) -> p k a n", a=nq, k=KX)
                    if ky >= 2:
                        act.wait_ge(s[f"spec_stored{ky % 2}"], 64 * (n // 2))
                    for f in (0, 2):
                        act.wait_ge(s["mix_done"], 4 * n + f + 1)
                        ks = MIX_SETS[f]
                        act.activation(stage[:, ks[0]:ks[-1] + 1],
                                       (turn_ps + inv_ps)[f][:, 0:len(ks) * ni].rearrange(
                                           "p (k a n) -> p k a n", k=len(ks), a=nq),
                                       ACT.Copy).then_inc(s["mix_act"], 1)

            def front(i, back, P=P):
                g = P * nq + i
                start = P == 0 and isinstance(i, int) and i == 0
                if P > 0:
                    gd = g - nq
                    if P > 1 or not (isinstance(i, int) and i == 0):
                        act.wait_ge(s["conv_done"], 8 * g)
                    for f in range(D_FILLS):
                        act.wait_ge(s["inv_half_ps"], D_FILLS * gd + f + 1)
                        out = half_inv[:].rearrange("p (w o e) -> p e o w", w=SIDE, e=8)[:, 2 * f:2 * f + 2]
                        act.activation(out, inv_ps[f % 2][0:SK * QI, :].rearrange(
                            "p (e o w) -> p e o w", e=2, o=4), ACT.Copy).then_inc(s["inv_half"], 1)
                for t in range(NCH):
                    act.wait_ge(s["dev_ready"], 8 * g + t + 1)
                    if t >= 2:
                        act.wait_ge(s["var_added"], 8 * g + t - 1)
                    elif not start:
                        act.wait_ge(s["var_added"], 8 * g - 1 + t)
                    act.activation(squares[:, (t % 2) * CHUNK:(t % 2 + 1) * CHUNK],
                                   dev[:, t * CHUNK:(t + 1) * CHUNK], ACT.Square
                                   ).then_inc(s["square_ready"], 1)
                if back is not None:
                    back(i - 1)
                if not start:
                    if P < LAYERS:
                        act.wait_ge(s["turned"], 8 * g)
                        act.wait_ge(s["h_stored"], 16 * g)
                    elif back is not None:
                        act.wait_ge(s["fc1_done"], 32 * i)
                for t in range(NCH):
                    act.wait_ge(s["normed"], 8 * g + t + 1)
                    act.activation(h_out[:, t * CHUNK:(t + 1) * CHUNK], dev[:, t * CHUNK:(t + 1) * CHUNK],
                                   ACT.Gelu if 1 <= P < LAYERS else ACT.Identity,
                                   bias=shift[:, P:P + 1], scale=gain[:, P:P + 1]
                                   ).then_inc(s["h_ready"], 1)
                if P < LAYERS:
                    act.wait_ge(s["h_ready"], 8 * (g + 1))
                    act.dma_start(h_dram[i], h_out[:]).then_inc(s["h_stored"], 16)

            def forward(i, P=P):
                g = P * nq + i
                start = P == 0 and isinstance(i, int) and i == 0
                rv = rows[:].rearrange("p (a w c) -> p w a c", a=2, w=WJ)
                if not start:
                    act.wait_ge(s["fy_done"], A_FILLS * g)
                for t in range(1, NCH, 2):
                    act.wait_ge(s["turned"], 8 * g + t + 1)
                    act.activation(rv[:, 2 * t:2 * t + 2], turn_ps[1][:].rearrange(
                        "p (w a c) -> p w a c", w=2, a=2), ACT.Copy).then_inc(s["turn_act"], 1)
                if not start:
                    act.wait_ge(s["fw_done"], B_FILLS * g)
                for f in range(A_FILLS):
                    act.wait_ge(s["fy_done"], A_FILLS * g + f + 1)
                    n = 8 * 2 * SK
                    yv = spec_y[:].rearrange("p (k e c) -> p c e k", k=KX, c=CH)
                    act.activation(yv[:, 8 * f:8 * f + 8], inv_ps[f % 2][:, 0:n].rearrange(
                        "p (c e k) -> p c e k", c=8, k=KX), ACT.Copy
                                   ).then_inc(s["fy_taken"], 1)

            def head(i):
                def gelu2(pr):
                    act.wait_ge(s["fc2_done"], 32 * i + 2 * pr + 2)
                    if pr >= 2:
                        act.wait_ge(s["fc3_done"], 16 * i + pr - 1)
                    elif not (isinstance(i, int) and i == 0):
                        act.wait_ge(s["fc3_done"], 16 * i - 1 + pr)
                    act.activation(hidden2[pr % 2], inv_ps[pr % 2][:], ACT.Gelu, bias=fc2_b[:]
                                   ).then_inc(s["fc2_act"], 1)

                for u in range(32 + 3):
                    if u < 32:
                        act.wait_ge(s["fc1_done"], 32 * i + u + 1)
                        if u >= 2:
                            act.wait_ge(s["fc2_done"], 32 * i + u - 1)
                        elif not (isinstance(i, int) and i == 0):
                            act.wait_ge(s["fc2_done"], 32 * i - 1 + u)
                        act.activation(hidden1[u % 2], turn_ps[u % 2][:], ACT.Gelu, bias=fc1_b[:]
                                       ).then_inc(s["fc1_act"], 1)
                    if u >= 3 and u % 2 == 1:
                        gelu2((u - 3) // 2)

            pipeline(act, P, front, forward if P < LAYERS else head)

    def dve_program(dve):
        dve.wait_ge(s["consts_in"], N_CONST)
        dve.memset(logits[:], 0.0).then_inc(s["consts_ready"], 1)
        dve.tensor_copy(ident_b[:], ident[:]).then_inc(s["consts_ready"], 1)
        dve.tensor_copy(spread_sel[:], spread_f[:]).then_inc(s["consts_ready"], 1)
        for n, w in enumerate((conv_w, fc0_w)):
            wv = w[:].rearrange("p (b o) -> p b o", o=CH)
            rows_, blocks = wv.shape[0], wv.shape[1]
            sums = col_sum[0:rows_, 0:blocks]
            if n > 0:
                dve.wait_ge(s["consts_ready"], 4)
            dve.tensor_reduce(sums, wv, AX.X, ALU.add).then_inc(s["fold_step"], 1)
            dve.wait_ge(s["fold_step"], 2 * n + 1)
            dve.tensor_scalar(sums, sums, 1.0 / CH, None, ALU.mult).then_inc(s["fold_step"], 1)
            dve.wait_ge(s["fold_step"], 2 * n + 2)
            dve.tensor_tensor(wv, wv, sums.unsqueeze(2).to_broadcast([rows_, blocks, CH]), ALU.subtract
                              ).then_inc(s["consts_ready"], 1)
        dve.wait_ge(s["bias_ps"], 1)
        dve.tensor_copy(bias[:], logit_ps[:, 0:LAYERS + 1]).then_inc(s["consts_ready"], 1)
        dve.wait_ge(s["consts_ready"], 6)
        for P in range(LAYERS + 1):
            if P > 0:
                dve.wait_ge(s["h_ready"], 8 * P * nq)
                for ky in range(KY):
                    n = (P - 1) * KY + ky
                    stage = v_stage[ky % 2].rearrange("p (a k n) -> p k a n", a=nq, k=KX)
                    if ky >= 2:
                        dve.wait_ge(s[f"spec_stored{ky % 2}"], 64 * (n // 2))
                    for f in (1, 3):
                        dve.wait_ge(s["mix_done"], 4 * n + f + 1)
                        ks = MIX_SETS[f]
                        dve.tensor_copy(stage[:, ks[0]:ks[-1] + 1],
                                        (turn_ps + inv_ps)[f][:, 0:len(ks) * ni].rearrange(
                                            "p (k a n) -> p k a n", k=len(ks), a=nq)
                                        ).then_inc(s["mix_dve"], 1)

            def inverse_root(g, start):
                st = s["rstd_step"]
                b = 15 * g

                def step(ins, k):
                    ins.then_inc(st, 1)
                    dve.wait_ge(st, b + k)

                dve.wait_ge(s["var_added"], 8 * (g + 1))
                step(dve.tensor_scalar(var_eps[:], var_ps[:, 0:128], EPS, None, ALU.add), 1)
                step(dve.tensor_scalar(seed[:], var_eps[:].bitcast(mybir.dt.int32), 1, None,
                                       ALU.logical_shift_right), 2)
                step(dve.tensor_scalar(rstd[:].bitcast(mybir.dt.int32), seed[:], -1.0, float(0x5F3759DF),
                                       ALU.mult, ALU.add), 3)
                for n in range(3):
                    step(dve.tensor_tensor(newton[:], rstd[:], rstd[:], ALU.mult), 4 + 3 * n)
                    step(dve.scalar_tensor_tensor(out=newton[:], in0=newton[:], scalar=-0.5,
                                                  in1=var_eps[:], op0=ALU.mult, op1=ALU.mult), 5 + 3 * n)
                    step(dve.scalar_tensor_tensor(out=rstd[:], in0=newton[:], scalar=1.5,
                                                  in1=rstd[:], op0=ALU.add, op1=ALU.mult), 6 + 3 * n)
                sv = split[:].rearrange("p (j a c) -> p a j c", j=4, a=3)
                rv = rstd[:].rearrange("p (j c) -> p j c", j=4)
                ev = rest[:].rearrange("p (j c) -> p j c", j=4)
                if not start:
                    dve.wait_ge(s["parts_turned"], g)
                step(dve.tensor_copy(sv[:, 0], rv), 13)
                step(dve.tensor_tensor(ev, rv, sv[:, 0], ALU.subtract), 14)
                step(dve.tensor_copy(sv[:, 1], ev), 15)
                dve.tensor_tensor(sv[:, 2], ev, sv[:, 1], ALU.subtract).then_inc(s["split_ready"], 1)

            def front(i, back, P=P):
                g = P * nq + i
                start = P == 0 and isinstance(i, int) and i == 0
                if P > 0 and isinstance(i, int) and i == 0:
                    dve.wait_ge(s["spec_stored0"], 32 * KY * P)
                    dve.wait_ge(s["spec_stored1"], 32 * KY * P)
                for t in range(NCH):
                    dve.wait_ge(s["conv_done"], 8 * g + t + 1)
                    if not start:
                        dve.wait_ge(s["h_ready"], 8 * g - 7 + t)
                    dve.tensor_scalar(dev[:, t * CHUNK:(t + 1) * CHUNK], conv_ps[t % 2][:],
                                      bias[:, P:P + 1], None, ALU.add).then_inc(s["dev_ready"], 1)
                if back is not None and P < LAYERS:
                    back(i - 1, lambda: inverse_root(g, start))
                else:
                    inverse_root(g, start)
                    if back is not None:
                        back(i - 1)
                dve.wait_ge(s["parts_turned"], g + 1)
                if not start:
                    dve.wait_ge(s["spread_done"], 8 * g)
                dve.tensor_copy(parts[:], var_ps[0:96, :]).then_inc(s["parts_ready"], 1)
                for t in range(NCH):
                    dve.wait_ge(s["spread_done"], 8 * g + t + 1)
                    d = dev[:, t * CHUNK:(t + 1) * CHUNK]
                    dve.tensor_tensor(d, d, conv_ps[t % 2][:], ALU.mult).then_inc(s["normed"], 1)

            def forward(i, between=None, P=P):
                g = P * nq + i
                start = P == 0 and isinstance(i, int) and i == 0
                rv = rows[:].rearrange("p (a w c) -> p w a c", a=2, w=WJ)
                if not start:
                    dve.wait_ge(s["fy_done"], A_FILLS * g)
                for t in range(0, NCH, 2):
                    dve.wait_ge(s["turned"], 8 * g + t + 1)
                    dve.tensor_copy(rv[:, 2 * t:2 * t + 2], turn_ps[0][:].rearrange(
                        "p (w a c) -> p w a c", w=2, a=2)).then_inc(s["turn_dve"], 1)
                if between is not None:
                    between()
                sv = spec[:].rearrange("p (q k a m e) -> p k m q a e", q=KY, k=KX, a=nq, m=2)
                for f, ks in enumerate(B_SETS):
                    dve.wait_ge(s["fw_done"], B_FILLS * g + f + 1)
                    pv = inv_ps[f % 2][:, 0:len(ks) * 2 * RK].rearrange(
                        "p (k m r q) -> p k m r q", m=2, r=2, q=KY)
                    for e in range(2):
                        for r in range(2):
                            cp = dve.tensor_copy(
                                sv[64 * r:64 * r + 64, ks[0]:ks[-1] + 1, :, :, i, e],
                                pv[64 * e:64 * e + 64, :, :, r, :])
                    cp.then_inc(s["fw_taken"], 1)

            def head(i):
                dve.wait_ge(s["fc3_done"], 16 * (i + 1))
                if not (isinstance(i, int) and i == 0):
                    dve.wait_ge(s["tok_turned"], i)
                dve.tensor_scalar(logits[0:32, :], logit_ps[0:32, :], fc3_b[:], None, ALU.add
                                  ).then_inc(s["logit_taken"], 1)
                dve.wait_ge(s["tok_turned"], i + 1)
                if not (isinstance(i, int) and i == 0):
                    dve.wait_ge(s["tok_stored"], 32 * i)
                dve.tensor_copy(tok_rows[:].rearrange("p (a t j q) -> p a j t q", a=2, t=NCH, j=2),
                                logit_ps[:].rearrange("p (a j u) -> p a j u", a=2, j=2)[:, :, :, 0:32].rearrange(
                                    "p a j (t q) -> p a j t q", q=WQ)
                                ).then_inc(s["tok_ready"], 1)

            pipeline(dve, P, front, forward if P < LAYERS else head)

    def pool_program(pool):
        def step(ins, value):
            ins.then_inc(s["prep_step"], 1)
            pool.wait_ge(s["prep_step"], value)

        PS = 19
        pool.wait_ge(s["consts_ready"], 6)
        pv = prep_in[:].rearrange("p (t e m) -> p t e m", t=2, e=2)
        col_type = (0, 1, 1, 0)

        def load_chunk(layer, ky, n):
            for grp in range(4):
                first = 0 if grp in (0, 3) else 1
                for t in range(2):
                    kind = first ^ t
                    pool.dma_start(prep_in[32 * grp:32 * grp + 32, t * 2 * KX * CH:(t + 1) * 2 * KX * CH],
                                   io["mix_w"][layer, kind, ky]).then_inc(s["prep_loaded"], 16)

        def prep_chunk(layer, ky, n, first):
            load_chunk(layer, ky, n)
            pool.wait_ge(s["prep_loaded"], 128 * (n + 1))
            b = PS * n
            v3 = prep_in[:].rearrange("p (m o) -> p m o", o=CH)
            fold = prep_fold[:].rearrange("p (m o) -> p m o", o=CH // 2)
            step(pool.tensor_tensor(fold, v3[:, :, 0:16], v3[:, :, 16:32], ALU.add), b + 1)
            for n_, w in enumerate((8, 4, 2, 1)):
                step(pool.tensor_tensor(fold[:, :, 0:w], fold[:, :, 0:w], fold[:, :, w:2 * w], ALU.add),
                     b + 2 + n_)
            step(pool.tensor_tensor(fold[:, :, 0:1], fold[:, :, 0:1],
                                    sign[:, 8:9].unsqueeze(2).to_broadcast([128, 4 * KX, 1]), ALU.mult), b + 6)
            step(pool.tensor_tensor(v3, v3, fold[:, :, 0:1].to_broadcast([128, 4 * KX, CH]),
                                    ALU.subtract), b + 7)
            if not first:
                pool.wait_ge(s["prep_stored"], 16 * n)
            ov = prep_out[:].rearrange("p (k v o) -> p k v o", k=KX, v=4)
            tv = prep_tmp[:].rearrange("p (k o) -> p k o", k=KX)
            for v in range(4):
                src = [pv[:, col_type[v], e, :].rearrange("p (k o) -> p k o", k=KX) for e in range(2)]
                sg = [sign[:, 2 * v + e:2 * v + e + 1].unsqueeze(2).to_broadcast([128, KX, CH])
                      for e in range(2)]
                step(pool.tensor_tensor(tv, src[1], sg[1], ALU.mult), b + 8 + 3 * v)
                step(pool.tensor_tensor(ov[:, :, v, :], src[0], sg[0], ALU.mult), b + 9 + 3 * v)
                step(pool.tensor_tensor(ov[:, :, v, :], ov[:, :, v, :], tv, ALU.add), b + 10 + 3 * v)
            pool.dma_start(mix_dram[n], prep_out[:]).then_inc(s["prep_stored"], 16)

        prep_chunk(0, 0, 0, True)
        quads(pool, 1, KY, lambda ky: prep_chunk(0, ky, ky, False))
        for layer in range(1, LAYERS):
            quads(pool, 0, KY, lambda ky: prep_chunk(layer, ky, layer * KY + ky, False))

        def store_tokens(i):
            pool.wait_ge(s["tok_ready"], i + 1)
            for e in range(2):
                pool.dma_start(tok[i, e], tok_rows[64 * e:64 * e + 64, :].rearrange(
                    "p (a w) -> p a w", a=2)).then_inc(s["tok_stored"], 16)

        quads(pool, 0, nq, store_tokens)

    return s, sp_program, pe_program, act_program, dve_program, pool_program, h_out, locals()



D = 64
SEQ = SIDE + 1
HEADS, HD = 8, 8
WIN = 64
EXPERTS = 8
HID = 128
LHEADS, LHD, MEM = 4, 32, 4
KEYS = SEQ + MEM


def tail_constants():
    c = {}
    c["head_rows"] = np.kron(np.eye(HEADS), np.ones((HD, 1)))
    c["pair_mask"] = np.kron(np.eye(2), np.ones((WIN, HD))).reshape(2 * WIN, 1, 2 * HD) * np.ones((1, 4, 1))
    c["context_mask"] = np.kron(np.eye(LHEADS), np.ones((LHD, LHD))) * LHD ** -0.5
    c["mem_ident"] = np.broadcast_to(np.eye(MEM)[:, None, :], (MEM, 128, MEM))
    c["expert_no"] = np.broadcast_to(np.arange(EXPERTS), (128, EXPERTS))
    return {k: np.ascontiguousarray(np.asarray(v, np.float32).reshape(v.shape[0], -1)) for k, v in c.items()}


def token_transformer(nc, io, bank, sem, sb, tower_done, tokens, out):
    NIMG = tokens.shape[0] // SEQ
    NTOK = NIMG * SEQ
    NT = NTOK // 128
    XC = NT * D
    assert NT * 128 == NTOK and NIMG == 128

    h = sb("tok_h", [128, XC], F32)
    x = sb("tok_x", [128, XC], F32)
    area = [sb(f"area{n}", [128, NTOK + (NIMG * MEM if n == 0 else 0)], F32) for n in range(4)]
    y, y_last = area[3][:, 0:XC], area[0][:, 0:XC]
    stat = sb("stat", [128, 6 * NT], F32)
    seed = sb("tok_seed", [128, NT], mybir.dt.int32)
    small = sb("small", [128, 6 * NT * EXPERTS], F32)
    keys_ex = sb("keys_ex", [128, 2 * 512], F32)
    work = sb("work", [128, 2 * 512], F32)
    wide = sb("wide", [128, 2 * 512], F32)
    narrow = sb("narrow", [128, 4 * 128], F32)
    sums = sb("sums", [128, 2 * 32], F32)

    shapes = {k: io[k].shape for k in (
        "head_rows pair_mask context_mask mem_ident expert_no ident a_wq a_wk a_wv a_wproj a_bproj a_rel "
        "a_rel1 b_gamma b_beta b_wr b_br b_w1 b_b1 b_w2 b_b2 c_wq c_wk c_wv c_wout c_bout c_gout c_gpre "
        "d_w1 d_b1 d_wg d_bg d_wd d_bd").split()}
    groups = {"all": "ident expert_no", "a": "head_rows pair_mask a_wq a_wk a_wv a_wproj a_bproj a_rel a_rel1",
              "b": "b_gamma b_beta b_wr b_br b_w1 b_b1 b_w2 b_b2",
              "c": "context_mask c_wq c_wk c_wv c_wout c_bout c_gout c_gpre",
              "d": "d_w1 d_b1 d_wg d_bg d_wd d_bd"}
    groups = {g: v.split() for g, v in groups.items()}
    W = {}
    size = {g: sum(int(np.prod(shapes[k][1:])) for k in v) for g, v in groups.items()}
    w_all = sb("w_all", [128, size["all"]], F32)
    w_stage = sb("w_stage", [128, max(size[g] for g in "abcd")], F32)
    for g, v in groups.items():
        at = 0
        for k in v:
            n = int(np.prod(shapes[k][1:]))
            W[k] = (w_all if g == "all" else w_stage)[0:shapes[k][0], at:at + n]
            at += n
    ones_row = sb("ones_row", [1, 128], F32)
    ident = W["ident"]

    s = {n: sem("t_" + n) for n in (
        "in weights step x_ready ones turned turn_dve turn_act "
        "qk_ps qk_dve qk_act keys_ready scores_ps logits_ready probs_ready probs_turned probs_back v_ps v_ready "
        "mixed_ps mixed_norm mixed_turned mixed_back proj_ps proj_taken one_ps one_step one_prod one_p one_exp "
        "route_ps route_done hid_ps hid_act y_ps y_taken "
        "aug_ready kk_ps kk_max kk_exp kk_norm kk_turned kk_back vv_ps vv_back ctx_ps ctx_ready "
        "q_ps q_max q_exp q_ready q_turned q_back lin_ps lin_back w_ps w_taken "
        "stage_done out_done").split()}
    n_in = [0]

    def t3(ap, n=D):
        return ap.rearrange("p (t d) -> p t d", d=n)

    hv, xv, yv = t3(h[:]), t3(x[:]), t3(y)
    wide_row = lambda ap, n: ap.unsqueeze(1).to_broadcast([128, n, ap.shape[1]])
    N_STAGE = {g: len(v) for g, v in groups.items()}
    w_count, at = {}, 0
    for g in ("all", "a", "b", "c", "d"):
        at += N_STAGE[g] + (1 if g == "c" else 0)
        w_count[g] = 16 * at
    TURNS = [("dve", "act")[f % 2] for f in range(-(-NT // 4))]

    def sp_program(sp):
        tower_done(sp)
        sp.dma_start(hv, tokens.rearrange("(t p) d -> p t d", p=128)).then_inc(s["in"], 16)
        for n, g in enumerate(("all", "a", "b", "c", "d")):
            if n >= 2:
                sp.wait_ge(s["stage_done"], n - 1)
            for k in groups[g]:
                sp.dma_start(W[k], io[k]).then_inc(s["weights"], 16)
            if g == "c":
                sp.wait_ge(s["aug_ready"], 1)
                sp.dma_start(area[0][64:64 + MEM, :].rearrange("p (b n) -> p b n", n=KEYS)[:, :, SEQ:],
                             io["mem_ident"].rearrange("p (b n) -> p b n", n=MEM)).then_inc(s["weights"], 16)
        sp.wait_ge(s["stage_done"], 4)
        sp.dma_start(out, hv).then_inc(s["out_done"], 16)
        sp.wait_ge(s["out_done"], 16)

    turns = [0]

    def turn_pe(pe, stage):
        pe.wait_ge(s["x_ready"], stage + 1)
        for f in range(len(TURNS)):
            n = stage * len(TURNS) + f
            if n >= 2:
                pe.wait_ge(s["turn_" + ("dve", "act")[f % 2]], prior(stage, f))
            for t in range(4 * f, min(4 * f + 4, NT)):
                mm = nc.tensor.transpose(bank[f % 2][0:D, (t % 4) * 128:(t % 4 + 1) * 128], xv[:, t, :], ident)
            mm.then_inc(s["turned"], 1)

    nd, na = TURNS.count("dve"), TURNS.count("act")

    def prior(stage, f):
        return stage * (nd if f % 2 == 0 else na) + f // 2

    def turn_back(eng, copy, stage, parity):
        for f in range(parity, len(TURNS), 2):
            eng.wait_ge(s["turned"], stage * len(TURNS) + f + 1)
            n = min(4, NT - 4 * f) * 128
            copy(area[1][0:D, f * 512:f * 512 + n], bank[f % 2][0:D, 0:n]).then_inc(
                s["turn_" + ("dve", "act")[parity]], 1)

    def turned(eng, stage):
        eng.wait_ge(s["turn_dve"], nd * (stage + 1))
        eng.wait_ge(s["turn_act"], na * (stage + 1))

    a_copy = lambda o, i: nc.scalar.activation(o, i, ACT.Copy)
    v_copy = lambda o, i: nc.vector.tensor_copy(o, i)

    NP = NIMG // 2
    xT = area[1]
    qT, kT, oT = area[2], area[3], area[0]
    xw = xT[0:D, :].rearrange("p (b n) -> p b n", n=SEQ)
    ow = oT[0:D, 0:NTOK].rearrange("p (b n) -> p b n", n=SEQ)
    CHUNKS = [(f * 4, min(4, NT - f * 4)) for f in range(len(TURNS))]
    NG = -(-NT // 8)
    KI = 4
    NK = NIMG // KI

    def pe_program(pe):
        pe.wait_ge(s["weights"], w_count["a"])
        turn_pe(pe, 0)
        turned(pe, 0)
        for n in range(2 * NIMG // 8):
            c, which = divmod(n, 2)
            if n >= 2:
                pe.wait_ge(s["qk_dve" if which == 0 else "qk_act"], c)
            nc.tensor.matmul(bank[2 + which][0:D, :], W["a_wq" if which == 0 else "a_wk"],
                             xw[:, 8 * c:8 * c + 8, 0:WIN], start=True, stop=True).then_inc(s["qk_ps"], 1)
        pe.wait_ge(s["qk_dve"], NIMG // 8)
        pe.wait_ge(s["qk_act"], NIMG // 8)

        def scores(n):
            pe.wait_ge(s["keys_ready"], 2 * n + 2)
            if n >= 2:
                pe.wait_ge(s["logits_ready"], 1 * (n - 1))
            for e in range(2):
                b = 2 * n + e
                mm = nc.tensor.matmul(bank[n % 2][64 * e:64 * e + 64, :], qT[0:D, b * WIN:(b + 1) * WIN],
                                      keys_ex[0:D, e * 512:(e + 1) * 512], start=True, stop=True)
            mm.then_inc(s["scores_ps"], 1)

        def values(n):
            if n >= 1:
                pe.wait_ge(s["v_ready"], n)
            for e in range(2):
                for half in range(2):
                    mm = nc.tensor.matmul(bank[4][64 * half:64 * half + 64, e * D:(e + 1) * D],
                                          xw[:, 2 * n + e, 0:WIN], W["a_wv"], start=True, stop=True)
            mm.then_inc(s["v_ps"], 1)

        def mix(n):
            pe.wait_ge(s["probs_ready"], n + 1)
            if n >= 1:
                pe.wait_ge(s["probs_back"], n)
            for hp in range(4):
                mm = nc.tensor.transpose(bank[5][:, hp * 128:(hp + 1) * 128],
                                         wide[:, (n % 2) * 512 + hp * 128:(n % 2) * 512 + (hp + 1) * 128], ident)
            mm.then_inc(s["probs_turned"], 1)

        def apply(n):
            pe.wait_ge(s["probs_back"], n + 1)
            pe.wait_ge(s["v_ready"], n + 1)
            if n >= 1:
                pe.wait_ge(s["mixed_norm"], n)
            for e in range(2):
                for hp in range(4):
                    mm = nc.tensor.matmul(bank[6][64 * e:64 * e + 64, hp * 16:(hp + 1) * 16],
                                          work[:, hp * 128 + 64 * e:hp * 128 + 64 * e + 64],
                                          narrow[:, e * D + hp * 16:e * D + (hp + 1) * 16],
                                          start=True, stop=True)
            mm.then_inc(s["mixed_ps"], 1)

        def turn_mixed(n):
            pe.wait_ge(s["mixed_norm"], n + 1)
            if n >= 1:
                pe.wait_ge(s["mixed_back"], n)
            nc.tensor.transpose(bank[7][0:D, 0:128], narrow[:, 2 * D + (n % 2) * D:2 * D + (n % 2 + 1) * D],
                                ident).then_inc(s["mixed_turned"], 1)

        for n in range(NP + 2):
            if n < NP:
                scores(n)
                values(n)
            if 1 <= n <= NP:
                mix(n - 1)
                apply(n - 1)
            if n >= 2:
                turn_mixed(n - 2)
        last = xw[:, :, WIN]
        nc.tensor.matmul(bank[2][0:D, 0:128], W["a_wq"], last, start=True, stop=True)
        nc.tensor.matmul(bank[2][0:D, 128:256], W["a_wk"], last, start=True, stop=True)
        nc.tensor.matmul(bank[2][:, 256:256 + D], last, W["a_wv"], start=True, stop=True).then_inc(s["one_ps"], 1)
        pe.wait_ge(s["one_prod"], 1)
        nc.tensor.matmul(bank[3][:, 0:HEADS], work[0:D, 256:384], W["head_rows"], start=True, stop=True
                         ).then_inc(s["one_ps"], 1)
        pe.wait_ge(s["one_p"], 1)
        nc.tensor.transpose(bank[3][0:D, 128:256], work[:, 384:384 + D], ident).then_inc(s["one_ps"], 1)
        pe.wait_ge(s["one_p"], 2)
        pe.wait_ge(s["mixed_back"], NP)
        for g in range(NG):
            if g >= 2:
                pe.wait_ge(s["proj_taken"], g - 1)
            for t in range(8 * g, min(8 * g + 8, NT)):
                mm = nc.tensor.matmul(bank[g % 2][:, (t % 8) * D:(t % 8 + 1) * D],
                                      oT[0:D, t * 128:(t + 1) * 128], W["a_wproj"], start=True, stop=True)
            mm.then_inc(s["proj_ps"], 1)
        pe.wait_ge(s["proj_taken"], NG)

        pe.wait_ge(s["weights"], w_count["b"])
        turn_pe(pe, 1)
        turned(pe, 1)
        for t in range(NT):
            mm = nc.tensor.matmul(bank[2 + t // 64][:, (t % 64) * 8:(t % 64 + 1) * 8],
                                  xT[0:D, t * 128:(t + 1) * 128], W["b_wr"], start=True, stop=True)
        mm.then_inc(s["route_ps"], 1)
        pe.wait_ge(s["route_done"], 1)
        hidden_b = [wide[:, 0:512], wide[:, 512:1024]]
        units = [(c, e) for c in range(len(CHUNKS)) for e in range(EXPERTS)]

        def hid_b(u):
            c, e = units[u]
            if u >= 2:
                pe.wait_ge(s["hid_act"], u - 1)
            n = CHUNKS[c][1] * 128
            nc.tensor.matmul(bank[u % 2][:, 0:n], W["b_w1"][:, e * HID:(e + 1) * HID],
                             xT[0:D, c * 512:c * 512 + n], start=True, stop=True).then_inc(s["hid_ps"], 1)

        def out_b(u):
            c, e = units[u]
            pe.wait_ge(s["hid_act"], u + 1)
            if e == 0:
                if c >= 1:
                    pe.wait_ge(s["y_taken"], sum(k for _, k in CHUNKS[:c]))
                for j in range(CHUNKS[c][1]):
                    nc.tensor.matmul(bank[2 + j][:], ones_row[:], W["b_b2"], start=True, stop=False)
            for j in range(CHUNKS[c][1]):
                mm = nc.tensor.matmul(bank[2 + j][:, e * D:(e + 1) * D], hidden_b[u % 2][:, j * 128:(j + 1) * 128],
                                      W["b_w2"][:, e * D:(e + 1) * D], start=False, stop=(e == EXPERTS - 1))
            mm.then_inc(s["y_ps"], 1)

        for u in range(len(units) + 1):
            if u < len(units):
                hid_b(u)
            if u >= 1:
                out_b(u - 1)
        pe.wait_ge(s["y_taken"], NT)

        pe.wait_ge(s["weights"], w_count["c"])
        turn_pe(pe, 2)
        turned(pe, 2)
        q_rows(pe)
        pe.wait_ge(s["q_back"], len(CHUNKS))
        pe.wait_ge(s["aug_ready"], 2)
        aug = area[0][0:D + MEM, :]

        def keys(n):
            if n >= 1:
                pe.wait_ge(s["kk_norm"], n)
            nc.tensor.matmul(bank[0][:, 0:KI * KEYS], W["c_wk"], aug[:, n * KI * KEYS:(n + 1) * KI * KEYS],
                             start=True, stop=True).then_inc(s["kk_ps"], 1)
            if n >= 1:
                pe.wait_ge(s["vv_back"], n)
            for i in range(KI):
                b = n * KI + i
                mm = nc.tensor.matmul(bank[1][0:KEYS, i * 128:(i + 1) * 128], aug[:, b * KEYS:(b + 1) * KEYS],
                                      W["c_wv"], start=True, stop=True)
            mm.then_inc(s["vv_ps"], 1)

        def turn_keys(n):
            pe.wait_ge(s["kk_exp"], n + 1)
            if n >= 1:
                pe.wait_ge(s["kk_back"], n)
            for i in range(KI):
                mm = nc.tensor.transpose(bank[2][0:KEYS, i * 128:(i + 1) * 128],
                                         keys_ex[:, (n % 2) * 512 + i * KEYS:(n % 2) * 512 + (i + 1) * KEYS],
                                         ident)
            mm.then_inc(s["kk_turned"], 1)

        def context(n):
            pe.wait_ge(s["kk_back"], n + 1)
            if n >= 1:
                pe.wait_ge(s["ctx_ready"], n)
            for i in range(KI):
                c = (n % 2) * 512 + i * 128
                mm = nc.tensor.matmul(bank[3][:, i * 128:(i + 1) * 128], wide[0:KEYS, c:c + 128],
                                      work[0:KEYS, c:c + 128], start=True, stop=True)
            mm.then_inc(s["ctx_ps"], 1)

        def linear(n):
            pe.wait_ge(s["ctx_ready"], n + 1)
            if n >= 1:
                pe.wait_ge(s["lin_back"], n)
            for i in range(KI):
                b = n * KI + i
                mm = nc.tensor.matmul(bank[4][:, i * SEQ:(i + 1) * SEQ], narrow[:, i * 128:(i + 1) * 128],
                                      area[2][:, b * SEQ:(b + 1) * SEQ], start=True, stop=True)
            mm.then_inc(s["lin_ps"], 1)

        for n in range(NK + 2):
            if n < NK:
                keys(n)
            if 1 <= n <= NK:
                turn_keys(n - 1)
                context(n - 1)
            if n >= 2:
                linear(n - 2)
        pe.wait_ge(s["lin_back"], NK)
        for g in range(NG):
            if g >= 2:
                pe.wait_ge(s["w_taken"], g - 1)
            for t in range(8 * g, min(8 * g + 8, NT)):
                mm = nc.tensor.matmul(bank[g % 2][:, (t % 8) * D:(t % 8 + 1) * D],
                                      area[1][:, t * 128:(t + 1) * 128], W["c_wout"], start=True, stop=True)
            mm.then_inc(s["w_ps"], 1)
        pe.wait_ge(s["w_taken"], NG)

        pe.wait_ge(s["weights"], w_count["d"])
        turn_pe(pe, 3)
        turned(pe, 3)
        base = len(units)
        for u in range(2 * len(CHUNKS)):
            c, half = divmod(u, 2)
            pe.wait_ge(s["hid_act"], base + u - 1)
            n = CHUNKS[c][1] * 128
            nc.tensor.matmul(bank[u % 2][:, 0:n], W["d_w1"][:, half * HID:(half + 1) * HID],
                             xT[0:D, c * 512:c * 512 + n], start=True, stop=True).then_inc(s["hid_ps"], 1)
        pe.wait_ge(s["hid_act"], base + 2 * len(CHUNKS))
        for t in range(NT):
            for half in range(2):
                mm = nc.tensor.matmul(bank[2 + t // 64][:, (t % 64) * 8:(t % 64 + 1) * 8],
                                      area[2 + half][:, t * 128:(t + 1) * 128],
                                      W["d_wg"][:, half * 8:(half + 1) * 8],
                                      start=(half == 0), stop=(half == 1))
        mm.then_inc(s["route_ps"], 1)
        pe.wait_ge(s["route_done"], 2)
        for t in range(NT):
            if t >= 4:
                pe.wait_ge(s["y_taken"], NT + t - 3)
            nc.tensor.matmul(bank[4 + t % 4][:], ones_row[:], W["d_bd"], start=True, stop=False)
            for half in range(2):
                mm = nc.tensor.matmul(bank[4 + t % 4][:], area[2 + half][:, t * 128:(t + 1) * 128],
                                      W["d_wd"][:, half * 512:(half + 1) * 512],
                                      start=False, stop=(half == 1))
            mm.then_inc(s["y_ps"], 1)

    def q_rows(pe):
        def q_ps(f):
            if f >= 1:
                pe.wait_ge(s["q_ready"], f)
            for t in range(CHUNKS[f][0], CHUNKS[f][0] + CHUNKS[f][1]):
                mm = nc.tensor.matmul(bank[2][:, (t % 4) * 128:(t % 4 + 1) * 128],
                                      xT[0:D, t * 128:(t + 1) * 128], W["c_wq"], start=True, stop=True)
            mm.then_inc(s["q_ps"], 1)

        def q_turn(f):
            pe.wait_ge(s["q_ready"], f + 1)
            if f >= 1:
                pe.wait_ge(s["q_back"], f)
            for j in range(CHUNKS[f][1]):
                c = (f % 2) * 512 + j * 128
                mm = nc.tensor.transpose(bank[3][:, j * 128:(j + 1) * 128], wide[:, c:c + 128], ident)
            mm.then_inc(s["q_turned"], 1)

        for f in range(len(CHUNKS) + 1):
            if f < len(CHUNKS):
                q_ps(f)
            if f >= 1:
                q_turn(f - 1)

    def act_program(act):
        turn_back(act, a_copy, 0, 1)
        for c in range(NIMG // 8):
            act.wait_ge(s["qk_ps"], 2 * c + 2)
            a_copy(kT[0:D, c * 512:(c + 1) * 512], bank[3][0:D, :]).then_inc(s["qk_act"], 1)
        for n in range(NP + 2):
            if n < NP:
                act.wait_ge(s["logits_ready"], n + 1)
                if n >= 2:
                    act.wait_ge(s["probs_turned"], n - 1)
                c = slice((n % 2) * 512, (n % 2 + 1) * 512)
                nc.scalar.activation(wide[:, c], wide[:, c], ACT.Exp).then_inc(s["probs_ready"], 1)
            if 1 <= n <= NP:
                act.wait_ge(s["probs_turned"], n)
                if n >= 2:
                    act.wait_ge(s["mixed_ps"], n - 1)
                a_copy(work[:, 0:512], bank[5][:]).then_inc(s["probs_back"], 1)
            if n >= 2:
                m = n - 2
                act.wait_ge(s["mixed_turned"], m + 1)
                a_copy(ow[:, 2 * m:2 * m + 2, 0:WIN], bank[7][0:D, 0:128].rearrange("p (e n) -> p e n", e=2)
                       ).then_inc(s["mixed_back"], 1)
        act.wait_ge(s["one_step"], 1)
        nc.scalar.activation(small[:, 128:208], small[:, 0:80], ACT.Exp).then_inc(s["one_exp"], 1)
        turn_back(act, a_copy, 1, 1)
        act.wait_ge(s["step"], STEP["route_exp0"])
        nc.scalar.activation(small[:, 0:NT], small[:, 0:NT], ACT.Exp).then_inc(s["route_exp"], 1)
        hidden_b = [wide[:, 0:512], wide[:, 512:1024]]
        nu = len(CHUNKS) * EXPERTS
        for u in range(nu):
            c, e = divmod(u, EXPERTS)
            act.wait_ge(s["hid_ps"], u + 1)
            if u >= 2:
                act.wait_ge(s["y_ps"], u - 1)
            n = CHUNKS[c][1] * 128
            nc.scalar.activation(hidden_b[u % 2][:, 0:n], bank[u % 2][:, 0:n], ACT.Gelu,
                                 bias=W["b_b1"][:, e:e + 1]).then_inc(s["hid_act"], 1)
        turn_back(act, a_copy, 2, 1)
        for f in range(len(CHUNKS) + 1):
            if f < len(CHUNKS):
                n = CHUNKS[f][1] * 128
                c = (f % 2) * 512
                act.wait_ge(s["q_max"], f + 1)
                nc.scalar.activation(wide[:, c:c + n], wide[:, c:c + n], ACT.Exp).then_inc(s["q_exp"], 1)
            if f >= 1:
                n = CHUNKS[f - 1][1] * 128
                act.wait_ge(s["q_turned"], f)
                a_copy(area[2][:, (f - 1) * 512:(f - 1) * 512 + n], bank[3][:, 0:n]).then_inc(s["q_back"], 1)
        for n in range(NK + 2):
            if n < NK:
                act.wait_ge(s["vv_ps"], n + 1)
                if n >= 2:
                    act.wait_ge(s["ctx_ps"], n - 1)
                a_copy(work[0:KEYS, (n % 2) * 512:(n % 2 + 1) * 512], bank[1][0:KEYS, :]
                       ).then_inc(s["vv_back"], 1)
                act.wait_ge(s["kk_norm"], n + 1)
                c = (n % 2) * 512
                nc.scalar.activation(keys_ex[:, c:c + KI * KEYS], keys_ex[:, c:c + KI * KEYS], ACT.Exp
                                     ).then_inc(s["kk_exp"], 1)
            if 1 <= n <= NK:
                act.wait_ge(s["kk_turned"], n)
                if n >= 3:
                    act.wait_ge(s["ctx_ps"], n - 2)
                c = ((n - 1) % 2) * 512
                a_copy(wide[0:KEYS, c:c + 512], bank[2][0:KEYS, :]).then_inc(s["kk_back"], 1)
            if n >= 2:
                m = n - 2
                act.wait_ge(s["lin_ps"], m + 1)
                a_copy(area[1][:, m * KI * SEQ:(m + 1) * KI * SEQ], bank[4][:, 0:KI * SEQ]
                       ).then_inc(s["lin_back"], 1)
        turn_back(act, a_copy, 3, 1)
        for u in range(2 * len(CHUNKS)):
            c, half = divmod(u, 2)
            act.wait_ge(s["hid_ps"], nu + u + 1)
            n = CHUNKS[c][1] * 128
            nc.scalar.activation(area[2 + half][:, c * 512:c * 512 + n], bank[u % 2][:, 0:n], ACT.Gelu,
                                 bias=W["d_b1"][:, half:half + 1]).then_inc(s["hid_act"], 1)
        act.wait_ge(s["step"], STEP["gate_exp"])
        nc.scalar.activation(small[:, 0:NT * 8], small[:, 0:NT * 8], ACT.Exp).then_inc(s["route_exp"], 1)

    STEP = {}
    s["route_exp"] = sem("t_route_exp")

    V = nc.vector
    st = [stat[:, n * NT:(n + 1) * NT] for n in range(6)]

    def dve_program(dve, dry=False):
        count = [0]

        def link(f):
            count[0] += 1
            if not dry:
                f().then_inc(s["step"], 1)
                dve.wait_ge(s["step"], count[0])

        def wait(name, value):
            if not dry:
                dve.wait_ge(s[name], value)

        def do(f, name=None):
            if not dry:
                ins = f()
                if name:
                    ins.then_inc(s[name], 1)

        def bc(ap, n=D):
            return ap.unsqueeze(2).to_broadcast([128, ap.shape[1], n])

        def inverse_root(v, r):
            link(lambda: V.tensor_scalar(seed[:], v.bitcast(mybir.dt.int32), 1, None, ALU.logical_shift_right))
            link(lambda: V.tensor_scalar(r.bitcast(mybir.dt.int32), seed[:], -1.0, float(0x5F3759DF),
                                         ALU.mult, ALU.add))
            for _ in range(3):
                link(lambda: V.tensor_tensor(st[4], r, r, ALU.mult))
                link(lambda: V.scalar_tensor_tensor(out=st[4], in0=st[4], scalar=-0.5, in1=v,
                                                    op0=ALU.mult, op1=ALU.mult))
                link(lambda: V.scalar_tensor_tensor(out=r, in0=st[4], scalar=1.5, in1=r,
                                                    op0=ALU.add, op1=ALU.mult))

        def layer_norm(dst, src, spare):
            link(lambda: V.tensor_reduce(st[0], src, AX.X, ALU.add))
            link(lambda: V.tensor_scalar(st[0], st[0], 1.0 / D, None, ALU.mult))
            link(lambda: V.tensor_tensor(dst, src, bc(st[0]), ALU.subtract))
            link(lambda: V.tensor_tensor(spare, dst, dst, ALU.mult))
            link(lambda: V.tensor_reduce(st[1], spare, AX.X, ALU.add))
            link(lambda: V.tensor_scalar(st[1], st[1], 1.0 / D, EPS, ALU.mult, ALU.add))
            inverse_root(st[1], st[2])
            link(lambda: V.tensor_tensor(dst, dst, bc(st[2]), ALU.mult))

        def rms_norm(dst, src, spare, gain):
            link(lambda: V.tensor_tensor(spare, src, src, ALU.mult))
            link(lambda: V.tensor_reduce(st[1], spare, AX.X, ALU.add))
            link(lambda: V.tensor_scalar(st[1], st[1], 1e-24, None, ALU.max))
            inverse_root(st[1], st[2])
            link(lambda: V.tensor_scalar(st[2], st[2], float(D) ** 0.5, None, ALU.mult))
            link(lambda: V.tensor_tensor(dst, src, bc(st[2]), ALU.mult))
            link(lambda: V.tensor_tensor(dst, dst, wide_row(gain, NT), ALU.mult))

        wait("in", 16)
        do(lambda: V.memset(ones_row[:], 1.0), "ones")
        layer_norm(xv, hv, yv)
        do(lambda: V.engine_nop(), "x_ready")
        if not dry:
            turn_back(dve, v_copy, 0, 0)
        for c in range(NIMG // 8):
            wait("qk_ps", 2 * c + 1)
            do(lambda: v_copy(qT[0:D, c * 512:(c + 1) * 512], bank[2][0:D, :]), "qk_dve")
        wait("qk_act", NIMG // 8)
        wait("weights", w_count["a"])
        rel = W["a_rel"].unsqueeze(1).to_broadcast([128, HEADS, WIN])
        hr = W["head_rows"].unsqueeze(2).to_broadcast([D, HEADS, WIN])

        def keys(n):
            if n >= 1:
                wait("scores_ps", n)
            for e in range(2):
                b = 2 * n + e
                kb = kT[0:D, b * WIN:(b + 1) * WIN].unsqueeze(1).to_broadcast([D, HEADS, WIN])
                do(lambda: V.tensor_tensor(keys_ex[0:D, e * 512:(e + 1) * 512].rearrange(
                    "p (h k) -> p h k", h=HEADS), kb, hr, ALU.mult), "keys_ready")

        def soft(n):
            L = wide[:, (n % 2) * 512:(n % 2 + 1) * 512].rearrange("p (h k) -> p h k", h=HEADS)
            m = sums[:, (n % 2) * 32:(n % 2) * 32 + 8]
            wait("scores_ps", n + 1)
            if n >= 2:
                wait("probs_turned", n - 1)
            link(lambda: V.scalar_tensor_tensor(out=L, in0=bank[n % 2][:].rearrange("p (h k) -> p h k", h=HEADS),
                                                scalar=HD ** -0.5, in1=rel, op0=ALU.mult, op1=ALU.add))
            link(lambda: V.tensor_reduce(m, L, AX.X, ALU.max))
            do(lambda: V.tensor_tensor(L, L, bc(m, WIN), ALU.subtract), "logits_ready")

        def norm(n):
            L = wide[:, (n % 2) * 512:(n % 2 + 1) * 512].rearrange("p (h k) -> p h k", h=HEADS)
            z = sums[:, (n % 2) * 32 + 8:(n % 2) * 32 + 16]
            wait("v_ps", n + 1)
            if n >= 1:
                wait("mixed_ps", n)
            do(lambda: V.tensor_tensor(narrow[:, 0:2 * D].rearrange("p (e c) -> p e c", e=2),
                                       bank[4][:, 0:2 * D].rearrange("p (e c) -> p e c", e=2),
                                       W["pair_mask"].unsqueeze(1).to_broadcast([128, 2, D]), ALU.mult),
               "v_ready")
            wait("probs_ready", n + 1)
            link(lambda: V.tensor_reduce(z, L, AX.X, ALU.add))
            link(lambda: V.reciprocal(z, z))
            wait("mixed_ps", n + 1)
            if n >= 2:
                wait("mixed_turned", n - 1)
            o = narrow[:, 2 * D + (n % 2) * D:2 * D + (n % 2 + 1) * D]
            do(lambda: V.tensor_tensor(o.rearrange("p (h d) -> p h d", h=HEADS),
                                       bank[6][:, 0:D].rearrange("p (h d) -> p h d", h=HEADS),
                                       bc(z, HD), ALU.mult), "mixed_norm")

        for n in range(NP + 1):
            if n < NP:
                keys(n)
                soft(n)
            if n >= 1:
                norm(n - 1)
        wait("one_ps", 1)
        wait("probs_back", NP)
        link(lambda: V.tensor_copy(work[0:D, 0:128], bank[2][0:D, 0:128]))
        do(lambda: V.tensor_tensor(work[0:D, 256:384], work[0:D, 0:128], bank[2][0:D, 128:256], ALU.mult),
           "one_prod")
        lg, zk, mx, zmax = small[:, 0:8], small[:, 8:72], small[:, 72:80], small[:, 96:97]
        link(lambda: V.tensor_reduce(zmax, W["a_rel1"][:, 1:64], AX.X, ALU.max))
        link(lambda: V.tensor_tensor(zk, W["a_rel1"], zmax.to_broadcast([128, 64]), ALU.subtract))
        wait("one_ps", 2)
        link(lambda: V.tensor_scalar(lg, bank[3][:, 0:HEADS], HD ** -0.5, W["a_rel1"][:, 0:1],
                                     ALU.mult, ALU.add))
        link(lambda: V.tensor_tensor(mx, lg, zmax.to_broadcast([128, 8]), ALU.max))
        link(lambda: V.tensor_tensor(lg, lg, mx, ALU.subtract))
        link(lambda: V.tensor_tensor(mx, zmax.to_broadcast([128, 8]), mx, ALU.subtract))
        do(lambda: V.engine_nop(), "one_step")
        wait("one_exp", 1)
        p, ez, em, zs = small[:, 128:136], small[:, 137:200], small[:, 200:208], small[:, 208:209]
        z8 = small[:, 216:224]
        link(lambda: V.tensor_reduce(zs, ez, AX.X, ALU.add))
        link(lambda: V.tensor_scalar(z8, em, zs, None, ALU.mult))
        link(lambda: V.tensor_tensor(z8, z8, p, ALU.add))
        link(lambda: V.reciprocal(z8, z8))
        link(lambda: V.tensor_tensor(z8, z8, p, ALU.mult))
        do(lambda: V.tensor_tensor(work[:, 384:384 + D].rearrange("p (h d) -> p h d", h=HEADS),
                                   bank[2][:, 256:256 + D].rearrange("p (h d) -> p h d", h=HEADS),
                                   bc(z8, HD), ALU.mult), "one_p")
        wait("one_ps", 3)
        do(lambda: V.tensor_copy(ow[:, :, WIN], bank[3][0:D, 128:256]), "one_p")

        def add_rows(g, bias, target, done, ps):
            n = min(8, NT - 8 * g)
            r = target[:, 8 * g:8 * g + n]
            wait(ps, g + 1)
            link(lambda: V.tensor_tensor(r, r, t3(bank[g % 2][:, 0:n * D]), ALU.add))
            do(lambda: V.tensor_tensor(r, r, wide_row(bias, n), ALU.add), done)

        for g in range(NG):
            add_rows(g, W["a_bproj"], hv, "proj_taken", "proj_ps")
        wait("proj_taken", NG)
        do(lambda: V.engine_nop(), "stage_done")

        layer_norm(xv, hv, yv)
        layer_norm(xv, xv, yv)
        wait("weights", w_count["b"])
        link(lambda: V.tensor_tensor(xv, xv, wide_row(W["b_gamma"], NT), ALU.mult))
        link(lambda: V.tensor_tensor(xv, xv, wide_row(W["b_beta"], NT), ALU.add))
        do(lambda: V.engine_nop(), "x_ready")
        if not dry:
            turn_back(dve, v_copy, 1, 0)
        NE = NT * EXPERTS
        L, one1, one2, tmp, wgt = [small[:, n * NE:(n + 1) * NE].rearrange("p (t e) -> p t e", e=EXPERTS)
                                   for n in range(5)]
        flat = lambda v: v.rearrange("p t e -> p (t e)")
        en = wide_row(W["expert_no"], NT)

        def first_max(oh, values, m):
            link(lambda: V.tensor_reduce(m, values, AX.X, ALU.max))
            link(lambda: V.tensor_tensor(tmp, values, bc(m, EXPERTS), ALU.is_equal))
            link(lambda: V.tensor_scalar(oh, en, -float(EXPERTS), None, ALU.add))
            link(lambda: V.tensor_tensor(tmp, tmp, oh, ALU.mult))
            link(lambda: V.tensor_reduce(st[3], tmp, AX.X, ALU.min))
            link(lambda: V.tensor_tensor(oh, oh, bc(st[3], EXPERTS), ALU.is_equal))

        def route_in(bias):
            for a, b, ps in ((0, 64, bank[2]), (64, NT, bank[3])):
                link(lambda: V.tensor_tensor(L[:, a:b], t3(ps[:, 0:(b - a) * 8], 8),
                                             wide_row(bias, b - a), ALU.add))

        wait("route_ps", 1)
        route_in(W["b_br"])
        first_max(one1, L, st[0])
        link(lambda: V.scalar_tensor_tensor(out=L, in0=one1, scalar=-3.0e38, in1=L, op0=ALU.mult, op1=ALU.add))
        first_max(one2, L, st[1])
        link(lambda: V.tensor_tensor(small[:, 0:NT], st[1], st[0], ALU.subtract))
        STEP["route_exp0"] = count[0]
        wait("route_exp", 1)
        link(lambda: V.tensor_scalar(st[0], small[:, 0:NT], 1.0, None, ALU.add))
        link(lambda: V.reciprocal(st[0], st[0]))
        link(lambda: V.tensor_tensor(st[1], small[:, 0:NT], st[0], ALU.mult))
        link(lambda: V.tensor_tensor(wgt, one1, bc(st[0], EXPERTS), ALU.mult))
        link(lambda: V.tensor_tensor(tmp, one2, bc(st[1], EXPERTS), ALU.mult))
        link(lambda: V.tensor_tensor(wgt, wgt, tmp, ALU.add))
        do(lambda: V.engine_nop(), "route_done")

        def combine(t, ps, taken, yv=yv):
            w = work[:, (t % 2) * 512:(t % 2 + 1) * 512]
            do(lambda: V.tensor_tensor(t3(w), t3(ps[:]), bc(wgt[:, t], D), ALU.mult), "y_taken")
            wait("y_taken", taken)
            do(lambda: V.tensor_reduce(yv[:, t], w.rearrange("p (e d) -> p d e", e=EXPERTS), AX.X, ALU.add),
               None if t < NT - 1 else "y_sum")

        for c, (t0, k) in enumerate(CHUNKS):
            wait("y_ps", EXPERTS * (c + 1))
            for j in range(k):
                combine(t0 + j, bank[2 + j], t0 + j + 1)
        wait("y_sum", 1)
        link(lambda: V.tensor_tensor(h[:], h[:], y, ALU.add))
        do(lambda: V.engine_nop(), "stage_done")

        layer_norm(yv, hv, xv)
        wait("weights", w_count["c"] - 16)
        do(lambda: V.memset(area[0][0:D + MEM, :], 0.0), "aug_ready")
        rms_norm(xv, yv, t3(area[2][:, 0:XC]), W["c_gpre"])
        do(lambda: V.engine_nop(), "x_ready")
        if not dry:
            turn_back(dve, v_copy, 2, 0)
            turned(dve, 2)
        wait("weights", w_count["c"])
        do(lambda: V.tensor_copy(area[0][0:D, :].rearrange("p (b n) -> p b n", n=KEYS)[:, :, 0:SEQ],
                                 xw), "aug_ready")
        for f, (t0, k) in enumerate(CHUNKS):
            n = k * 128
            qv = wide[:, (f % 2) * 512:(f % 2) * 512 + n].rearrange("p (g d) -> p g d", d=LHD)
            m = sums[:, 0:4 * k]
            wait("q_ps", f + 1)
            link(lambda: V.tensor_reduce(m, bank[2][:, 0:n].rearrange("p (g d) -> p g d", d=LHD), AX.X, ALU.max))
            if f >= 2:
                wait("q_turned", f - 1)
            do(lambda: V.tensor_tensor(qv, bank[2][:, 0:n].rearrange("p (g d) -> p g d", d=LHD), bc(m, LHD),
                                       ALU.subtract), "q_max")
            wait("q_exp", f + 1)
            link(lambda: V.tensor_reduce(m, qv, AX.X, ALU.add))
            link(lambda: V.reciprocal(m, m))
            do(lambda: V.tensor_tensor(qv, qv, bc(m, LHD), ALU.mult), "q_ready")

        def key_max(n):
            kv = bank[0][:, 0:KI * KEYS].rearrange("p (i n) -> p i n", i=KI)
            dst = keys_ex[:, (n % 2) * 512:(n % 2) * 512 + KI * KEYS].rearrange("p (i n) -> p i n", i=KI)
            m = sums[:, (n % 2) * 32:(n % 2) * 32 + KI]
            wait("kk_ps", n + 1)
            link(lambda: V.tensor_reduce(m, kv, AX.X, ALU.max))
            if n >= 2:
                wait("kk_turned", n - 1)
            do(lambda: V.tensor_tensor(dst, kv, bc(m, KEYS), ALU.subtract), "kk_norm")

        def contexts(n):
            src = keys_ex[:, (n % 2) * 512:(n % 2) * 512 + KI * KEYS].rearrange("p (i n) -> p i n", i=KI)
            z = sums[:, (n % 2) * 32 + 8:(n % 2) * 32 + 8 + KI]
            wait("kk_exp", n + 1)
            link(lambda: V.tensor_reduce(z, src, AX.X, ALU.add))
            link(lambda: V.reciprocal(z, z))
            wait("ctx_ps", n + 1)
            if n >= 1:
                wait("lin_ps", n)
            for i in range(KI):
                do(lambda: V.scalar_tensor_tensor(out=narrow[:, i * 128:(i + 1) * 128],
                                                  in0=bank[3][:, i * 128:(i + 1) * 128], scalar=z[:, i:i + 1],
                                                  in1=W["context_mask"], op0=ALU.mult, op1=ALU.mult),
                   "ctx_ready" if i == KI - 1 else None)

        for n in range(NK + 1):
            if n < NK:
                key_max(n)
            if n >= 1:
                contexts(n - 1)
        wait("lin_ps", NK)
        for g in range(NG):
            n = min(8, NT - 8 * g)
            wait("w_ps", g + 1)
            do(lambda: V.tensor_tensor(xv[:, 8 * g:8 * g + n], t3(bank[g % 2][:, 0:n * D]),
                                       wide_row(W["c_bout"], n), ALU.add), "w_taken")
        wait("w_taken", NG)
        link(lambda: V.tensor_tensor(h[:], h[:], y, ALU.add))
        rms_norm(xv, xv, yv, W["c_gout"])
        link(lambda: V.tensor_tensor(h[:], h[:], x[:], ALU.add))
        do(lambda: V.engine_nop(), "stage_done")

        layer_norm(xv, hv, t3(y_last))
        do(lambda: V.engine_nop(), "x_ready")
        if not dry:
            turn_back(dve, v_copy, 3, 0)
        wait("weights", w_count["d"])
        wait("route_ps", 2)
        route_in(W["d_bg"])
        link(lambda: V.tensor_reduce(st[0], L, AX.X, ALU.max))
        link(lambda: V.tensor_tensor(L, L, bc(st[0], EXPERTS), ALU.subtract))
        STEP["gate_exp"] = count[0]
        wait("route_exp", 2)
        link(lambda: V.tensor_reduce(st[0], L, AX.X, ALU.add))
        link(lambda: V.reciprocal(st[0], st[0]))
        link(lambda: V.tensor_tensor(L, L, bc(st[0], EXPERTS), ALU.mult))
        first_max(one1, L, st[1])
        link(lambda: V.tensor_tensor(wgt, L, one1, ALU.mult))
        do(lambda: V.engine_nop(), "route_done")
        for t in range(NT):
            wait("y_ps", EXPERTS * len(CHUNKS) + t + 1)
            combine(t, bank[4 + t % 4], NT + t + 1, t3(y_last))
        wait("y_sum", 2)
        link(lambda: V.tensor_tensor(h[:], h[:], y_last, ALU.add))
        do(lambda: V.engine_nop(), "stage_done")

    s["y_sum"] = sem("t_y_sum")
    dve_program(None, dry=True)

    def pool_program(pool):
        pass

    return sp_program, pe_program, act_program, dve_program, pool_program

def lay_out(inp, nq):
    f = {k: np.asarray(v) for k, v in inp.items()}
    io = dict(constants())
    x = f['x'][:nq*QI]
    x = x.reshape(nq, QI, SIDE, WJ, WQ, 3)
    io['x'] = np.ascontiguousarray(x.transpose(0, 4, 5, 3, 1, 2).reshape(nq, 12, QCOLS))
    def blockdiag(w, n):
        z = np.zeros((n, w.shape[0], n, w.shape[1]), w.dtype)
        for q in range(n): z[q, :, q] = w
        return z.reshape(n * w.shape[0], n * w.shape[1])
    io['fc0_w'] = blockdiag(f['L0_tok_fc0_w'], WQ)
    io['conv_w'] = np.concatenate([blockdiag(f['L0_tok_conv_w'][l].T, WQ) for l in range(LAYERS)], 1)
    col = lambda first, rest: np.ascontiguousarray(np.tile(np.concatenate([first[None], rest]), (1, WQ)).T)
    io['bias_in'] = col(f['L0_tok_fc0_b'], f['L0_tok_conv_b'])
    io['gain'] = col(f['L0_tok_ln0_g'], f['L0_tok_ln_g'])
    io['shift'] = col(f['L0_tok_ln0_b'], f['L0_tok_ln_b'])
    io['fc1_w'] = np.tile(f['L0_tok_fc1_w'], (WQ, 1))
    io['fc1_b'] = f['L0_tok_fc1_b'][:, None]
    io['fc2_w'] = f['L0_tok_fc2_w']
    io['fc2_b'] = np.tile(f['L0_tok_fc2_b'], 2)[:, None]
    z = np.zeros((2, 64, 16, 32), np.float32)
    for pr in range(16):
        for e in range(2):
            z[e, :, pr, 2 * pr + e] = f['L0_tok_fc3_w'][:, 0]
    io['fc3_sel'] = z.reshape(128, 512)
    io['fc3_b'] = np.broadcast_to(f['L0_tok_fc3_b'][:, None], (32, 1))
    mw = np.zeros((LAYERS, 2, KY, CH, 2, KX, CH), np.float32)
    for kind, (a, b) in enumerate((('w1r', 'w2r'), ('w1i', 'w2i'))):
        wp, wm = f['L0_tok_' + a], f['L0_tok_' + b]
        mw[:, kind, :, :, 0, :12] = wp.transpose(0, 4, 1, 3, 2)
        mw[:, kind, :, :, 1, 1:] = wm[:, :, :, ::-1].transpose(0, 4, 1, 3, 2)
    io['mix_w'] = mw.reshape(LAYERS, 2, KY, CH, 2 * KX * CH)
    return {k: np.ascontiguousarray(v) for k, v in io.items()}


def lay_out_tail(inp):
    f = {k: np.asarray(v) for k, v in inp.items()}
    io = dict(tail_constants())
    over = lambda v: np.broadcast_to(v.reshape(1, -1), (128, v.size))
    w = f["L0_attn_w_qkv"].T
    io["a_wq"], io["a_wk"], io["a_wv"] = w[:, 0:64], w[:, 64:128], w[:, 128:192]
    io["a_wproj"] = f["L0_attn_w_proj"].T
    io["a_bproj"] = over(f["L0_attn_b_proj"])
    pos = np.arange(WIN)
    io["a_rel"] = np.tile(f["L0_attn_rel_bias"][pos[None, :] - pos[:, None] + WIN - 1], (2, 1))
    io["a_rel1"] = over(f["L0_attn_rel_bias"][WIN - 1:])
    io["b_gamma"], io["b_beta"] = over(f["L0_ffn_gamma"]), over(f["L0_ffn_beta"])
    io["b_wr"], io["b_br"] = f["L0_ffn_Wr"], over(f["L0_ffn_br"])
    io["b_w1"] = f["L0_ffn_W1"].transpose(1, 0, 2).reshape(D, -1)
    io["b_b1"] = f["L0_ffn_b1"].T
    io["b_w2"] = f["L0_ffn_W2"].transpose(1, 0, 2).reshape(HID, -1)
    io["b_b2"] = f["L0_ffn_b2"].reshape(1, -1)
    w, mem = f["L1_attn_w_qkv"], f["L1_attn_mem_kv"]
    io["c_wq"] = w[:, 0:128]
    io["c_wk"] = np.concatenate([w[:, 128:256], mem[0].reshape(128, MEM).T])
    io["c_wv"] = np.concatenate([w[:, 256:384], mem[1].reshape(128, MEM).T])
    io["c_wout"], io["c_bout"] = f["L1_attn_w_out"], over(f["L1_attn_b_out"])
    io["c_gout"], io["c_gpre"] = over(f["L1_attn_g_out"]), over(f["L1_attn_g_pre"])
    io["d_w1"] = f["L1_ffn_W1"]
    io["d_b1"] = f["L1_ffn_b1"].reshape(2, HID).T
    halves = lambda v: v.reshape(2, HID, -1).transpose(1, 0, 2).reshape(HID, -1)
    io["d_wg"], io["d_bg"] = halves(f["L1_ffn_Wg"]), over(f["L1_ffn_bg"])
    io["d_wd"] = halves(f["L1_ffn_Wd"].transpose(1, 0, 2))
    io["d_bd"] = f["L1_ffn_bd"].reshape(1, -1)
    io["cls"] = f["cls_tok"].reshape(1, -1)
    return {k: np.ascontiguousarray(v) for k, v in io.items()}


def build(nc, io, out, nq=32):
    with ExitStack() as ctx:
        bank = [ctx.enter_context(nc.psum_tensor(f"bank{n}", [128, CHUNK], F32)) for n in range(8)]

        def sem(name):
            return ctx.enter_context(nc.semaphore(name))

        tokens = nc.dram_tensor("tokens", [nq * QI * SEQ, D], F32, kind="Internal").ap()
        grid = tokens.rearrange("(q a e n) w -> q e n a w", a=2, e=2, n=SEQ)[:, :, 1:]
        with ExitStack() as first:
            tower = token_tower(
                nc, io, nq, bank, sem, lambda n, sh, dt: first.enter_context(nc.sbuf_tensor(n, sh, dt)),
                lambda n, sh, dt: nc.dram_tensor(n, sh, dt, kind="Internal").ap(), grid)
        ts = tower[0]

        def tower_done(sp):
            sp.dma_start(tokens.rearrange("(b n) w -> n b w", n=SEQ)[0],
                         io["cls"].to_broadcast([nq * QI, D])).then_inc(ts["cls_stored"], 16)
            sp.wait_ge(ts["cls_stored"], 16)
            sp.wait_ge(ts["tok_stored"], 32 * nq)

        rest = token_transformer(
            nc, io, bank, sem, lambda n, sh, dt: ctx.enter_context(nc.sbuf_tensor(n, sh, dt)), tower_done,
            tokens, out.rearrange("b n d -> (b n) d").rearrange("(t p) d -> p t d", p=128))
        block = ctx.enter_context(nc.Block())

        @block.sync
        def _(sp):
            tower[1](sp)
            rest[0](sp)

        @block.tensor
        def _(pe):
            tower[2](pe)
            rest[1](pe)

        @block.scalar
        def _(act):
            tower[3](act)
            rest[2](act)

        @block.vector
        def _(dve):
            tower[4](dve)
            rest[3](dve)

        @block.gpsimd
        def _(pool):
            tower[5](pool)


def kernel(**inputs):
    import concourse.bacc as bacc
    from concourse.bass_utils import run_bass_kernel_spmd

    nc = bacc.Bacc("TRN2", target_bir_lowering=False, num_devices=1)
    arrays = {f"in_{k}": v for k, v in {**lay_out(inputs, 32), **lay_out_tail(inputs)}.items()}
    io = {k[3:]: nc.dram_tensor(k, v.shape, mybir.dt.from_np(v.dtype), kind="ExternalInput").ap()
          for k, v in arrays.items()}
    out = nc.dram_tensor("out", (128, SEQ, D), F32, kind="ExternalOutput").ap()
    build(nc, io, out)
    return run_bass_kernel_spmd(nc, [arrays], core_ids=[0]).results[0]["out"]
```

```python
from contextlib import ExitStack

import numpy as np

import concourse.bass as bass
from concourse import mybir

ALU = mybir.AluOpType
ACT = mybir.ActivationFunctionType
AX = mybir.AxisListType
F32 = mybir.dt.float32
BF16 = mybir.dt.bfloat16
F16 = mybir.dt.float16

SIDE = 64
CH = 32
LAYERS = 4
KY = 12
KX = 13
WQ = 4
WJ = SIDE // WQ
QI = 4
CHUNK = 512
QCOLS = WJ * QI * SIDE
NCH = QCOLS // CHUNK
EPS = 1e-5
SK = 2 * KX
RK = 2 * KY
MODES = KY * KX
VCOLS = CH // 4 * 2 * KX * QI
D_FILLS, A_FILLS, B_FILLS, T_FILLS = 4, 4, 2, 4
W_SCALE = 64.0
MIX_SCALE = 1.0 / 8
INV_SCALE = W_SCALE / MIX_SCALE
B_SETS = (range(0, 7), range(7, 13))


def split16(v):
    high = v.astype(np.float16)
    return np.concatenate([high, (v - high.astype(v.dtype)).astype(np.float16)], 1)


def constants():
    y = np.arange(SIDE)
    ky, kx = np.arange(KY), np.arange(KX)
    th = 2 * np.pi * np.outer(y, kx) / SIDE
    ph = 2 * np.pi * np.outer(y, ky) / SIDE
    fy = np.concatenate([np.cos(th), np.sin(th)], 1)
    fw = np.concatenate([np.cos(ph), np.sin(ph)], 1)
    two = np.eye(2)
    weight = INV_SCALE * np.where(ky == 0, 1.0, 2.0)[:, None] / SIDE ** 2
    iw = np.concatenate([weight * np.cos(ph.T), -weight * np.sin(ph.T)], 0)
    iy = fy.T
    c = {
        "fwd_y": np.kron(two, fy),
        "fwd_w": np.kron(two, fw),
        "inv_w": np.einsum("rw,ab->rabw", iw, np.eye(4)).reshape(RK * 4, 4 * SIDE),
        "inv_y": np.einsum("sy,ab->saby", iy, np.eye(QI)).reshape(SK * QI, QI * SIDE),
        "ident": np.eye(128),
        "center": np.eye(128) - np.kron(np.eye(4), np.full((CH, CH), 1.0 / CH)),
    }
    c["mean_sel"] = np.kron(np.eye(WQ), np.full((CH, 1), 1.0 / CH))
    back = np.zeros((96, NCH, 128))
    for part in range(3):
        for q in range(WQ):
            for t in range(NCH):
                back[part * 32 + t * WQ + q, t, q * CH:(q + 1) * CH] = 1.0
    c["spread_sel"] = back.reshape(96, NCH * 128)
    pos = np.array([[1, 1, 1, -1], [1, -1, -1, -1], [-1, 1, 1, 1], [1, 1, 1, -1]], float).T
    neg = np.array([[1, -1, 1, 1], [1, 1, -1, 1], [1, 1, -1, 1], [-1, 1, -1, -1]], float).T
    signs = np.stack([pos, neg], 2).reshape(4, 8)
    c["sign"] = np.repeat(np.concatenate([signs, np.full((4, 1), 1.0 / CH), np.ones((4, 1))], 1), CH, 0)
    out = {k: v.astype(np.float32) for k, v in c.items()}
    for name in ("fwd_y", "fwd_w", "inv_w", "inv_y"):
        out[name] = split16(c[name])
    out["ident16"] = c["ident"].astype(np.float16)
    return {k: np.ascontiguousarray(v) for k, v in out.items()}


def token_tower(nc, io, nq, bank, sem, sb, dram, tok):
    ni = nq * QI

    h_dram = dram("h_dram", [nq, 128, 2 * QCOLS], F16)
    mix_dram = dram("mix_dram", [LAYERS * KY, 128, KX * 128], F32)
    spec_dram = dram("spec_dram", [nq, RK, 4 * VCOLS], F32)

    fwd_y = sb("fwd_y", [128, 2 * 2 * SK], F16)
    fwd_w = sb("fwd_w", [128, 2 * 2 * RK], F16)
    inv_w = sb("inv_w", [96, 2 * 4 * SIDE], F16)
    inv_y = sb("inv_y", [SK * QI, 2 * QI * SIDE], F16)
    ident = sb("ident", [128, 128], F32)
    ident16 = sb("ident16", [128, 128], F16)
    center = sb("center", [128, 128], F32)
    mean_sel = sb("mean_sel", [128, WQ], F32)
    ident_b = sb("ident_b", [128, 128], BF16)
    spread_sel = sb("spread_sel", [96, NCH * 128], BF16)
    sign = sb("sign", [128, 10], F32)
    fc0_w = sb("fc0_w", [12, 128], F32)
    conv_w = sb("conv_w", [128, 2 * LAYERS * 128], F16)
    col_sum = sb("col_sum", [128, LAYERS * 4], F32)
    bias_in = sb("bias_in", [128, LAYERS + 1], F32)
    bias = sb("bias", [128, LAYERS + 1], F32)
    gain = sb("gain", [128, LAYERS + 1], F32)
    shift = sb("shift", [128, LAYERS + 1], F32)
    fc1_w = sb("fc1_w", [128, 2 * WQ * 128], F16)
    fc1_b = sb("fc1_b", [128, 1], F32)
    fc2_w = sb("fc2_w", [128, 2 * 64], F16)
    fc2_b = sb("fc2_b", [128, 1], F32)
    fc3_sel = sb("fc3_sel", [128, 2 * 16 * 32], F16)
    fc3_b = sb("fc3_b", [32, 1], F32)

    h_in = sb("h_in", [128, QCOLS], F32)
    h_next = sb("h_next", [128, QCOLS], F32)
    dev = sb("dev", [128, QCOLS], F32)
    rows = sb("rows", [128, QCOLS], F32)
    SQ = 3
    squares = sb("squares", [128, SQ * CHUNK], F32)
    spec_y = sb("spec_y", [128, 2 * CH * 2 * SK], F16)
    half_inv = sb("half_inv", [SK * QI, 2 * CH * SIDE], F16)
    mixed_in = sb("mixed_in", [96, VCOLS], F32)
    mixed = sb("mixed", [96, 2 * VCOLS], F16)
    spec = sb("spec", [128, MODES * ni], F32)
    var_eps = sb("var_eps", [128, 128], F32)
    seed = sb("seed", [128, 128], mybir.dt.int32)
    rstd = sb("rstd", [128, 128], F32)
    newton = sb("newton", [128, 128], F32)
    rest = sb("rest", [128, 128], F32)
    split = sb("split", [128, 4 * 96], BF16)
    parts = sb("parts", [96, CHUNK], BF16)
    prep_in = sb("prep_in", [128, 4 * KX * CH], F32)
    prep_fold = sb("prep_fold", [128, 4 * KX * CH // 2], F32)
    prep_tmp = sb("prep_tmp", [128, KX * CH], F32)
    prep_out = sb("prep_out", [128, KX * 128], F32)
    stage_cols = nq * KX * QI
    h_in16, h_next16, rows16 = (t[:].bitcast(F16) for t in (h_in, h_next, rows))
    spec16 = spec[:].bitcast(F16)
    H1, H2 = 4, 2
    hidden1_full = [rows[:, b * CHUNK:(b + 1) * CHUNK] for b in range(H1)]
    hidden1 = [[rows16[:, (2 * H1 + 2 * b + e) * CHUNK:(2 * H1 + 2 * b + e + 1) * CHUNK] for e in range(2)]
               for b in range(H1)]
    hidden2_full = [spec[:, b * CHUNK:(b + 1) * CHUNK] for b in range(H2)]
    hidden2 = [[spec16[:, (2 * H2 + 2 * b + e) * CHUNK:(2 * H2 + 2 * b + e + 1) * CHUNK] for e in range(2)]
               for b in range(H2)]
    logits = spec_y[:].bitcast(F32)[:, 0:CHUNK]
    tok_rows = spec_y[:].bitcast(F32)[:, CHUNK:CHUNK + 2 * SIDE]
    raw, at = {}, 0
    for name, p, cols in (("spread_sel", 96, NCH * 128), ("conv_w", 128, LAYERS * 128),
                          ("fc1_w", 128, WQ * 128), ("fc2_w", 128, 64), ("fc3_sel", 128, 16 * 32)):
        raw[name] = dev[0:p, at:at + cols]
        at += cols

    PASSES = ((0, 0), (1, 0), (0, 1))

    def product(out, left, right, start=True, stop=True):
        for n, (a, b) in enumerate(PASSES):
            mm = nc.tensor.matmul(out, left(a), right(b), start=start and n == 0, stop=stop and n == 2)
        return mm

    turn_ps, inv_ps, conv_ps = (bank[0], bank[1]), (bank[2], bank[3]), (bank[4], bank[5])
    var_ps, logit_ps = bank[6], bank[7]

    names = ("consts_in consts_ready h_loaded0 h_loaded1 h_loaded2 h_loaded3 mixed_loaded mixed_high mixed_split h_stored spec_stored0 spec_stored1 "
             "mix_loaded0 mix_loaded1 prep_loaded prep_stored tok_stored prep_step "
             "inv_half_ps inv_half_high inv_half conv_done dev_ready square_ready var_added split_ready "
             "parts_turned rstd_step fold_step cls_stored parts_ready spread_done normed gelu_done "
             "h_high h_ready turned_high turned_low turn_dve turn_act fy_done fy_high fy_taken "
             "fw_done fw_taken mix_done mix_act mix_dve bias_ps "
             "fc1_done fc1_act high1 low1 fc2_done fc2_act high2 low2 fc3_done logits_zero logit_taken tok_turned tok_ready")
    s = {n: sem(n) for n in names.split()}

    v_mix_w = [h_next[:, b * KX * 128:(b + 1) * KX * 128] for b in range(2)]
    v_stage = [dev[:, b * stage_cols:(b + 1) * stage_cols] for b in range(2)]
    spec_v = spec[:].rearrange("p (q k n) -> p q k n", q=KY, k=KX)

    loads = [(t[:], n) for t, n in (
        (fwd_y, "fwd_y"), (fwd_w, "fwd_w"), (inv_w, "inv_w"), (inv_y, "inv_y"), (ident, "ident"),
        (ident16, "ident16"), (center, "center"), (mean_sel, "mean_sel"), (sign, "sign"), (fc0_w, "fc0_w"),
        (bias_in, "bias_in"), (gain, "gain"), (shift, "shift"), (fc1_b, "fc1_b"), (fc2_b, "fc2_b"),
        (fc3_b, "fc3_b"))] + [(raw[n], n) for n in raw]
    N_CONST = 16 * len(loads)
    MIX_SETS = (range(0, 4), range(4, 8), range(8, 12), range(12, 13))

    def quads(eng, first, last, body):
        if last - first == 1:
            body(first)
        elif last > first:
            with eng.Fori(first, last) as i:
                body(i)

    def pipeline(eng, P, front, back):
        front(0)
        peeled = 2 if P in (0, LAYERS) else 1
        if peeled == 2:
            front(1)
        quads(eng, peeled, nq - 1, front)
        front(nq - 1, last=True)
        back(nq - 1)

    def is_first(i):
        return isinstance(i, int) and i == 0

    def h_piece(h, piece):
        return h.rearrange("p (e c) -> p e c", e=2)[:, :, 2 * piece * CHUNK:2 * (piece + 1) * CHUNK]

    def half_view(part, f):
        return half_inv[:].rearrange("p (h w o e) -> p h e o w", h=2, w=SIDE, e=8)[:, part, 2 * f:2 * f + 2]

    def rows_view(part, f):
        return rows16.rearrange("p (h a w c) -> p h w a c", h=2, a=2, w=WJ)[:, part, 4 * f:4 * f + 4]

    def spec_y_view(part, f):
        return spec_y[:].rearrange("p (h k e c) -> p h c e k", h=2, k=KX, c=CH)[:, part, 8 * f:8 * f + 8]

    HEAD_STEPS = 39
    CONST_STEPS = 13
    PREP_STEPS = 19

    def sp_program(sp):
        for t, name in loads:
            sp.dma_start(t, io[name]).then_inc(s["consts_in"], 16)
        for P in range(LAYERS + 1):
            if P > 0:
                sp.wait_ge(s["turned_low"], T_FILLS * P * nq)
                for piece in range(4):
                    sp.dma_start(h_piece(h_in16, piece), h_piece(h_dram[0], piece)
                                 ).then_inc(s[f"h_loaded{piece}"], 16)
                for ky in range(KY + 2):
                    n = (P - 1) * KY + ky
                    if ky >= 2:
                        sp.wait_ge(s["mix_act"], 2 * (n - 1))
                        sp.wait_ge(s["mix_dve"], 2 * (n - 1))
                        dst = spec_dram.rearrange("a (r q) (o s m) -> r s q o a m", r=2, o=CH, s=2)
                        src = v_stage[ky % 2].rearrange("p (a m) -> p a m", a=nq)
                        for sr in range(4):
                            sp.dma_start(dst[sr % 2, sr // 2, ky - 2], src[32 * sr:32 * sr + 32]
                                         ).then_inc(s[f"spec_stored{ky % 2}"], 16)
                    if ky < KY:
                        sp.wait_ge(s["prep_stored"], 16 * (n + 1))
                        if ky >= 2:
                            sp.wait_ge(s["mix_done"], 4 * (n - 1))
                        sp.dma_start(v_mix_w[ky % 2], mix_dram[n]).then_inc(s[f"mix_loaded{ky % 2}"], 16)

            def load_mixed(i, P=P):
                sp.dma_start(mixed_in[:], spec_dram[i].rearrange("r (a c) -> (r a) c", a=4)
                             ).then_inc(s["mixed_loaded"], 16)

            def store_h(i, P=P):
                sp.wait_ge(s["h_ready"], 8 * (P * nq + i + 1))
                sp.dma_start(h_dram[i], h_next[:].bitcast(F16)).then_inc(s["h_stored"], 16)

            def store_prep(ky, P=P):
                sp.wait_ge(s["prep_step"], PREP_STEPS * (P * KY + ky + 1))
                sp.dma_start(mix_dram[P * KY + ky], prep_out[:]).then_inc(s["prep_stored"], 16)

            def load_prep(ky, P=P):
                for grp in range(4):
                    first = 0 if grp in (0, 3) else 1
                    for t in range(2):
                        sp.dma_start(prep_in[32 * grp:32 * grp + 32, t * 2 * KX * CH:(t + 1) * 2 * KX * CH],
                                     io["mix_w"][P, first ^ t, ky]).then_inc(s["prep_loaded"], 16)

            def one(i, prep=False, last=False, P=P):
                g = P * nq + i
                first = isinstance(i, int) and i == 0
                for piece in range(4):
                    if not first:
                        sp.wait_ge(s["conv_done"], 8 * (g - 1) + 2 * piece + 2)
                    if P == 0:
                        cols = slice(2 * piece * CHUNK, 2 * (piece + 1) * CHUNK)
                        sp.dma_start(h_in[0:12, cols], io["x"][i][:, cols]
                                     ).then_inc(s[f"h_loaded{piece}"], 16)
                    elif not first:
                        sp.dma_start(h_piece(h_in16, piece), h_piece(h_dram[i], piece)
                                     ).then_inc(s[f"h_loaded{piece}"], 16)
                if P > 0:
                    if first:
                        sp.wait_ge(s["spec_stored0"], 32 * KY * P)
                        sp.wait_ge(s["spec_stored1"], 32 * KY * P)
                        load_mixed(0)
                    if not last:
                        sp.wait_ge(s["mixed_split"], g - nq + 1)
                        load_mixed(i + 1)
                if prep:
                    if not first:
                        store_prep(i - 1)
                    load_prep(i)
                if P < LAYERS and not first:
                    store_h(i - 1)

            preps = min(KY, nq - 1) if P < LAYERS else 1
            if P < LAYERS and P > 0:
                sp.wait_ge(s["prep_stored"], 16 * P * KY)
            one(0, prep=P < LAYERS)
            quads(sp, 1, preps, lambda i: one(i, prep=True))
            if P < LAYERS:
                store_prep(preps - 1)
            quads(sp, preps, nq - 1, one)
            one(nq - 1, last=True)
            if P < LAYERS:
                for ky in range(preps, KY):
                    load_prep(ky)
                    store_prep(ky)
                store_h(nq - 1)
                sp.wait_ge(s["h_stored"], 16 * (P + 1) * nq)
        sp.wait_ge(s["tok_stored"], 32 * nq)

    def pe_program(pe):
        pe.wait_ge(s["consts_in"], N_CONST)
        nc.tensor.matmul(logit_ps[:, 0:LAYERS + 1], center[:], bias_in[:], start=True, stop=True
                         ).then_inc(s["bias_ps"], 1)
        pe.wait_ge(s["consts_ready"], CONST_STEPS)
        for P in range(LAYERS + 1):
            if P > 0:
                pe.wait_ge(s["fw_taken"], B_FILLS * P * nq)
                for ky in range(KY):
                    n = (P - 1) * KY + ky
                    pe.wait_ge(s[f"mix_loaded{ky % 2}"], 16 * (n // 2 + 1))
                    for f, ks in enumerate(MIX_SETS):
                        ps = (turn_ps + inv_ps)[f]
                        if n > 0:
                            pe.wait_ge(s["mix_act" if f % 2 == 0 else "mix_dve"], 2 * (n - 1) + f // 2 + 1)
                        for j, k in enumerate(ks):
                            mm = nc.tensor.matmul(ps[:, j * ni:(j + 1) * ni],
                                                  v_mix_w[ky % 2][:, k * 128:(k + 1) * 128],
                                                  spec_v[:, ky, k, :], start=True, stop=True)
                        mm.then_inc(s["mix_done"], 1)
                pe.wait_ge(s["mix_act"], 2 * P * KY)
                pe.wait_ge(s["mix_dve"], 2 * P * KY)

            def inverse_w(i, f, P=P):
                gd = (P - 1) * nq + i
                if f == 0:
                    pe.wait_ge(s["mixed_split"], gd + 1)
                if f >= 2:
                    pe.wait_ge(s["inv_half"], D_FILLS * gd + f - 1)
                mv = mixed[:].rearrange("p (e o m) -> p e o m", e=2, o=8)
                for j in range(2):
                    mm = product(inv_ps[f % 2][0:SK * QI, j * 256:(j + 1) * 256],
                                 lambda e: mv[:, e, 2 * f + j, :],
                                 lambda e: inv_w[:, e * 256:(e + 1) * 256])
                mm.then_inc(s["inv_half_ps"], 1)

            def front(i, last=False, P=P):
                g = P * nq + i
                start = P == 0 and is_first(i)
                if P > 0:
                    if is_first(i):
                        for f in range(D_FILLS):
                            inverse_w(0, f)
                    pe.wait_ge(s["inv_half"], D_FILLS * (g - nq + 1))

                def add_var(t):
                    pe.wait_ge(s["square_ready"], 8 * g + t + 1)
                    if t == 0 and not start:
                        pe.wait_ge(s["parts_ready"], g)
                    for j in range(4):
                        c = (t % SQ) * CHUNK + j * 128
                        o = j * 32 + t * WQ
                        mm = nc.tensor.matmul(var_ps[:, o:o + WQ], squares[:, c:c + 128], mean_sel[:],
                                              start=True, stop=True)
                    mm.then_inc(s["var_added"], 1)

                hv = half_inv[:].rearrange("p (e w o) -> p e w o", e=2, w=SIDE)
                for t in range(NCH):
                    if t % 2 == 0:
                        pe.wait_ge(s[f"h_loaded{t // 2}"], 16 * (g + 1))
                    if t >= 2:
                        pe.wait_ge(s["dev_ready"], 8 * g + t - 1)
                    elif not start:
                        pe.wait_ge(s["normed"], 8 * g - 1 + t)
                    cols = slice(t * CHUNK, (t + 1) * CHUNK)
                    if P == 0:
                        mm = nc.tensor.matmul(conv_ps[t % 2][:], fc0_w[:], h_in[0:12, cols],
                                              start=True, stop=True)
                    else:
                        product(conv_ps[t % 2][:],
                                lambda e: conv_w[:, (e * LAYERS + P - 1) * 128:(e * LAYERS + P) * 128],
                                lambda e: h_in16[:, e * QCOLS + t * CHUNK:e * QCOLS + (t + 1) * CHUNK],
                                stop=False)
                        for j in range(2):
                            wj = 2 * t + j
                            mm = product(conv_ps[t % 2][:, j * 256:(j + 1) * 256],
                                         lambda e: hv[:, e, wj * WQ:(wj + 1) * WQ, :],
                                         lambda e: inv_y[:, e * 256:(e + 1) * 256],
                                         start=False, stop=(j == 1))
                    mm.then_inc(s["conv_done"], 1)
                    if t >= 2:
                        add_var(t - 2)
                    if P < LAYERS and not is_first(i):
                        forward_step(i - 1, t)
                add_var(NCH - 2)
                add_var(NCH - 1)
                if P < LAYERS and not is_first(i):
                    forward_step(i - 1, NCH)
                elif P == LAYERS and not is_first(i):
                    head(i - 1)
                pe.wait_ge(s["split_ready"], g + 1)
                for j in range(4):
                    mm = nc.tensor.matmul(var_ps[0:96, j * 128:(j + 1) * 128],
                                          split[:, j * 96:(j + 1) * 96], ident_b[:], start=True, stop=True)
                mm.then_inc(s["parts_turned"], 1)
                if P < LAYERS and not is_first(i):
                    forward_w(i - 1)
                pe.wait_ge(s["parts_ready"], g + 1)
                for t in range(NCH):
                    if t < 2:
                        pe.wait_ge(s["dev_ready"], 8 * g + 7 + t)
                    else:
                        pe.wait_ge(s["normed"], 8 * g + t - 1)
                    nc.tensor.matmul(conv_ps[t % 2][:], spread_sel[:, t * 128:(t + 1) * 128], parts[:],
                                     start=True, stop=True).then_inc(s["spread_done"], 1)
                    if P > 0 and not last and t % 2 == 1:
                        inverse_w(i + 1, t // 2)

            def forward_step(i, t, P=P):
                g = P * nq + i
                if 1 <= t <= T_FILLS:
                    f = t - 1
                    pe.wait_ge(s["h_ready"], 8 * g + 2 * f + 2)
                    if f == 0 and not (P == 0 and is_first(i)):
                        pe.wait_ge(s["fw_taken"], B_FILLS * g)
                    for e, name, left in ((0, "turned_high", "turn_act"), (1, "turned_low", "turn_dve")):
                        if f > 0:
                            pe.wait_ge(s[left], T_FILLS * g + f)
                        ps = turn_ps[e][:].bitcast(F16)
                        for j in range(8):
                            c = e * QCOLS + 2 * f * CHUNK + j * 128
                            mm = nc.tensor.transpose(ps[:, j * 128:(j + 1) * 128],
                                                     h_next16[:, c:c + 128], ident16[:])
                        mm.then_inc(s[name], 1)
                if t > T_FILLS:
                    f = t - T_FILLS - 1
                    if f == 0:
                        pe.wait_ge(s["turn_dve"], T_FILLS * (g + 1))
                        pe.wait_ge(s["turn_act"], T_FILLS * (g + 1))
                    if f >= 2:
                        pe.wait_ge(s["fy_taken"], A_FILLS * g + f - 1)
                    rv = rows16.rearrange("p (e a w c) -> p e a w c", e=2, a=2, w=SIDE)
                    for j in range(8):
                        mm = product(inv_ps[f % 2][:, j * 2 * SK:(j + 1) * 2 * SK],
                                     lambda e: rv[:, e, :, :, 8 * f + j],
                                     lambda e: fwd_y[:, e * 2 * SK:(e + 1) * 2 * SK])
                    mm.then_inc(s["fy_done"], 1)

            def forward_w(i, P=P):
                pe.wait_ge(s["fy_taken"], A_FILLS * (P * nq + i + 1))
                yv = spec_y[:].rearrange("p (e k m) -> p e k m", e=2, k=KX)
                for f, ks in enumerate(B_SETS):
                    for j, k in enumerate(ks):
                        mm = product(turn_ps[f][:, j * 2 * RK:(j + 1) * 2 * RK],
                                     lambda e: yv[:, e, k, :],
                                     lambda e: fwd_w[:, e * 2 * RK:(e + 1) * 2 * RK])
                    mm.then_inc(s["fw_done"], 1)

            def forward(i):
                for t in range(1, NCH + 1):
                    forward_step(i, t)
                forward_w(i)

            def head(i):
                def fc1(u):
                    t, q = divmod(u, WQ)
                    if q == 0:
                        pe.wait_ge(s["h_ready"], 8 * (LAYERS * nq + i) + t + 1)
                    if u >= 2 or not (isinstance(i, int) and i == 0):
                        pe.wait_ge(s["fc1_act"], 32 * i + u - 1)
                    product(turn_ps[u % 2][:], lambda e: fc1_w[:, (e * WQ + q) * 128:(e * WQ + q + 1) * 128],
                            lambda e: h_next16[:, e * QCOLS + t * CHUNK:e * QCOLS + (t + 1) * CHUNK]
                            ).then_inc(s["fc1_done"], 1)

                def fc2(u):
                    pr = u // 2
                    pe.wait_ge(s["low1"], 32 * i + u + 1)
                    if u % 2 == 0 and (pr >= 2 or not (isinstance(i, int) and i == 0)):
                        pe.wait_ge(s["fc2_act"], 16 * i + pr - 1)
                    half = slice(64 * (u % 2), 64 * (u % 2) + 64)
                    product(inv_ps[pr % 2][half, :], lambda e: fc2_w[:, e * 64:(e + 1) * 64],
                            lambda e: hidden1[u % H1][e]).then_inc(s["fc2_done"], 1)

                def fc3(pr):
                    pe.wait_ge(s["low2"], 16 * i + pr + 1)
                    if pr == 0 and not (isinstance(i, int) and i == 0):
                        pe.wait_ge(s["tok_ready"], i)
                    product(logit_ps[0:32, :], lambda e: fc3_sel[:, (e * 16 + pr) * 32:(e * 16 + pr + 1) * 32],
                            lambda e: hidden2[pr % H2][e], start=(pr == 0), stop=(pr == 15)
                            ).then_inc(s["fc3_done"], 1)

                for u in range(HEAD_STEPS):
                    if u < 32:
                        fc1(u)
                    if 3 <= u < 35:
                        fc2(u - 3)
                    if u >= 8 and u % 2 == 0:
                        fc3((u - 8) // 2)
                pe.wait_ge(s["logit_taken"], i + 1)
                for a in range(2):
                    for j in range(2):
                        c = j * 256 + a * 128
                        o = (a * 2 + j) * 128
                        mm = nc.tensor.transpose(logit_ps[:, o:o + 128], logits[:, c:c + 128], ident[:])
                mm.then_inc(s["tok_turned"], 1)

            pipeline(pe, P, front, forward if P < LAYERS else head)

    def act_program(act):
        act.wait_ge(s["consts_ready"], CONST_STEPS)
        for P in range(LAYERS + 1):
            if P > 0:
                act.wait_ge(s["gelu_done"], 8 * P * nq)
                for ky in range(KY):
                    n = (P - 1) * KY + ky
                    stage = v_stage[ky % 2].rearrange("p (a k n) -> p k a n", a=nq, k=KX)
                    if ky >= 2:
                        act.wait_ge(s[f"spec_stored{ky % 2}"], 64 * (n // 2))
                    for f in (0, 2):
                        act.wait_ge(s["mix_done"], 4 * n + f + 1)
                        ks = MIX_SETS[f]
                        act.activation(stage[:, ks[0]:ks[-1] + 1],
                                       (turn_ps + inv_ps)[f][:, 0:len(ks) * ni].rearrange(
                                           "p (k a n) -> p k a n", k=len(ks), a=nq),
                                       ACT.Copy, scale=MIX_SCALE).then_inc(s["mix_act"], 1)

            def half_high(i, f, P=P):
                if f == 0:
                    act.wait_ge(s["conv_done"], 8 * (P * nq + i))
                act.wait_ge(s["inv_half_ps"], D_FILLS * ((P - 1) * nq + i) + f + 1)
                act.activation(half_view(0, f), inv_ps[f % 2][0:SK * QI, :].rearrange(
                    "p (e o w) -> p e o w", e=2, o=4), ACT.Copy).then_inc(s["inv_half_high"], 1)

            def front(i, last=False, P=P):
                g = P * nq + i
                start = P == 0 and is_first(i)
                if P > 0 and is_first(i):
                    for f in range(D_FILLS):
                        half_high(0, f)
                for t in range(NCH):
                    act.wait_ge(s["dev_ready"], 8 * g + t + 1)
                    if t >= SQ:
                        act.wait_ge(s["var_added"], 8 * g + t + 1 - SQ)
                    elif not start:
                        act.wait_ge(s["var_added"], 8 * g + t + 1 - SQ)
                    act.activation(squares[:, (t % SQ) * CHUNK:(t % SQ + 1) * CHUNK],
                                   dev[:, t * CHUNK:(t + 1) * CHUNK], ACT.Square
                                   ).then_inc(s["square_ready"], 1)
                    if P < LAYERS and not is_first(i):
                        forward_step(i - 1, t)
                if P < LAYERS and not is_first(i):
                    forward_step(i - 1, NCH)
                elif P == LAYERS and not is_first(i):
                    head(i - 1)
                for t in range(NCH):
                    act.wait_ge(s["normed"], 8 * g + t + 1)
                    chunk = dev[:, t * CHUNK:(t + 1) * CHUNK]
                    act.activation(chunk, chunk, ACT.Gelu if 1 <= P < LAYERS else ACT.Identity,
                                   bias=shift[:, P:P + 1], scale=gain[:, P:P + 1]
                                   ).then_inc(s["gelu_done"], 1)
                    if t == 0 and not start:
                        if P < LAYERS or is_first(i):
                            act.wait_ge(s["turned_low"], T_FILLS * g)
                            act.wait_ge(s["h_stored"], 16 * g)
                        else:
                            act.wait_ge(s["fc1_done"], 32 * i)
                        if is_first(i):
                            act.wait_ge(s["mix_done"], 4 * P * KY)
                    act.wait_ge(s["gelu_done"], 8 * g + t + 1)
                    act.activation(h_next16[:, t * CHUNK:(t + 1) * CHUNK], chunk, ACT.Copy
                                   ).then_inc(s["h_high"], 1)
                    if P > 0 and not last and t % 2 == 1:
                        half_high(i + 1, t // 2)

            def forward_step(i, t, P=P):
                g = P * nq + i
                start = P == 0 and is_first(i)
                if 1 <= t <= T_FILLS:
                    f = t - 1
                    if f == 0 and not start:
                        act.wait_ge(s["fy_done"], A_FILLS * g)
                    act.wait_ge(s["turned_high"], T_FILLS * g + f + 1)
                    act.activation(rows_view(0, f), turn_ps[0][:].bitcast(F16).rearrange(
                        "p (w a c) -> p w a c", w=4, a=2), ACT.Copy).then_inc(s["turn_act"], 1)
                if t > T_FILLS:
                    f = t - T_FILLS - 1
                    if f == 0 and not start:
                        act.wait_ge(s["fw_done"], B_FILLS * g)
                    act.wait_ge(s["fy_done"], A_FILLS * g + f + 1)
                    act.activation(spec_y_view(0, f), inv_ps[f % 2][:, 0:8 * 2 * SK].rearrange(
                        "p (c e k) -> p c e k", c=8, k=KX), ACT.Copy).then_inc(s["fy_high"], 1)

            def forward(i):
                for t in range(1, NCH + 1):
                    forward_step(i, t)

            def head(i):
                begin = isinstance(i, int) and i == 0

                def gelu1(u):
                    act.wait_ge(s["fc1_done"], 32 * i + u + 1)
                    if u >= H1 or not begin:
                        act.wait_ge(s["low1"], 32 * i + u + 1 - H1)
                    act.activation(hidden1_full[u % H1], turn_ps[u % 2][:], ACT.Gelu, bias=fc1_b[:],
                                   scale=1 / W_SCALE).then_inc(s["fc1_act"], 1)

                def gelu2(pr):
                    act.wait_ge(s["fc2_done"], 32 * i + 2 * pr + 2)
                    if pr >= H2 or not begin:
                        act.wait_ge(s["low2"], 16 * i + pr + 1 - H2)
                    act.activation(hidden2_full[pr % H2], inv_ps[pr % 2][:], ACT.Gelu, bias=fc2_b[:],
                                   scale=1 / W_SCALE).then_inc(s["fc2_act"], 1)

                for u in range(HEAD_STEPS):
                    if u < 32:
                        gelu1(u)
                    if 5 <= u < 37 and u % 2 == 1:
                        gelu2((u - 5) // 2)

            pipeline(act, P, front, forward if P < LAYERS else head)

    def dve_program(dve):
        dve.wait_ge(s["consts_in"], N_CONST)
        dve.tensor_copy(ident_b[:], ident[:]).then_inc(s["consts_ready"], 1)
        dve.tensor_copy(spread_sel[:], raw["spread_sel"]).then_inc(s["consts_ready"], 1)
        for n, w in enumerate((raw["conv_w"], fc0_w[:])):
            wv = w.rearrange("p (b o) -> p b o", o=CH)
            rows_, blocks = wv.shape[0], wv.shape[1]
            sums = col_sum[0:rows_, 0:blocks]
            if n > 0:
                dve.wait_ge(s["consts_ready"], 3)
            dve.tensor_reduce(sums, wv, AX.X, ALU.add).then_inc(s["fold_step"], 1)
            dve.wait_ge(s["fold_step"], 2 * n + 1)
            dve.tensor_scalar(sums, sums, 1.0 / CH, None, ALU.mult).then_inc(s["fold_step"], 1)
            dve.wait_ge(s["fold_step"], 2 * n + 2)
            dve.tensor_tensor(wv, wv, sums.unsqueeze(2).to_broadcast([rows_, blocks, CH]), ALU.subtract
                              ).then_inc(s["consts_ready"], 1)
        dve.wait_ge(s["consts_ready"], 4)
        for n, (w, name) in enumerate(((conv_w, "conv_w"), (fc1_w, "fc1_w"), (fc2_w, "fc2_w"),
                                       (fc3_sel, "fc3_sel"))):
            half = w.shape[1] // 2
            dve.tensor_scalar(w[:, 0:half], raw[name], W_SCALE, None, ALU.mult
                              ).then_inc(s["consts_ready"], 1)
            dve.wait_ge(s["consts_ready"], 5 + 2 * n)
            dve.scalar_tensor_tensor(out=w[:, half:], in0=raw[name], scalar=W_SCALE, in1=w[:, 0:half],
                                     op0=ALU.mult, op1=ALU.subtract).then_inc(s["consts_ready"], 1)
            dve.wait_ge(s["consts_ready"], 6 + 2 * n)
        dve.wait_ge(s["bias_ps"], 1)
        dve.tensor_copy(bias[:], logit_ps[:, 0:LAYERS + 1]).then_inc(s["consts_ready"], 1)
        dve.wait_ge(s["consts_ready"], CONST_STEPS)
        for P in range(LAYERS + 1):
            if P > 0:
                dve.wait_ge(s["gelu_done"], 8 * P * nq)
                for ky in range(KY):
                    n = (P - 1) * KY + ky
                    stage = v_stage[ky % 2].rearrange("p (a k n) -> p k a n", a=nq, k=KX)
                    if ky >= 2:
                        dve.wait_ge(s[f"spec_stored{ky % 2}"], 64 * (n // 2))
                    for f in (1, 3):
                        dve.wait_ge(s["mix_done"], 4 * n + f + 1)
                        ks = MIX_SETS[f]
                        dve.tensor_scalar(stage[:, ks[0]:ks[-1] + 1],
                                          (turn_ps + inv_ps)[f][:, 0:len(ks) * ni].rearrange(
                                              "p (k a n) -> p k a n", k=len(ks), a=nq),
                                          MIX_SCALE, None, ALU.mult).then_inc(s["mix_dve"], 1)

            def inverse_root(g, start):
                st = s["rstd_step"]
                b = 15 * g

                def step(ins, k):
                    ins.then_inc(st, 1)
                    dve.wait_ge(st, b + k)

                dve.wait_ge(s["var_added"], 8 * (g + 1))
                step(dve.tensor_scalar(var_eps[:], var_ps[:, 0:128], EPS, None, ALU.add), 1)
                step(dve.tensor_scalar(seed[:], var_eps[:].bitcast(mybir.dt.int32), 1, None,
                                       ALU.logical_shift_right), 2)
                step(dve.tensor_scalar(rstd[:].bitcast(mybir.dt.int32), seed[:], -1.0, float(0x5F3759DF),
                                       ALU.mult, ALU.add), 3)
                for n in range(3):
                    step(dve.tensor_tensor(newton[:], rstd[:], rstd[:], ALU.mult), 4 + 3 * n)
                    step(dve.scalar_tensor_tensor(out=newton[:], in0=newton[:], scalar=-0.5,
                                                  in1=var_eps[:], op0=ALU.mult, op1=ALU.mult), 5 + 3 * n)
                    step(dve.scalar_tensor_tensor(out=rstd[:], in0=newton[:], scalar=1.5,
                                                  in1=rstd[:], op0=ALU.add, op1=ALU.mult), 6 + 3 * n)
                sv = split[:].rearrange("p (j a c) -> p a j c", j=4, a=3)
                rv = rstd[:].rearrange("p (j c) -> p j c", j=4)
                ev = rest[:].rearrange("p (j c) -> p j c", j=4)
                if not start:
                    dve.wait_ge(s["parts_turned"], g)
                step(dve.tensor_copy(sv[:, 0], rv), 13)
                step(dve.tensor_tensor(ev, rv, sv[:, 0], ALU.subtract), 14)
                step(dve.tensor_copy(sv[:, 1], ev), 15)
                dve.tensor_tensor(sv[:, 2], ev, sv[:, 1], ALU.subtract).then_inc(s["split_ready"], 1)

            def half_low(i, f, P=P):
                dve.wait_ge(s["inv_half_high"], D_FILLS * ((P - 1) * nq + i) + f + 1)
                dve.tensor_tensor(half_view(1, f), inv_ps[f % 2][0:SK * QI, :].rearrange(
                    "p (e o w) -> p e o w", e=2, o=4), half_view(0, f), ALU.subtract
                                  ).then_inc(s["inv_half"], 1)

            def front(i, last=False, P=P):
                g = P * nq + i
                start = P == 0 and is_first(i)
                if P > 0 and is_first(i):
                    dve.wait_ge(s["spec_stored0"], 32 * KY * P)
                    dve.wait_ge(s["spec_stored1"], 32 * KY * P)
                    for f in range(D_FILLS):
                        half_low(0, f)
                for t in range(NCH):
                    dve.wait_ge(s["conv_done"], 8 * g + t + 1)
                    if not start:
                        dve.wait_ge(s["h_ready"], 8 * g - 7 + t)
                    dve.tensor_scalar(dev[:, t * CHUNK:(t + 1) * CHUNK], conv_ps[t % 2][:],
                                      1 / W_SCALE if P > 0 else 1.0, bias[:, P:P + 1], ALU.mult, ALU.add
                                      ).then_inc(s["dev_ready"], 1)
                    if P < LAYERS and not is_first(i):
                        forward_step(i - 1, t)
                inverse_root(g, start)
                if P < LAYERS and not is_first(i):
                    forward_step(i - 1, NCH)
                elif P == LAYERS and not is_first(i):
                    head(i - 1)
                dve.wait_ge(s["parts_turned"], g + 1)
                if not start:
                    dve.wait_ge(s["spread_done"], 8 * g)
                dve.tensor_copy(parts[:], var_ps[0:96, :]).then_inc(s["parts_ready"], 1)
                for t in range(NCH):
                    dve.wait_ge(s["spread_done"], 8 * g + t + 1)
                    d = dev[:, t * CHUNK:(t + 1) * CHUNK]
                    dve.tensor_tensor(d, d, conv_ps[t % 2][:], ALU.mult).then_inc(s["normed"], 1)
                    if P > 0 and not last and t % 2 == 1:
                        half_low(i + 1, t // 2)
                if P < LAYERS and not is_first(i):
                    take_spectra(i - 1)

            def forward_step(i, t, P=P):
                g = P * nq + i
                if 1 <= t <= T_FILLS:
                    f = t - 1
                    if f == 0 and not (P == 0 and is_first(i)):
                        dve.wait_ge(s["fy_done"], A_FILLS * g)
                    dve.wait_ge(s["turned_low"], T_FILLS * g + f + 1)
                    dve.tensor_copy(rows_view(1, f), turn_ps[1][:].bitcast(F16).rearrange(
                        "p (w a c) -> p w a c", w=4, a=2)).then_inc(s["turn_dve"], 1)
                if t > T_FILLS:
                    f = t - T_FILLS - 1
                    dve.wait_ge(s["fy_high"], A_FILLS * g + f + 1)
                    dve.tensor_tensor(spec_y_view(1, f), inv_ps[f % 2][:, 0:8 * 2 * SK].rearrange(
                        "p (c e k) -> p c e k", c=8, k=KX), spec_y_view(0, f), ALU.subtract
                                      ).then_inc(s["fy_taken"], 1)

            def take_spectra(i, P=P):
                sv = spec[:].rearrange("p (q k a m e) -> p k m q a e", q=KY, k=KX, a=nq, m=2)
                for f, ks in enumerate(B_SETS):
                    dve.wait_ge(s["fw_done"], B_FILLS * (P * nq + i) + f + 1)
                    pv = turn_ps[f][:, 0:len(ks) * 2 * RK].rearrange(
                        "p (k m r q) -> p k m r q", m=2, r=2, q=KY)
                    for e in range(2):
                        for r in range(2):
                            cp = dve.tensor_copy(
                                sv[64 * r:64 * r + 64, ks[0]:ks[-1] + 1, :, :, i, e],
                                pv[64 * e:64 * e + 64, :, :, r, :])
                    cp.then_inc(s["fw_taken"], 1)

            def forward(i):
                for t in range(1, NCH + 1):
                    forward_step(i, t)
                take_spectra(i)

            def head(i):
                begin = isinstance(i, int) and i == 0

                def high1(u):
                    dve.wait_ge(s["fc1_act"], 32 * i + u + 1)
                    if u >= H1 or not begin:
                        dve.wait_ge(s["fc2_done"], 32 * i + u + 1 - H1)
                    dve.tensor_copy(hidden1[u % H1][0], hidden1_full[u % H1]).then_inc(s["high1"], 1)

                def high2(pr):
                    dve.wait_ge(s["fc2_act"], 16 * i + pr + 1)
                    if pr >= H2 or not begin:
                        dve.wait_ge(s["fc3_done"], 16 * i + pr + 1 - H2)
                    dve.tensor_copy(hidden2[pr % H2][0], hidden2_full[pr % H2]).then_inc(s["high2"], 1)

                for u in range(HEAD_STEPS):
                    if u < 32:
                        high1(u)
                    if 6 <= u < 38 and u % 2 == 0:
                        high2((u - 6) // 2)
                dve.wait_ge(s["fc3_done"], 16 * (i + 1))
                if not (isinstance(i, int) and i == 0):
                    dve.wait_ge(s["tok_turned"], i)
                dve.tensor_scalar(logits[0:32, :], logit_ps[0:32, :], 1 / W_SCALE, fc3_b[:], ALU.mult, ALU.add
                                  ).then_inc(s["logit_taken"], 1)
                dve.wait_ge(s["tok_turned"], i + 1)
                if not (isinstance(i, int) and i == 0):
                    dve.wait_ge(s["tok_stored"], 32 * i)
                dve.tensor_copy(tok_rows.rearrange("p (a t j q) -> p a j t q", a=2, t=NCH, j=2),
                                logit_ps[:].rearrange("p (a j u) -> p a j u", a=2, j=2)[:, :, :, 0:32].rearrange(
                                    "p a j (t q) -> p a j t q", q=WQ)
                                ).then_inc(s["tok_ready"], 1)

            if P == LAYERS:
                dve.wait_ge(s["mix_done"], 4 * P * KY)
                dve.memset(logits, 0.0).then_inc(s["logits_zero"], 1)
                dve.wait_ge(s["logits_zero"], 1)
            pipeline(dve, P, front, forward if P < LAYERS else head)

    def pool_program(pool):
        def step(ins, value):
            ins.then_inc(s["prep_step"], 1)
            pool.wait_ge(s["prep_step"], value)

        pool.wait_ge(s["consts_ready"], CONST_STEPS)
        pv = prep_in[:].rearrange("p (t e m) -> p t e m", t=2, e=2)
        col_type = (0, 1, 1, 0)

        def prep_chunk(n):
            first = isinstance(n, int) and n == 0
            pool.wait_ge(s["prep_loaded"], 128 * (n + 1))
            b = PREP_STEPS * n
            v3 = prep_in[:].rearrange("p (m o) -> p m o", o=CH)
            fold = prep_fold[:].rearrange("p (m o) -> p m o", o=CH // 2)
            step(pool.tensor_tensor(fold, v3[:, :, 0:16], v3[:, :, 16:32], ALU.add), b + 1)
            for n_, w in enumerate((8, 4, 2, 1)):
                step(pool.tensor_tensor(fold[:, :, 0:w], fold[:, :, 0:w], fold[:, :, w:2 * w], ALU.add),
                     b + 2 + n_)
            step(pool.tensor_tensor(fold[:, :, 0:1], fold[:, :, 0:1],
                                    sign[:, 8:9].unsqueeze(2).to_broadcast([128, 4 * KX, 1]), ALU.mult), b + 6)
            step(pool.tensor_tensor(v3, v3, fold[:, :, 0:1].to_broadcast([128, 4 * KX, CH]),
                                    ALU.subtract), b + 7)
            if not first:
                pool.wait_ge(s["prep_stored"], 16 * n)
            ov = prep_out[:].rearrange("p (k v o) -> p k v o", k=KX, v=4)
            tv = prep_tmp[:].rearrange("p (k o) -> p k o", k=KX)
            for v in range(4):
                src = [pv[:, col_type[v], e, :].rearrange("p (k o) -> p k o", k=KX) for e in range(2)]
                sg = [sign[:, 2 * v + e:2 * v + e + 1].unsqueeze(2).to_broadcast([128, KX, CH])
                      for e in range(2)]
                step(pool.tensor_tensor(tv, src[1], sg[1], ALU.mult), b + 8 + 3 * v)
                step(pool.tensor_tensor(ov[:, :, v, :], src[0], sg[0], ALU.mult), b + 9 + 3 * v)
                step(pool.tensor_tensor(ov[:, :, v, :], ov[:, :, v, :], tv, ALU.add), b + 10 + 3 * v)

        for P in range(LAYERS + 1):
            def split_mixed(i, P=P):
                gd = (P - 1) * nq + i
                pool.wait_ge(s["mixed_loaded"], 16 * (gd + 1))
                if P > 1 or not isinstance(i, int) or i > 0:
                    pool.wait_ge(s["inv_half_ps"], D_FILLS * gd)
                pool.tensor_tensor(mixed[:, 0:VCOLS], mixed_in[:], sign[0:96, 9:10].to_broadcast([96, VCOLS]),
                                   ALU.mult).then_inc(s["mixed_high"], 1)
                pool.wait_ge(s["mixed_high"], gd + 1)
                pool.tensor_tensor(mixed[:, VCOLS:], mixed_in[:], mixed[:, 0:VCOLS], ALU.subtract
                                   ).then_inc(s["mixed_split"], 1)

            def low_h(i, P=P):
                g = P * nq + i
                for t in range(NCH):
                    pool.wait_ge(s["h_high"], 8 * g + t + 1)
                    pool.tensor_tensor(h_next16[:, QCOLS + t * CHUNK:QCOLS + (t + 1) * CHUNK],
                                       dev[:, t * CHUNK:(t + 1) * CHUNK],
                                       h_next16[:, t * CHUNK:(t + 1) * CHUNK], ALU.subtract
                                       ).then_inc(s["h_ready"], 1)

            def head(i):
                for u in range(HEAD_STEPS):
                    if u < 32:
                        pool.wait_ge(s["high1"], 32 * i + u + 1)
                        pool.tensor_tensor(hidden1[u % H1][1], hidden1_full[u % H1], hidden1[u % H1][0],
                                           ALU.subtract).then_inc(s["low1"], 1)
                    if 6 <= u < 38 and u % 2 == 0:
                        pr = (u - 6) // 2
                        pool.wait_ge(s["high2"], 16 * i + pr + 1)
                        pool.tensor_tensor(hidden2[pr % H2][1], hidden2_full[pr % H2], hidden2[pr % H2][0],
                                           ALU.subtract).then_inc(s["low2"], 1)

            def store_tokens(i):
                pool.wait_ge(s["tok_ready"], i + 1)
                for e in range(2):
                    pool.dma_start(tok[i, e], tok_rows[64 * e:64 * e + 64, :].rearrange(
                        "p (a w) -> p a w", a=2)).then_inc(s["tok_stored"], 16)

            def one(i, prep=False, last=False, P=P):
                first = isinstance(i, int) and i == 0
                if P > 0 and not last:
                    split_mixed(i + 1)
                if P == LAYERS and not first:
                    head(i - 1)
                low_h(i)
                if P == LAYERS and not first:
                    store_tokens(i - 1)
                if prep:
                    prep_chunk(P * KY + i)

            if P > 0:
                split_mixed(0)
            preps = min(KY, nq - 1) if P < LAYERS else 1
            one(0, prep=P < LAYERS)
            quads(pool, 1, preps, lambda i: one(i, prep=True))
            quads(pool, preps, nq - 1, one)
            one(nq - 1, last=True)
            if P < LAYERS:
                for ky in range(preps, KY):
                    prep_chunk(P * KY + ky)
            else:
                head(nq - 1)
                store_tokens(nq - 1)

    return s, sp_program, pe_program, act_program, dve_program, pool_program



D = 64
SEQ = SIDE + 1
HEADS, HD = 8, 8
WIN = 64
EXPERTS = 8
HID = 128
LHEADS, LHD, MEM = 4, 32, 4
KEYS = SEQ + MEM


def tail_constants():
    c = {}
    c["head_rows"] = np.kron(np.eye(HEADS), np.ones((HD, 1)))
    c["pair_mask"] = np.kron(np.eye(2), np.ones((WIN, HD))).reshape(2 * WIN, 1, 2 * HD) * np.ones((1, 4, 1))
    c["context_mask"] = np.kron(np.eye(LHEADS), np.ones((LHD, LHD))) * LHD ** -0.5
    c["mem_ident"] = np.broadcast_to(np.eye(MEM)[:, None, :], (MEM, 128, MEM))
    c["expert_no"] = np.broadcast_to(np.arange(EXPERTS), (128, EXPERTS))
    return {k: np.ascontiguousarray(np.asarray(v, np.float32).reshape(v.shape[0], -1)) for k, v in c.items()}


def token_transformer(nc, io, bank, sem, sb, tower_done, tokens, out):
    NIMG = tokens.shape[0] // SEQ
    NTOK = NIMG * SEQ
    NT = NTOK // 128
    XC = NT * D
    assert NT * 128 == NTOK and NIMG == 128

    h = sb("tok_h", [128, XC], F32)
    x = sb("tok_x", [128, XC], F32)
    area = [sb(f"area{n}", [128, NTOK + (NIMG * MEM if n == 0 else 0)], F32) for n in range(4)]
    y, y_last = area[3][:, 0:XC], area[0][:, 0:XC]
    stat = sb("stat", [128, 6 * NT], F32)
    seed = sb("tok_seed", [128, NT], mybir.dt.int32)
    small = sb("small", [128, 6 * NT * EXPERTS], F32)
    keys_ex = sb("keys_ex", [128, 2 * 512], F32)
    work = sb("work", [128, 2 * 512], F32)
    wide = sb("wide", [128, 2 * 512], F32)
    narrow = sb("narrow", [128, 4 * 128], F32)
    sums = sb("sums", [128, 2 * 32], F32)

    shapes = {k: io[k].shape for k in (
        "head_rows pair_mask context_mask mem_ident expert_no ident a_wq a_wk a_wv a_wproj a_bproj a_rel "
        "a_rel1 b_gamma b_beta b_wr b_br b_w1 b_b1 b_w2 b_b2 c_wq c_wk c_wv c_wout c_bout c_gout c_gpre "
        "d_w1 d_b1 d_wg d_bg d_wd d_bd").split()}
    groups = {"all": "ident expert_no", "a": "head_rows pair_mask a_wq a_wk a_wv a_wproj a_bproj a_rel a_rel1",
              "b": "b_gamma b_beta b_wr b_br b_w1 b_b1 b_w2 b_b2",
              "c": "context_mask c_wq c_wk c_wv c_wout c_bout c_gout c_gpre",
              "d": "d_w1 d_b1 d_wg d_bg d_wd d_bd"}
    groups = {g: v.split() for g, v in groups.items()}
    W = {}
    size = {g: sum(int(np.prod(shapes[k][1:])) for k in v) for g, v in groups.items()}
    w_all = sb("w_all", [128, size["all"]], F32)
    w_stage = sb("w_stage", [128, max(size[g] for g in "abcd")], F32)
    for g, v in groups.items():
        at = 0
        for k in v:
            n = int(np.prod(shapes[k][1:]))
            W[k] = (w_all if g == "all" else w_stage)[0:shapes[k][0], at:at + n]
            at += n
    ones_row = sb("ones_row", [1, 128], F32)
    ident = W["ident"]

    s = {n: sem("t_" + n) for n in (
        "in weights step x_ready ones turned turn_dve turn_act "
        "qk_ps qk_dve qk_act keys_ready scores_ps logits_ready probs_ready probs_turned probs_back v_ps v_ready "
        "mixed_ps mixed_norm mixed_turned mixed_back proj_ps proj_taken one_ps one_step one_prod one_p one_exp "
        "route_ps route_done hid_ps hid_act y_ps y_taken "
        "aug_ready kk_ps kk_max kk_exp kk_norm kk_turned kk_back vv_ps vv_back ctx_ps ctx_ready "
        "q_ps q_max q_exp q_ready q_turned q_back lin_ps lin_back w_ps w_taken "
        "stage_done out_done").split()}
    n_in = [0]

    def t3(ap, n=D):
        return ap.rearrange("p (t d) -> p t d", d=n)

    hv, xv, yv = t3(h[:]), t3(x[:]), t3(y)
    wide_row = lambda ap, n: ap.unsqueeze(1).to_broadcast([128, n, ap.shape[1]])
    N_STAGE = {g: len(v) for g, v in groups.items()}
    w_count, at = {}, 0
    for g in ("all", "a", "b", "c", "d"):
        at += N_STAGE[g] + (1 if g == "c" else 0)
        w_count[g] = 16 * at
    TURNS = [("dve", "act")[f % 2] for f in range(-(-NT // 4))]

    def sp_program(sp):
        tower_done(sp)
        sp.dma_start(hv, tokens.rearrange("(t p) d -> p t d", p=128)).then_inc(s["in"], 16)
        for n, g in enumerate(("all", "a", "b", "c", "d")):
            if n >= 2:
                sp.wait_ge(s["stage_done"], n - 1)
            for k in groups[g]:
                sp.dma_start(W[k], io[k]).then_inc(s["weights"], 16)
            if g == "c":
                sp.wait_ge(s["aug_ready"], 1)
                sp.dma_start(area[0][64:64 + MEM, :].rearrange("p (b n) -> p b n", n=KEYS)[:, :, SEQ:],
                             io["mem_ident"].rearrange("p (b n) -> p b n", n=MEM)).then_inc(s["weights"], 16)
        sp.wait_ge(s["stage_done"], 4)
        sp.dma_start(out, hv).then_inc(s["out_done"], 16)
        sp.wait_ge(s["out_done"], 16)

    turns = [0]

    def turn_pe(pe, stage):
        pe.wait_ge(s["x_ready"], stage + 1)
        for f in range(len(TURNS)):
            n = stage * len(TURNS) + f
            if n >= 2:
                pe.wait_ge(s["turn_" + ("dve", "act")[f % 2]], prior(stage, f))
            for t in range(4 * f, min(4 * f + 4, NT)):
                mm = nc.tensor.transpose(bank[f % 2][0:D, (t % 4) * 128:(t % 4 + 1) * 128], xv[:, t, :], ident)
            mm.then_inc(s["turned"], 1)

    nd, na = TURNS.count("dve"), TURNS.count("act")

    def prior(stage, f):
        return stage * (nd if f % 2 == 0 else na) + f // 2

    def turn_back(eng, copy, stage, parity):
        for f in range(parity, len(TURNS), 2):
            eng.wait_ge(s["turned"], stage * len(TURNS) + f + 1)
            n = min(4, NT - 4 * f) * 128
            copy(area[1][0:D, f * 512:f * 512 + n], bank[f % 2][0:D, 0:n]).then_inc(
                s["turn_" + ("dve", "act")[parity]], 1)

    def turned(eng, stage):
        eng.wait_ge(s["turn_dve"], nd * (stage + 1))
        eng.wait_ge(s["turn_act"], na * (stage + 1))

    a_copy = lambda o, i: nc.scalar.activation(o, i, ACT.Copy)
    v_copy = lambda o, i: nc.vector.tensor_copy(o, i)

    NP = NIMG // 2
    xT = area[1]
    qT, kT, oT = area[2], area[3], area[0]
    xw = xT[0:D, :].rearrange("p (b n) -> p b n", n=SEQ)
    ow = oT[0:D, 0:NTOK].rearrange("p (b n) -> p b n", n=SEQ)
    CHUNKS = [(f * 4, min(4, NT - f * 4)) for f in range(len(TURNS))]
    NG = -(-NT // 8)
    KI = 4
    NK = NIMG // KI

    def pe_program(pe):
        pe.wait_ge(s["weights"], w_count["a"])
        turn_pe(pe, 0)
        turned(pe, 0)
        for n in range(2 * NIMG // 8):
            c, which = divmod(n, 2)
            if n >= 2:
                pe.wait_ge(s["qk_dve" if which == 0 else "qk_act"], c)
            nc.tensor.matmul(bank[2 + which][0:D, :], W["a_wq" if which == 0 else "a_wk"],
                             xw[:, 8 * c:8 * c + 8, 0:WIN], start=True, stop=True).then_inc(s["qk_ps"], 1)
        pe.wait_ge(s["qk_dve"], NIMG // 8)
        pe.wait_ge(s["qk_act"], NIMG // 8)

        def scores(n):
            pe.wait_ge(s["keys_ready"], 2 * n + 2)
            if n >= 2:
                pe.wait_ge(s["logits_ready"], 1 * (n - 1))
            for e in range(2):
                b = 2 * n + e
                mm = nc.tensor.matmul(bank[n % 2][64 * e:64 * e + 64, :], qT[0:D, b * WIN:(b + 1) * WIN],
                                      keys_ex[0:D, e * 512:(e + 1) * 512], start=True, stop=True)
            mm.then_inc(s["scores_ps"], 1)

        def values(n):
            if n >= 1:
                pe.wait_ge(s["v_ready"], n)
            for e in range(2):
                for half in range(2):
                    mm = nc.tensor.matmul(bank[4][64 * half:64 * half + 64, e * D:(e + 1) * D],
                                          xw[:, 2 * n + e, 0:WIN], W["a_wv"], start=True, stop=True)
            mm.then_inc(s["v_ps"], 1)

        def mix(n):
            pe.wait_ge(s["probs_ready"], n + 1)
            if n >= 1:
                pe.wait_ge(s["probs_back"], n)
            for hp in range(4):
                mm = nc.tensor.transpose(bank[5][:, hp * 128:(hp + 1) * 128],
                                         wide[:, (n % 2) * 512 + hp * 128:(n % 2) * 512 + (hp + 1) * 128], ident)
            mm.then_inc(s["probs_turned"], 1)

        def apply(n):
            pe.wait_ge(s["probs_back"], n + 1)
            pe.wait_ge(s["v_ready"], n + 1)
            if n >= 1:
                pe.wait_ge(s["mixed_norm"], n)
            for e in range(2):
                for hp in range(4):
                    mm = nc.tensor.matmul(bank[6][64 * e:64 * e + 64, hp * 16:(hp + 1) * 16],
                                          work[:, hp * 128 + 64 * e:hp * 128 + 64 * e + 64],
                                          narrow[:, e * D + hp * 16:e * D + (hp + 1) * 16],
                                          start=True, stop=True)
            mm.then_inc(s["mixed_ps"], 1)

        def turn_mixed(n):
            pe.wait_ge(s["mixed_norm"], n + 1)
            if n >= 1:
                pe.wait_ge(s["mixed_back"], n)
            nc.tensor.transpose(bank[7][0:D, 0:128], narrow[:, 2 * D + (n % 2) * D:2 * D + (n % 2 + 1) * D],
                                ident).then_inc(s["mixed_turned"], 1)

        for n in range(NP + 2):
            if n < NP:
                scores(n)
                values(n)
            if 1 <= n <= NP:
                mix(n - 1)
                apply(n - 1)
            if n >= 2:
                turn_mixed(n - 2)
        last = xw[:, :, WIN]
        nc.tensor.matmul(bank[2][0:D, 0:128], W["a_wq"], last, start=True, stop=True)
        nc.tensor.matmul(bank[2][0:D, 128:256], W["a_wk"], last, start=True, stop=True)
        nc.tensor.matmul(bank[2][:, 256:256 + D], last, W["a_wv"], start=True, stop=True).then_inc(s["one_ps"], 1)
        pe.wait_ge(s["one_prod"], 1)
        nc.tensor.matmul(bank[3][:, 0:HEADS], work[0:D, 256:384], W["head_rows"], start=True, stop=True
                         ).then_inc(s["one_ps"], 1)
        pe.wait_ge(s["one_p"], 1)
        nc.tensor.transpose(bank[3][0:D, 128:256], work[:, 384:384 + D], ident).then_inc(s["one_ps"], 1)
        pe.wait_ge(s["one_p"], 2)
        pe.wait_ge(s["mixed_back"], NP)
        for g in range(NG):
            if g >= 2:
                pe.wait_ge(s["proj_taken"], g - 1)
            for t in range(8 * g, min(8 * g + 8, NT)):
                mm = nc.tensor.matmul(bank[g % 2][:, (t % 8) * D:(t % 8 + 1) * D],
                                      oT[0:D, t * 128:(t + 1) * 128], W["a_wproj"], start=True, stop=True)
            mm.then_inc(s["proj_ps"], 1)
        pe.wait_ge(s["proj_taken"], NG)

        pe.wait_ge(s["weights"], w_count["b"])
        turn_pe(pe, 1)
        turned(pe, 1)
        for t in range(NT):
            mm = nc.tensor.matmul(bank[2 + t // 64][:, (t % 64) * 8:(t % 64 + 1) * 8],
                                  xT[0:D, t * 128:(t + 1) * 128], W["b_wr"], start=True, stop=True)
        mm.then_inc(s["route_ps"], 1)
        pe.wait_ge(s["route_done"], 1)
        hidden_b = [wide[:, 0:512], wide[:, 512:1024]]
        units = [(c, e) for c in range(len(CHUNKS)) for e in range(EXPERTS)]

        def hid_b(u):
            c, e = units[u]
            if u >= 2:
                pe.wait_ge(s["hid_act"], u - 1)
            n = CHUNKS[c][1] * 128
            nc.tensor.matmul(bank[u % 2][:, 0:n], W["b_w1"][:, e * HID:(e + 1) * HID],
                             xT[0:D, c * 512:c * 512 + n], start=True, stop=True).then_inc(s["hid_ps"], 1)

        def out_b(u):
            c, e = units[u]
            pe.wait_ge(s["hid_act"], u + 1)
            if e == 0:
                if c >= 1:
                    pe.wait_ge(s["y_taken"], sum(k for _, k in CHUNKS[:c]))
                for j in range(CHUNKS[c][1]):
                    nc.tensor.matmul(bank[2 + j][:], ones_row[:], W["b_b2"], start=True, stop=False)
            for j in range(CHUNKS[c][1]):
                mm = nc.tensor.matmul(bank[2 + j][:, e * D:(e + 1) * D], hidden_b[u % 2][:, j * 128:(j + 1) * 128],
                                      W["b_w2"][:, e * D:(e + 1) * D], start=False, stop=(e == EXPERTS - 1))
            mm.then_inc(s["y_ps"], 1)

        for u in range(len(units) + 1):
            if u < len(units):
                hid_b(u)
            if u >= 1:
                out_b(u - 1)
        pe.wait_ge(s["y_taken"], NT)

        pe.wait_ge(s["weights"], w_count["c"])
        turn_pe(pe, 2)
        turned(pe, 2)
        q_rows(pe)
        pe.wait_ge(s["q_back"], len(CHUNKS))
        pe.wait_ge(s["aug_ready"], 2)
        aug = area[0][0:D + MEM, :]

        def keys(n):
            if n >= 1:
                pe.wait_ge(s["kk_norm"], n)
            nc.tensor.matmul(bank[0][:, 0:KI * KEYS], W["c_wk"], aug[:, n * KI * KEYS:(n + 1) * KI * KEYS],
                             start=True, stop=True).then_inc(s["kk_ps"], 1)
            if n >= 1:
                pe.wait_ge(s["vv_back"], n)
            for i in range(KI):
                b = n * KI + i
                mm = nc.tensor.matmul(bank[1][0:KEYS, i * 128:(i + 1) * 128], aug[:, b * KEYS:(b + 1) * KEYS],
                                      W["c_wv"], start=True, stop=True)
            mm.then_inc(s["vv_ps"], 1)

        def turn_keys(n):
            pe.wait_ge(s["kk_exp"], n + 1)
            if n >= 1:
                pe.wait_ge(s["kk_back"], n)
            for i in range(KI):
                mm = nc.tensor.transpose(bank[2][0:KEYS, i * 128:(i + 1) * 128],
                                         keys_ex[:, (n % 2) * 512 + i * KEYS:(n % 2) * 512 + (i + 1) * KEYS],
                                         ident)
            mm.then_inc(s["kk_turned"], 1)

        def context(n):
            pe.wait_ge(s["kk_back"], n + 1)
            if n >= 1:
                pe.wait_ge(s["ctx_ready"], n)
            for i in range(KI):
                c = (n % 2) * 512 + i * 128
                mm = nc.tensor.matmul(bank[3][:, i * 128:(i + 1) * 128], wide[0:KEYS, c:c + 128],
                                      work[0:KEYS, c:c + 128], start=True, stop=True)
            mm.then_inc(s["ctx_ps"], 1)

        def linear(n):
            pe.wait_ge(s["ctx_ready"], n + 1)
            if n >= 1:
                pe.wait_ge(s["lin_back"], n)
            for i in range(KI):
                b = n * KI + i
                mm = nc.tensor.matmul(bank[4][:, i * SEQ:(i + 1) * SEQ], narrow[:, i * 128:(i + 1) * 128],
                                      area[2][:, b * SEQ:(b + 1) * SEQ], start=True, stop=True)
            mm.then_inc(s["lin_ps"], 1)

        for n in range(NK + 2):
            if n < NK:
                keys(n)
            if 1 <= n <= NK:
                turn_keys(n - 1)
                context(n - 1)
            if n >= 2:
                linear(n - 2)
        pe.wait_ge(s["lin_back"], NK)
        for g in range(NG):
            if g >= 2:
                pe.wait_ge(s["w_taken"], g - 1)
            for t in range(8 * g, min(8 * g + 8, NT)):
                mm = nc.tensor.matmul(bank[g % 2][:, (t % 8) * D:(t % 8 + 1) * D],
                                      area[1][:, t * 128:(t + 1) * 128], W["c_wout"], start=True, stop=True)
            mm.then_inc(s["w_ps"], 1)
        pe.wait_ge(s["w_taken"], NG)

        pe.wait_ge(s["weights"], w_count["d"])
        turn_pe(pe, 3)
        turned(pe, 3)
        base = len(units)
        for u in range(2 * len(CHUNKS)):
            c, half = divmod(u, 2)
            pe.wait_ge(s["hid_act"], base + u - 1)
            n = CHUNKS[c][1] * 128
            nc.tensor.matmul(bank[u % 2][:, 0:n], W["d_w1"][:, half * HID:(half + 1) * HID],
                             xT[0:D, c * 512:c * 512 + n], start=True, stop=True).then_inc(s["hid_ps"], 1)
        pe.wait_ge(s["hid_act"], base + 2 * len(CHUNKS))
        for t in range(NT):
            for half in range(2):
                mm = nc.tensor.matmul(bank[2 + t // 64][:, (t % 64) * 8:(t % 64 + 1) * 8],
                                      area[2 + half][:, t * 128:(t + 1) * 128],
                                      W["d_wg"][:, half * 8:(half + 1) * 8],
                                      start=(half == 0), stop=(half == 1))
        mm.then_inc(s["route_ps"], 1)
        pe.wait_ge(s["route_done"], 2)
        for t in range(NT):
            if t >= 4:
                pe.wait_ge(s["y_taken"], NT + t - 3)
            nc.tensor.matmul(bank[4 + t % 4][:], ones_row[:], W["d_bd"], start=True, stop=False)
            for half in range(2):
                mm = nc.tensor.matmul(bank[4 + t % 4][:], area[2 + half][:, t * 128:(t + 1) * 128],
                                      W["d_wd"][:, half * 512:(half + 1) * 512],
                                      start=False, stop=(half == 1))
            mm.then_inc(s["y_ps"], 1)

    def q_rows(pe):
        def q_ps(f):
            if f >= 1:
                pe.wait_ge(s["q_ready"], f)
            for t in range(CHUNKS[f][0], CHUNKS[f][0] + CHUNKS[f][1]):
                mm = nc.tensor.matmul(bank[2][:, (t % 4) * 128:(t % 4 + 1) * 128],
                                      xT[0:D, t * 128:(t + 1) * 128], W["c_wq"], start=True, stop=True)
            mm.then_inc(s["q_ps"], 1)

        def q_turn(f):
            pe.wait_ge(s["q_ready"], f + 1)
            if f >= 1:
                pe.wait_ge(s["q_back"], f)
            for j in range(CHUNKS[f][1]):
                c = (f % 2) * 512 + j * 128
                mm = nc.tensor.transpose(bank[3][:, j * 128:(j + 1) * 128], wide[:, c:c + 128], ident)
            mm.then_inc(s["q_turned"], 1)

        for f in range(len(CHUNKS) + 1):
            if f < len(CHUNKS):
                q_ps(f)
            if f >= 1:
                q_turn(f - 1)

    def act_program(act):
        turn_back(act, a_copy, 0, 1)
        for c in range(NIMG // 8):
            act.wait_ge(s["qk_ps"], 2 * c + 2)
            a_copy(kT[0:D, c * 512:(c + 1) * 512], bank[3][0:D, :]).then_inc(s["qk_act"], 1)
        for n in range(NP + 2):
            if n < NP:
                act.wait_ge(s["logits_ready"], n + 1)
                if n >= 2:
                    act.wait_ge(s["probs_turned"], n - 1)
                c = slice((n % 2) * 512, (n % 2 + 1) * 512)
                nc.scalar.activation(wide[:, c], wide[:, c], ACT.Exp).then_inc(s["probs_ready"], 1)
            if 1 <= n <= NP:
                act.wait_ge(s["probs_turned"], n)
                if n >= 2:
                    act.wait_ge(s["mixed_ps"], n - 1)
                a_copy(work[:, 0:512], bank[5][:]).then_inc(s["probs_back"], 1)
            if n >= 2:
                m = n - 2
                act.wait_ge(s["mixed_turned"], m + 1)
                a_copy(ow[:, 2 * m:2 * m + 2, 0:WIN], bank[7][0:D, 0:128].rearrange("p (e n) -> p e n", e=2)
                       ).then_inc(s["mixed_back"], 1)
        act.wait_ge(s["one_step"], 1)
        nc.scalar.activation(small[:, 128:208], small[:, 0:80], ACT.Exp).then_inc(s["one_exp"], 1)
        turn_back(act, a_copy, 1, 1)
        act.wait_ge(s["step"], STEP["route_exp0"])
        nc.scalar.activation(small[:, 0:NT], small[:, 0:NT], ACT.Exp).then_inc(s["route_exp"], 1)
        hidden_b = [wide[:, 0:512], wide[:, 512:1024]]
        nu = len(CHUNKS) * EXPERTS
        for u in range(nu):
            c, e = divmod(u, EXPERTS)
            act.wait_ge(s["hid_ps"], u + 1)
            if u >= 2:
                act.wait_ge(s["y_ps"], u - 1)
            n = CHUNKS[c][1] * 128
            nc.scalar.activation(hidden_b[u % 2][:, 0:n], bank[u % 2][:, 0:n], ACT.Gelu,
                                 bias=W["b_b1"][:, e:e + 1]).then_inc(s["hid_act"], 1)
        turn_back(act, a_copy, 2, 1)
        for f in range(len(CHUNKS) + 1):
            if f < len(CHUNKS):
                n = CHUNKS[f][1] * 128
                c = (f % 2) * 512
                act.wait_ge(s["q_max"], f + 1)
                nc.scalar.activation(wide[:, c:c + n], wide[:, c:c + n], ACT.Exp).then_inc(s["q_exp"], 1)
            if f >= 1:
                n = CHUNKS[f - 1][1] * 128
                act.wait_ge(s["q_turned"], f)
                a_copy(area[2][:, (f - 1) * 512:(f - 1) * 512 + n], bank[3][:, 0:n]).then_inc(s["q_back"], 1)
        for n in range(NK + 2):
            if n < NK:
                act.wait_ge(s["vv_ps"], n + 1)
                if n >= 2:
                    act.wait_ge(s["ctx_ps"], n - 1)
                a_copy(work[0:KEYS, (n % 2) * 512:(n % 2 + 1) * 512], bank[1][0:KEYS, :]
                       ).then_inc(s["vv_back"], 1)
                act.wait_ge(s["kk_norm"], n + 1)
                c = (n % 2) * 512
                nc.scalar.activation(keys_ex[:, c:c + KI * KEYS], keys_ex[:, c:c + KI * KEYS], ACT.Exp
                                     ).then_inc(s["kk_exp"], 1)
            if 1 <= n <= NK:
                act.wait_ge(s["kk_turned"], n)
                if n >= 3:
                    act.wait_ge(s["ctx_ps"], n - 2)
                c = ((n - 1) % 2) * 512
                a_copy(wide[0:KEYS, c:c + 512], bank[2][0:KEYS, :]).then_inc(s["kk_back"], 1)
            if n >= 2:
                m = n - 2
                act.wait_ge(s["lin_ps"], m + 1)
                a_copy(area[1][:, m * KI * SEQ:(m + 1) * KI * SEQ], bank[4][:, 0:KI * SEQ]
                       ).then_inc(s["lin_back"], 1)
        turn_back(act, a_copy, 3, 1)
        for u in range(2 * len(CHUNKS)):
            c, half = divmod(u, 2)
            act.wait_ge(s["hid_ps"], nu + u + 1)
            n = CHUNKS[c][1] * 128
            nc.scalar.activation(area[2 + half][:, c * 512:c * 512 + n], bank[u % 2][:, 0:n], ACT.Gelu,
                                 bias=W["d_b1"][:, half:half + 1]).then_inc(s["hid_act"], 1)
        act.wait_ge(s["step"], STEP["gate_exp"])
        nc.scalar.activation(small[:, 0:NT * 8], small[:, 0:NT * 8], ACT.Exp).then_inc(s["route_exp"], 1)

    STEP = {}
    s["route_exp"] = sem("t_route_exp")

    V = nc.vector
    st = [stat[:, n * NT:(n + 1) * NT] for n in range(6)]

    def dve_program(dve, dry=False):
        count = [0]

        def link(f):
            count[0] += 1
            if not dry:
                f().then_inc(s["step"], 1)
                dve.wait_ge(s["step"], count[0])

        def wait(name, value):
            if not dry:
                dve.wait_ge(s[name], value)

        def do(f, name=None):
            if not dry:
                ins = f()
                if name:
                    ins.then_inc(s[name], 1)

        def bc(ap, n=D):
            return ap.unsqueeze(2).to_broadcast([128, ap.shape[1], n])

        def inverse_root(v, r):
            link(lambda: V.tensor_scalar(seed[:], v.bitcast(mybir.dt.int32), 1, None, ALU.logical_shift_right))
            link(lambda: V.tensor_scalar(r.bitcast(mybir.dt.int32), seed[:], -1.0, float(0x5F3759DF),
                                         ALU.mult, ALU.add))
            for _ in range(3):
                link(lambda: V.tensor_tensor(st[4], r, r, ALU.mult))
                link(lambda: V.scalar_tensor_tensor(out=st[4], in0=st[4], scalar=-0.5, in1=v,
                                                    op0=ALU.mult, op1=ALU.mult))
                link(lambda: V.scalar_tensor_tensor(out=r, in0=st[4], scalar=1.5, in1=r,
                                                    op0=ALU.add, op1=ALU.mult))

        def layer_norm(dst, src, spare):
            link(lambda: V.tensor_reduce(st[0], src, AX.X, ALU.add))
            link(lambda: V.tensor_scalar(st[0], st[0], 1.0 / D, None, ALU.mult))
            link(lambda: V.tensor_tensor(dst, src, bc(st[0]), ALU.subtract))
            link(lambda: V.tensor_tensor(spare, dst, dst, ALU.mult))
            link(lambda: V.tensor_reduce(st[1], spare, AX.X, ALU.add))
            link(lambda: V.tensor_scalar(st[1], st[1], 1.0 / D, EPS, ALU.mult, ALU.add))
            inverse_root(st[1], st[2])
            link(lambda: V.tensor_tensor(dst, dst, bc(st[2]), ALU.mult))

        def rms_norm(dst, src, spare, gain):
            link(lambda: V.tensor_tensor(spare, src, src, ALU.mult))
            link(lambda: V.tensor_reduce(st[1], spare, AX.X, ALU.add))
            link(lambda: V.tensor_scalar(st[1], st[1], 1e-24, None, ALU.max))
            inverse_root(st[1], st[2])
            link(lambda: V.tensor_scalar(st[2], st[2], float(D) ** 0.5, None, ALU.mult))
            link(lambda: V.tensor_tensor(dst, src, bc(st[2]), ALU.mult))
            link(lambda: V.tensor_tensor(dst, dst, wide_row(gain, NT), ALU.mult))

        wait("in", 16)
        do(lambda: V.memset(ones_row[:], 1.0), "ones")
        layer_norm(xv, hv, yv)
        do(lambda: V.engine_nop(), "x_ready")
        if not dry:
            turn_back(dve, v_copy, 0, 0)
        for c in range(NIMG // 8):
            wait("qk_ps", 2 * c + 1)
            do(lambda: v_copy(qT[0:D, c * 512:(c + 1) * 512], bank[2][0:D, :]), "qk_dve")
        wait("qk_act", NIMG // 8)
        wait("weights", w_count["a"])
        rel = W["a_rel"].unsqueeze(1).to_broadcast([128, HEADS, WIN])
        hr = W["head_rows"].unsqueeze(2).to_broadcast([D, HEADS, WIN])

        def keys(n):
            if n >= 1:
                wait("scores_ps", n)
            for e in range(2):
                b = 2 * n + e
                kb = kT[0:D, b * WIN:(b + 1) * WIN].unsqueeze(1).to_broadcast([D, HEADS, WIN])
                do(lambda: V.tensor_tensor(keys_ex[0:D, e * 512:(e + 1) * 512].rearrange(
                    "p (h k) -> p h k", h=HEADS), kb, hr, ALU.mult), "keys_ready")

        def soft(n):
            L = wide[:, (n % 2) * 512:(n % 2 + 1) * 512].rearrange("p (h k) -> p h k", h=HEADS)
            m = sums[:, (n % 2) * 32:(n % 2) * 32 + 8]
            wait("scores_ps", n + 1)
            if n >= 2:
                wait("probs_turned", n - 1)
            link(lambda: V.scalar_tensor_tensor(out=L, in0=bank[n % 2][:].rearrange("p (h k) -> p h k", h=HEADS),
                                                scalar=HD ** -0.5, in1=rel, op0=ALU.mult, op1=ALU.add))
            link(lambda: V.tensor_reduce(m, L, AX.X, ALU.max))
            do(lambda: V.tensor_tensor(L, L, bc(m, WIN), ALU.subtract), "logits_ready")

        def norm(n):
            L = wide[:, (n % 2) * 512:(n % 2 + 1) * 512].rearrange("p (h k) -> p h k", h=HEADS)
            z = sums[:, (n % 2) * 32 + 8:(n % 2) * 32 + 16]
            wait("v_ps", n + 1)
            if n >= 1:
                wait("mixed_ps", n)
            do(lambda: V.tensor_tensor(narrow[:, 0:2 * D].rearrange("p (e c) -> p e c", e=2),
                                       bank[4][:, 0:2 * D].rearrange("p (e c) -> p e c", e=2),
                                       W["pair_mask"].unsqueeze(1).to_broadcast([128, 2, D]), ALU.mult),
               "v_ready")
            wait("probs_ready", n + 1)
            link(lambda: V.tensor_reduce(z, L, AX.X, ALU.add))
            link(lambda: V.reciprocal(z, z))
            wait("mixed_ps", n + 1)
            if n >= 2:
                wait("mixed_turned", n - 1)
            o = narrow[:, 2 * D + (n % 2) * D:2 * D + (n % 2 + 1) * D]
            do(lambda: V.tensor_tensor(o.rearrange("p (h d) -> p h d", h=HEADS),
                                       bank[6][:, 0:D].rearrange("p (h d) -> p h d", h=HEADS),
                                       bc(z, HD), ALU.mult), "mixed_norm")

        for n in range(NP + 1):
            if n < NP:
                keys(n)
                soft(n)
            if n >= 1:
                norm(n - 1)
        wait("one_ps", 1)
        wait("probs_back", NP)
        link(lambda: V.tensor_copy(work[0:D, 0:128], bank[2][0:D, 0:128]))
        do(lambda: V.tensor_tensor(work[0:D, 256:384], work[0:D, 0:128], bank[2][0:D, 128:256], ALU.mult),
           "one_prod")
        lg, zk, mx, zmax = small[:, 0:8], small[:, 8:72], small[:, 72:80], small[:, 96:97]
        link(lambda: V.tensor_reduce(zmax, W["a_rel1"][:, 1:64], AX.X, ALU.max))
        link(lambda: V.tensor_tensor(zk, W["a_rel1"], zmax.to_broadcast([128, 64]), ALU.subtract))
        wait("one_ps", 2)
        link(lambda: V.tensor_scalar(lg, bank[3][:, 0:HEADS], HD ** -0.5, W["a_rel1"][:, 0:1],
                                     ALU.mult, ALU.add))
        link(lambda: V.tensor_tensor(mx, lg, zmax.to_broadcast([128, 8]), ALU.max))
        link(lambda: V.tensor_tensor(lg, lg, mx, ALU.subtract))
        link(lambda: V.tensor_tensor(mx, zmax.to_broadcast([128, 8]), mx, ALU.subtract))
        do(lambda: V.engine_nop(), "one_step")
        wait("one_exp", 1)
        p, ez, em, zs = small[:, 128:136], small[:, 137:200], small[:, 200:208], small[:, 208:209]
        z8 = small[:, 216:224]
        link(lambda: V.tensor_reduce(zs, ez, AX.X, ALU.add))
        link(lambda: V.tensor_scalar(z8, em, zs, None, ALU.mult))
        link(lambda: V.tensor_tensor(z8, z8, p, ALU.add))
        link(lambda: V.reciprocal(z8, z8))
        link(lambda: V.tensor_tensor(z8, z8, p, ALU.mult))
        do(lambda: V.tensor_tensor(work[:, 384:384 + D].rearrange("p (h d) -> p h d", h=HEADS),
                                   bank[2][:, 256:256 + D].rearrange("p (h d) -> p h d", h=HEADS),
                                   bc(z8, HD), ALU.mult), "one_p")
        wait("one_ps", 3)
        do(lambda: V.tensor_copy(ow[:, :, WIN], bank[3][0:D, 128:256]), "one_p")

        def add_rows(g, bias, target, done, ps):
            n = min(8, NT - 8 * g)
            r = target[:, 8 * g:8 * g + n]
            wait(ps, g + 1)
            link(lambda: V.tensor_tensor(r, r, t3(bank[g % 2][:, 0:n * D]), ALU.add))
            do(lambda: V.tensor_tensor(r, r, wide_row(bias, n), ALU.add), done)

        for g in range(NG):
            add_rows(g, W["a_bproj"], hv, "proj_taken", "proj_ps")
        wait("proj_taken", NG)
        do(lambda: V.engine_nop(), "stage_done")

        layer_norm(xv, hv, yv)
        layer_norm(xv, xv, yv)
        wait("weights", w_count["b"])
        link(lambda: V.tensor_tensor(xv, xv, wide_row(W["b_gamma"], NT), ALU.mult))
        link(lambda: V.tensor_tensor(xv, xv, wide_row(W["b_beta"], NT), ALU.add))
        do(lambda: V.engine_nop(), "x_ready")
        if not dry:
            turn_back(dve, v_copy, 1, 0)
        NE = NT * EXPERTS
        L, one1, one2, tmp, wgt = [small[:, n * NE:(n + 1) * NE].rearrange("p (t e) -> p t e", e=EXPERTS)
                                   for n in range(5)]
        flat = lambda v: v.rearrange("p t e -> p (t e)")
        en = wide_row(W["expert_no"], NT)

        def first_max(oh, values, m):
            link(lambda: V.tensor_reduce(m, values, AX.X, ALU.max))
            link(lambda: V.tensor_tensor(tmp, values, bc(m, EXPERTS), ALU.is_equal))
            link(lambda: V.tensor_scalar(oh, en, -float(EXPERTS), None, ALU.add))
            link(lambda: V.tensor_tensor(tmp, tmp, oh, ALU.mult))
            link(lambda: V.tensor_reduce(st[3], tmp, AX.X, ALU.min))
            link(lambda: V.tensor_tensor(oh, oh, bc(st[3], EXPERTS), ALU.is_equal))

        def route_in(bias):
            for a, b, ps in ((0, 64, bank[2]), (64, NT, bank[3])):
                link(lambda: V.tensor_tensor(L[:, a:b], t3(ps[:, 0:(b - a) * 8], 8),
                                             wide_row(bias, b - a), ALU.add))

        wait("route_ps", 1)
        route_in(W["b_br"])
        first_max(one1, L, st[0])
        link(lambda: V.scalar_tensor_tensor(out=L, in0=one1, scalar=-3.0e38, in1=L, op0=ALU.mult, op1=ALU.add))
        first_max(one2, L, st[1])
        link(lambda: V.tensor_tensor(small[:, 0:NT], st[1], st[0], ALU.subtract))
        STEP["route_exp0"] = count[0]
        wait("route_exp", 1)
        link(lambda: V.tensor_scalar(st[0], small[:, 0:NT], 1.0, None, ALU.add))
        link(lambda: V.reciprocal(st[0], st[0]))
        link(lambda: V.tensor_tensor(st[1], small[:, 0:NT], st[0], ALU.mult))
        link(lambda: V.tensor_tensor(wgt, one1, bc(st[0], EXPERTS), ALU.mult))
        link(lambda: V.tensor_tensor(tmp, one2, bc(st[1], EXPERTS), ALU.mult))
        link(lambda: V.tensor_tensor(wgt, wgt, tmp, ALU.add))
        do(lambda: V.engine_nop(), "route_done")

        def combine(t, ps, taken, yv=yv):
            w = work[:, (t % 2) * 512:(t % 2 + 1) * 512]
            do(lambda: V.tensor_tensor(t3(w), t3(ps[:]), bc(wgt[:, t], D), ALU.mult), "y_taken")
            wait("y_taken", taken)
            do(lambda: V.tensor_reduce(yv[:, t], w.rearrange("p (e d) -> p d e", e=EXPERTS), AX.X, ALU.add),
               None if t < NT - 1 else "y_sum")

        for c, (t0, k) in enumerate(CHUNKS):
            wait("y_ps", EXPERTS * (c + 1))
            for j in range(k):
                combine(t0 + j, bank[2 + j], t0 + j + 1)
        wait("y_sum", 1)
        link(lambda: V.tensor_tensor(h[:], h[:], y, ALU.add))
        do(lambda: V.engine_nop(), "stage_done")

        layer_norm(yv, hv, xv)
        wait("weights", w_count["c"] - 16)
        do(lambda: V.memset(area[0][0:D + MEM, :], 0.0), "aug_ready")
        rms_norm(xv, yv, t3(area[2][:, 0:XC]), W["c_gpre"])
        do(lambda: V.engine_nop(), "x_ready")
        if not dry:
            turn_back(dve, v_copy, 2, 0)
            turned(dve, 2)
        wait("weights", w_count["c"])
        do(lambda: V.tensor_copy(area[0][0:D, :].rearrange("p (b n) -> p b n", n=KEYS)[:, :, 0:SEQ],
                                 xw), "aug_ready")
        for f, (t0, k) in enumerate(CHUNKS):
            n = k * 128
            qv = wide[:, (f % 2) * 512:(f % 2) * 512 + n].rearrange("p (g d) -> p g d", d=LHD)
            m = sums[:, 0:4 * k]
            wait("q_ps", f + 1)
            link(lambda: V.tensor_reduce(m, bank[2][:, 0:n].rearrange("p (g d) -> p g d", d=LHD), AX.X, ALU.max))
            if f >= 2:
                wait("q_turned", f - 1)
            do(lambda: V.tensor_tensor(qv, bank[2][:, 0:n].rearrange("p (g d) -> p g d", d=LHD), bc(m, LHD),
                                       ALU.subtract), "q_max")
            wait("q_exp", f + 1)
            link(lambda: V.tensor_reduce(m, qv, AX.X, ALU.add))
            link(lambda: V.reciprocal(m, m))
            do(lambda: V.tensor_tensor(qv, qv, bc(m, LHD), ALU.mult), "q_ready")

        def key_max(n):
            kv = bank[0][:, 0:KI * KEYS].rearrange("p (i n) -> p i n", i=KI)
            dst = keys_ex[:, (n % 2) * 512:(n % 2) * 512 + KI * KEYS].rearrange("p (i n) -> p i n", i=KI)
            m = sums[:, (n % 2) * 32:(n % 2) * 32 + KI]
            wait("kk_ps", n + 1)
            link(lambda: V.tensor_reduce(m, kv, AX.X, ALU.max))
            if n >= 2:
                wait("kk_turned", n - 1)
            do(lambda: V.tensor_tensor(dst, kv, bc(m, KEYS), ALU.subtract), "kk_norm")

        def contexts(n):
            src = keys_ex[:, (n % 2) * 512:(n % 2) * 512 + KI * KEYS].rearrange("p (i n) -> p i n", i=KI)
            z = sums[:, (n % 2) * 32 + 8:(n % 2) * 32 + 8 + KI]
            wait("kk_exp", n + 1)
            link(lambda: V.tensor_reduce(z, src, AX.X, ALU.add))
            link(lambda: V.reciprocal(z, z))
            wait("ctx_ps", n + 1)
            if n >= 1:
                wait("lin_ps", n)
            for i in range(KI):
                do(lambda: V.scalar_tensor_tensor(out=narrow[:, i * 128:(i + 1) * 128],
                                                  in0=bank[3][:, i * 128:(i + 1) * 128], scalar=z[:, i:i + 1],
                                                  in1=W["context_mask"], op0=ALU.mult, op1=ALU.mult),
                   "ctx_ready" if i == KI - 1 else None)

        for n in range(NK + 1):
            if n < NK:
                key_max(n)
            if n >= 1:
                contexts(n - 1)
        wait("lin_ps", NK)
        for g in range(NG):
            n = min(8, NT - 8 * g)
            wait("w_ps", g + 1)
            do(lambda: V.tensor_tensor(xv[:, 8 * g:8 * g + n], t3(bank[g % 2][:, 0:n * D]),
                                       wide_row(W["c_bout"], n), ALU.add), "w_taken")
        wait("w_taken", NG)
        link(lambda: V.tensor_tensor(h[:], h[:], y, ALU.add))
        rms_norm(xv, xv, yv, W["c_gout"])
        link(lambda: V.tensor_tensor(h[:], h[:], x[:], ALU.add))
        do(lambda: V.engine_nop(), "stage_done")

        layer_norm(xv, hv, t3(y_last))
        do(lambda: V.engine_nop(), "x_ready")
        if not dry:
            turn_back(dve, v_copy, 3, 0)
        wait("weights", w_count["d"])
        wait("route_ps", 2)
        route_in(W["d_bg"])
        link(lambda: V.tensor_reduce(st[0], L, AX.X, ALU.max))
        link(lambda: V.tensor_tensor(L, L, bc(st[0], EXPERTS), ALU.subtract))
        STEP["gate_exp"] = count[0]
        wait("route_exp", 2)
        link(lambda: V.tensor_reduce(st[0], L, AX.X, ALU.add))
        link(lambda: V.reciprocal(st[0], st[0]))
        link(lambda: V.tensor_tensor(L, L, bc(st[0], EXPERTS), ALU.mult))
        first_max(one1, L, st[1])
        link(lambda: V.tensor_tensor(wgt, L, one1, ALU.mult))
        do(lambda: V.engine_nop(), "route_done")
        for t in range(NT):
            wait("y_ps", EXPERTS * len(CHUNKS) + t + 1)
            combine(t, bank[4 + t % 4], NT + t + 1, t3(y_last))
        wait("y_sum", 2)
        link(lambda: V.tensor_tensor(h[:], h[:], y_last, ALU.add))
        do(lambda: V.engine_nop(), "stage_done")

    s["y_sum"] = sem("t_y_sum")
    dve_program(None, dry=True)

    def pool_program(pool):
        pass

    return sp_program, pe_program, act_program, dve_program, pool_program

def lay_out(inp, nq):
    f = {k: np.asarray(v) for k, v in inp.items()}
    io = dict(constants())
    x = f['x'][:nq*QI]
    x = x.reshape(nq, QI, SIDE, WJ, WQ, 3)
    io['x'] = np.ascontiguousarray(x.transpose(0, 4, 5, 3, 1, 2).reshape(nq, 12, QCOLS))
    def blockdiag(w, n):
        z = np.zeros((n, w.shape[0], n, w.shape[1]), w.dtype)
        for q in range(n): z[q, :, q] = w
        return z.reshape(n * w.shape[0], n * w.shape[1])
    io['fc0_w'] = blockdiag(f['L0_tok_fc0_w'], WQ)
    io['conv_w'] = np.concatenate([blockdiag(f['L0_tok_conv_w'][l].T, WQ) for l in range(LAYERS)], 1)
    col = lambda first, rest: np.ascontiguousarray(np.tile(np.concatenate([first[None], rest]), (1, WQ)).T)
    io['bias_in'] = col(f['L0_tok_fc0_b'], f['L0_tok_conv_b'])
    io['gain'] = col(f['L0_tok_ln0_g'], f['L0_tok_ln_g'])
    io['shift'] = col(f['L0_tok_ln0_b'], f['L0_tok_ln_b'])
    io['fc1_w'] = blockdiag(f['L0_tok_fc1_w'], WQ)
    io['fc1_b'] = f['L0_tok_fc1_b'][:, None]
    io['fc2_w'] = f['L0_tok_fc2_w']
    io['fc2_b'] = np.tile(f['L0_tok_fc2_b'], 2)[:, None]
    z = np.zeros((2, 64, 16, 32), np.float32)
    for pr in range(16):
        for e in range(2):
            z[e, :, pr, 2 * pr + e] = f['L0_tok_fc3_w'][:, 0]
    io['fc3_sel'] = z.reshape(128, 512)
    io['fc3_b'] = np.broadcast_to(f['L0_tok_fc3_b'][:, None], (32, 1))
    mw = np.zeros((LAYERS, 2, KY, CH, 2, KX, CH), np.float32)
    for kind, (a, b) in enumerate((('w1r', 'w2r'), ('w1i', 'w2i'))):
        wp, wm = f['L0_tok_' + a], f['L0_tok_' + b]
        mw[:, kind, :, :, 0, :12] = wp.transpose(0, 4, 1, 3, 2)
        mw[:, kind, :, :, 1, 1:] = wm[:, :, :, ::-1].transpose(0, 4, 1, 3, 2)
    io['mix_w'] = mw.reshape(LAYERS, 2, KY, CH, 2 * KX * CH)
    return {k: np.ascontiguousarray(v) for k, v in io.items()}


def lay_out_tail(inp):
    f = {k: np.asarray(v) for k, v in inp.items()}
    io = dict(tail_constants())
    over = lambda v: np.broadcast_to(v.reshape(1, -1), (128, v.size))
    w = f["L0_attn_w_qkv"].T
    io["a_wq"], io["a_wk"], io["a_wv"] = w[:, 0:64], w[:, 64:128], w[:, 128:192]
    io["a_wproj"] = f["L0_attn_w_proj"].T
    io["a_bproj"] = over(f["L0_attn_b_proj"])
    pos = np.arange(WIN)
    io["a_rel"] = np.tile(f["L0_attn_rel_bias"][pos[None, :] - pos[:, None] + WIN - 1], (2, 1))
    io["a_rel1"] = over(f["L0_attn_rel_bias"][WIN - 1:])
    io["b_gamma"], io["b_beta"] = over(f["L0_ffn_gamma"]), over(f["L0_ffn_beta"])
    io["b_wr"], io["b_br"] = f["L0_ffn_Wr"], over(f["L0_ffn_br"])
    io["b_w1"] = f["L0_ffn_W1"].transpose(1, 0, 2).reshape(D, -1)
    io["b_b1"] = f["L0_ffn_b1"].T
    io["b_w2"] = f["L0_ffn_W2"].transpose(1, 0, 2).reshape(HID, -1)
    io["b_b2"] = f["L0_ffn_b2"].reshape(1, -1)
    w, mem = f["L1_attn_w_qkv"], f["L1_attn_mem_kv"]
    io["c_wq"] = w[:, 0:128]
    io["c_wk"] = np.concatenate([w[:, 128:256], mem[0].reshape(128, MEM).T])
    io["c_wv"] = np.concatenate([w[:, 256:384], mem[1].reshape(128, MEM).T])
    io["c_wout"], io["c_bout"] = f["L1_attn_w_out"], over(f["L1_attn_b_out"])
    io["c_gout"], io["c_gpre"] = over(f["L1_attn_g_out"]), over(f["L1_attn_g_pre"])
    io["d_w1"] = f["L1_ffn_W1"]
    io["d_b1"] = f["L1_ffn_b1"].reshape(2, HID).T
    halves = lambda v: v.reshape(2, HID, -1).transpose(1, 0, 2).reshape(HID, -1)
    io["d_wg"], io["d_bg"] = halves(f["L1_ffn_Wg"]), over(f["L1_ffn_bg"])
    io["d_wd"] = halves(f["L1_ffn_Wd"].transpose(1, 0, 2))
    io["d_bd"] = f["L1_ffn_bd"].reshape(1, -1)
    io["cls"] = f["cls_tok"].reshape(1, -1)
    return {k: np.ascontiguousarray(v) for k, v in io.items()}


def build(nc, io, out, nq=32):
    with ExitStack() as ctx:
        bank = [ctx.enter_context(nc.psum_tensor(f"bank{n}", [128, CHUNK], F32)) for n in range(8)]

        def sem(name):
            return ctx.enter_context(nc.semaphore(name))

        tokens = nc.dram_tensor("tokens", [nq * QI * SEQ, D], F32, kind="Internal").ap()
        grid = tokens.rearrange("(q a e n) w -> q e n a w", a=2, e=2, n=SEQ)[:, :, 1:]
        with ExitStack() as first:
            tower = token_tower(
                nc, io, nq, bank, sem, lambda n, sh, dt: first.enter_context(nc.sbuf_tensor(n, sh, dt)),
                lambda n, sh, dt: nc.dram_tensor(n, sh, dt, kind="Internal").ap(), grid)
        ts = tower[0]

        def tower_done(sp):
            sp.dma_start(tokens.rearrange("(b n) w -> n b w", n=SEQ)[0],
                         io["cls"].to_broadcast([nq * QI, D])).then_inc(ts["cls_stored"], 16)
            sp.wait_ge(ts["cls_stored"], 16)
            sp.wait_ge(ts["tok_stored"], 32 * nq)

        rest = token_transformer(
            nc, io, bank, sem, lambda n, sh, dt: ctx.enter_context(nc.sbuf_tensor(n, sh, dt)), tower_done,
            tokens, out.rearrange("b n d -> (b n) d").rearrange("(t p) d -> p t d", p=128))
        block = ctx.enter_context(nc.Block())

        @block.sync
        def _(sp):
            tower[1](sp)
            rest[0](sp)

        @block.tensor
        def _(pe):
            tower[2](pe)
            rest[1](pe)

        @block.scalar
        def _(act):
            tower[3](act)
            rest[2](act)

        @block.vector
        def _(dve):
            tower[4](dve)
            rest[3](dve)

        @block.gpsimd
        def _(pool):
            tower[5](pool)


def kernel(**inputs):
    import concourse.bacc as bacc
    from concourse.bass_utils import run_bass_kernel_spmd

    nc = bacc.Bacc("TRN2", target_bir_lowering=False, num_devices=1)
    arrays = {f"in_{k}": v for k, v in {**lay_out(inputs, 32), **lay_out_tail(inputs)}.items()}
    io = {k[3:]: nc.dram_tensor(k, v.shape, mybir.dt.from_np(v.dtype), kind="ExternalInput").ap()
          for k, v in arrays.items()}
    out = nc.dram_tensor("out", (128, SEQ, D), F32, kind="ExternalOutput").ap()
    build(nc, io, out)
    return run_bass_kernel_spmd(nc, [arrays], core_ids=[0]).results[0]["out"]
```

```python
from contextlib import ExitStack

import numpy as np

import concourse.bass as bass
from concourse import mybir

ALU = mybir.AluOpType
ACT = mybir.ActivationFunctionType
AX = mybir.AxisListType
F32 = mybir.dt.float32
BF16 = mybir.dt.bfloat16
F16 = mybir.dt.float16

SIDE = 64
CH = 32
LAYERS = 4
KY = 12
KX = 13
WQ = 4
WJ = SIDE // WQ
QI = 4
CHUNK = 512
QCOLS = WJ * QI * SIDE
NCH = QCOLS // CHUNK
EPS = 1e-5
SK = 2 * KX
XROWS = NCH * 3 * WQ
RK = 2 * KY
MODES = KY * KX
VCOLS = CH // 4 * 2 * KX * QI
D_FILLS, A_FILLS, B_FILLS, T_FILLS = 4, 4, 2, 4
W_SCALE = 64.0
MIX_SCALE = 1.0 / 8
INV_SCALE = W_SCALE / MIX_SCALE
B_SETS = (range(0, 7), range(7, 13))


def split16(v):
    high = v.astype(np.float16)
    return np.concatenate([high, (v - high.astype(v.dtype)).astype(np.float16)], 1)


def constants():
    y = np.arange(SIDE)
    ky, kx = np.arange(KY), np.arange(KX)
    th = 2 * np.pi * np.outer(y, kx) / SIDE
    ph = 2 * np.pi * np.outer(y, ky) / SIDE
    fy = np.concatenate([np.cos(th), np.sin(th)], 1)
    fw = np.concatenate([np.cos(ph), np.sin(ph)], 1)
    two = np.eye(2)
    weight = INV_SCALE * np.where(ky == 0, 1.0, 2.0)[:, None] / SIDE ** 2
    iw = np.concatenate([weight * np.cos(ph.T), -weight * np.sin(ph.T)], 0)
    iy = fy.T
    c = {
        "fwd_y": np.kron(two, fy),
        "fwd_w": np.kron(two, fw),
        "inv_w": np.einsum("rw,ab->rabw", iw, np.eye(4)).reshape(RK * 4, 4 * SIDE),
        "inv_y": np.einsum("sy,ab->saby", iy, np.eye(QI)).reshape(SK * QI, QI * SIDE),
        "ident": np.eye(128),
        "center": np.eye(128) - np.kron(np.eye(4), np.full((CH, CH), 1.0 / CH)),
    }
    c["mean_sel"] = np.kron(np.eye(WQ), np.full((CH, 1), 1.0 / CH))
    back = np.zeros((96, NCH, 128))
    for part in range(3):
        for q in range(WQ):
            for t in range(NCH):
                back[part * 32 + t * WQ + q, t, q * CH:(q + 1) * CH] = 1.0
    c["spread_sel"] = back.reshape(96, NCH * 128)
    pos = np.array([[1, 1, 1, -1], [1, -1, -1, -1], [-1, 1, 1, 1], [1, 1, 1, -1]], float).T
    neg = np.array([[1, -1, 1, 1], [1, 1, -1, 1], [1, 1, -1, 1], [-1, 1, -1, -1]], float).T
    signs = np.stack([pos, neg], 2).reshape(4, 8)
    c["sign"] = np.repeat(np.concatenate([signs, np.full((4, 1), 1.0 / CH), np.ones((4, 1))], 1), CH, 0)
    out = {k: v.astype(np.float32) for k, v in c.items()}
    for name in ("fwd_y", "fwd_w", "inv_w", "inv_y"):
        out[name] = split16(c[name])
    out["ident16"] = c["ident"].astype(np.float16)
    return {k: np.ascontiguousarray(v) for k, v in out.items()}


def token_tower(nc, io, nq, bank, sem, sb, dram, tok):
    ni = nq * QI

    h_dram = dram("h_dram", [nq, 128, 2 * QCOLS], F16)
    mix_dram = dram("mix_dram", [LAYERS * KY, 128, KX * 128], F32)
    spec_dram = dram("spec_dram", [nq, RK, 4 * VCOLS], F32)

    fwd_y = sb("fwd_y", [128, 2 * 2 * SK], F16)
    fwd_w = sb("fwd_w", [128, 2 * 2 * RK], F16)
    inv_w = sb("inv_w", [96, 2 * 4 * SIDE], F16)
    inv_y = sb("inv_y", [SK * QI, 2 * QI * SIDE], F16)
    ident = sb("ident", [128, 128], F32)
    ident16 = sb("ident16", [128, 128], F16)
    center = sb("center", [128, 128], F32)
    mean_sel = sb("mean_sel", [128, WQ], F32)
    ident_b = sb("ident_b", [128, 128], BF16)
    spread_sel = sb("spread_sel", [96, NCH * 128], BF16)
    sign = sb("sign", [128, 10], F32)
    conv_w = sb("conv_w", [128, 2 * LAYERS * 128], F16)
    col_sum = sb("col_sum", [128, NCH * WQ], F32)
    bias_in = sb("bias_in", [128, LAYERS + 1], F32)
    bias = sb("bias", [128, LAYERS + 1], F32)
    gain = sb("gain", [128, LAYERS + 1], F32)
    shift = sb("shift", [128, LAYERS + 1], F32)
    fc1_w = sb("fc1_w", [128, 2 * WQ * 128], F16)
    fc1_b = sb("fc1_b", [128, 1], F32)
    fc2_w = sb("fc2_w", [128, 2 * 64], F16)
    fc2_b = sb("fc2_b", [128, 1], F32)
    fc3_sel = sb("fc3_sel", [128, 2 * 16 * 32], F16)
    fc3_b = sb("fc3_b", [32, 1], F32)

    h_in = sb("h_in", [128, QCOLS], F32)
    h_next = sb("h_next", [128, QCOLS], F32)
    dev = sb("dev", [128, QCOLS], F32)
    rows = sb("rows", [128, QCOLS], F32)
    SQ = 2
    squares = sb("squares", [128, SQ * CHUNK], F32)
    spec_y = sb("spec_y", [128, 2 * CH * 2 * SK], F16)
    half_inv = sb("half_inv", [SK * QI, 2 * CH * SIDE], F16)
    mixed_in = sb("mixed_in", [96, VCOLS], F32)
    mixed = sb("mixed", [96, 2 * VCOLS], F16)
    spec = sb("spec", [128, MODES * ni], F32)
    var_eps = sb("var_eps", [128, 128], F32)
    seed = sb("seed", [128, 128], mybir.dt.int32)
    rstd = sb("rstd", [128, 128], F32)
    newton = sb("newton", [128, 128], F32)
    rest = sb("rest", [128, 128], F32)
    split = sb("split", [128, 4 * 96], BF16)
    parts = sb("parts", [96, CHUNK], BF16)
    prep_in = sb("prep_in", [128, 4 * KX * CH], F32)
    prep_fold = sb("prep_fold", [128, 4 * KX * CH // 2], F32)
    prep_tmp = sb("prep_tmp", [128, 4 * KX * CH], F32)
    prep_out = sb("prep_out", [128, KX * 128], F32)
    stage_cols = nq * KX * QI
    h_in16, h_next16, rows16 = (t[:].bitcast(F16) for t in (h_in, h_next, rows))
    spec16 = spec[:].bitcast(F16)
    H1, H2 = 4, 2
    hidden1_full = [rows[:, b * CHUNK:(b + 1) * CHUNK] for b in range(H1)]
    hidden1 = [[rows16[:, (2 * H1 + 2 * b + e) * CHUNK:(2 * H1 + 2 * b + e + 1) * CHUNK] for e in range(2)]
               for b in range(H1)]
    hidden2_full = [spec[:, b * CHUNK:(b + 1) * CHUNK] for b in range(H2)]
    hidden2 = [[spec16[:, (2 * H2 + 2 * b + e) * CHUNK:(2 * H2 + 2 * b + e + 1) * CHUNK] for e in range(2)]
               for b in range(H2)]
    logits = spec_y[:].bitcast(F32)[:, 0:CHUNK]
    tok_rows = spec_y[:].bitcast(F32)[:, CHUNK:CHUNK + 2 * SIDE]
    fc0_w = half_inv[0:XROWS, 0:2 * NCH * 128]
    x_in = h_in[0:XROWS, 0:CHUNK]
    x16 = h_in16[0:XROWS, 2 * CHUNK:4 * CHUNK]
    raw, at = {}, 0
    for name, p, cols in (("spread_sel", 96, NCH * 128), ("conv_w", 128, LAYERS * 128),
                          ("fc1_w", 128, WQ * 128), ("fc2_w", 128, 64), ("fc3_sel", 128, 16 * 32), ("fc0_w", XROWS, NCH * 128)):
        raw[name] = dev[0:p, at:at + cols]
        at += cols

    PASSES = ((0, 0), (1, 0), (0, 1))

    def product(out, left, right, start=True, stop=True):
        for n, (a, b) in enumerate(PASSES):
            mm = nc.tensor.matmul(out, left(a), right(b), start=start and n == 0, stop=stop and n == 2)
        return mm

    turn_ps, inv_ps, conv_ps = (bank[0], bank[1]), (bank[2], bank[3]), (bank[4], bank[5])
    var_ps, logit_ps, spread_ps = bank[6], bank[7], bank[7]

    names = ("consts_in consts_ready h_loaded0 h_loaded1 h_loaded2 h_loaded3 mixed_loaded mixed_high mixed_split h_stored0 h_stored1 h_stored2 h_stored3 spec_stored0 spec_stored1 "
             "mix_loaded0 mix_loaded1 mix_loaded2 mix_loaded3 prep_loaded prep_stored tok_stored prep_step prep_signed prep_term x_loaded x_high x_split "
             "inv_half_ps inv_half_high inv_half conv_done dev_ready square_ready var_added split_ready "
             "parts_turned rstd_step fold_step cls_stored parts_ready spread_done normed gelu_done "
             "h_high h_ready turned_high turned_low turn_dve turn_act fy_done fy_high fy_taken "
             "fw_done fw_taken mix_done mix_act mix_dve bias_ps "
             "fc1_done fc1_act high1 low1 low1_dve fc2_done fc2_act high2 low2 fc3_done logits_zero logit_taken tok_turned tok_ready")
    s = {n: sem(n) for n in names.split()}

    v_mix_w = [t[:, b * KX * 128:(b + 1) * KX * 128] for t in (h_next, rows) for b in range(2)]
    v_stage = [dev[:, b * stage_cols:(b + 1) * stage_cols] for b in range(2)]
    spec_v = spec[:].rearrange("p (q k n) -> p q k n", q=KY, k=KX)

    loads = [(t[:], n) for t, n in (
        (fwd_y, "fwd_y"), (fwd_w, "fwd_w"), (inv_w, "inv_w"), (inv_y, "inv_y"), (ident, "ident"),
        (ident16, "ident16"), (center, "center"), (mean_sel, "mean_sel"), (sign, "sign"),
        (bias_in, "bias_in"), (gain, "gain"), (shift, "shift"), (fc1_b, "fc1_b"), (fc2_b, "fc2_b"),
        (fc3_b, "fc3_b"))] + [(raw[n], n) for n in raw]
    N_CONST = 16 * len(loads)
    MIX_SETS = (range(0, 4), range(4, 8), range(8, 12), range(12, 13))

    def quads(eng, first, last, body):
        if last - first == 1:
            body(first)
        elif last > first:
            with eng.Fori(first, last) as i:
                body(i)

    def pipeline(eng, P, steps, between, prologue, epilogue, preps=0):
        prologue()
        steps(-1, 2, False)
        between(-1, 2)
        for i in (0, 1):
            steps(i, 2, i < preps)
            between(i, 2)

        def both(i, prep):
            steps(i, 2, prep)
            between(i, 2)

        middle = max(2, min(preps, nq - 2))
        quads(eng, 2, middle, lambda i: both(i, True))
        quads(eng, middle, nq - 2, lambda i: both(i, False))
        for i in (nq - 2, nq - 1):
            steps(i, nq - 1 - i, i < preps)
            between(i, nq - 1 - i)
        epilogue()

    def has(i, before=0):
        return not isinstance(i, int) or i - before >= 0

    def low1_count(u):
        return u // H1 + 1 if u % H1 == H1 - 1 else (H1 - 1) * (u // H1) + u % H1 + 1

    def low1_signal(i, u):
        return ((s["low1_dve"], 32 // H1 * i + low1_count(u)) if u % H1 == H1 - 1
                else (s["low1"], 32 // H1 * (H1 - 1) * i + low1_count(u)))

    def h_piece(h, piece):
        return h.rearrange("p (e c) -> p e c", e=2)[:, :, 2 * piece * CHUNK:2 * (piece + 1) * CHUNK]

    def half_view(part, f):
        return half_inv[:].rearrange("p (h w o e) -> p h e o w", h=2, w=SIDE, e=8)[:, part, 2 * f:2 * f + 2]

    def rows_view(part, f):
        return rows16.rearrange("p (h a w c) -> p h w a c", h=2, a=2, w=WJ)[:, part, 4 * f:4 * f + 4]

    def spec_y_view(part, f):
        return spec_y[:].rearrange("p (h k e c) -> p h c e k", h=2, k=KX, c=CH)[:, part, 8 * f:8 * f + 8]

    TURN_AT = {4: 0, 6: 1, 8: 2, 10: 3}
    STEPS, LAG = NCH + 3, 3
    ROOT_STEP = 8
    HEAD_STEPS = 39
    CONST_STEPS = 15
    PREP_STEPS = 11

    def sp_program(sp):
        for t, name in loads:
            sp.dma_start(t, io[name]).then_inc(s["consts_in"], 16)
        for P in range(LAYERS + 1):
            if P > 0:
                sp.wait_ge(s["turned_low"], T_FILLS * P * nq)
                for piece in range(4):
                    sp.dma_start(h_piece(h_in16, piece), h_piece(h_dram[0], piece)
                                 ).then_inc(s[f"h_loaded{piece}"], 16)
                sp.wait_ge(s["fy_done"], A_FILLS * P * nq)

                def load_mix(ky, P=P):
                    n = (P - 1) * KY + ky
                    sp.wait_ge(s["prep_stored"], 16 * (n + 1))
                    if ky >= 4:
                        sp.wait_ge(s["mix_done"], 4 * (n - 3))
                    sp.dma_start(v_mix_w[ky % 4], mix_dram[n]).then_inc(s[f"mix_loaded{ky % 4}"], 16)

                for ky in range(3):
                    load_mix(ky)
                for ky in range(KY):
                    n = (P - 1) * KY + ky
                    if ky + 3 < KY:
                        load_mix(ky + 3)
                    sp.wait_ge(s["mix_act"], 2 * (n + 1))
                    sp.wait_ge(s["mix_dve"], 2 * (n + 1))
                    dst = spec_dram.rearrange("a (r q) (o s m) -> r s q o a m", r=2, o=CH, s=2)
                    src = v_stage[ky % 2].rearrange("p (a m) -> p a m", a=nq)
                    for sr in range(4):
                        sp.dma_start(dst[sr % 2, sr // 2, ky], src[32 * sr:32 * sr + 32]
                                     ).then_inc(s[f"spec_stored{ky % 2}"], 16)

            def load_mixed(i, P=P):
                sp.dma_start(mixed_in[:], spec_dram[i].rearrange("r (a c) -> (r a) c", a=4)
                             ).then_inc(s["mixed_loaded"], 16)

            def store_h(i, piece, P=P):
                sp.wait_ge(s["h_ready"], 8 * (P * nq + i) + 2 * piece + 2)
                sp.dma_start(h_piece(h_dram[i], piece), h_piece(h_next16, piece)
                             ).then_inc(s[f"h_stored{piece}"], 16)

            def load_h(i, piece, P=P):
                g = P * nq + i
                if has(i, 1):
                    sp.wait_ge(s["conv_done"], 8 * (g - 1) + 2 * piece + 2)
                sp.dma_start(h_piece(h_in16, piece), h_piece(h_dram[i], piece)
                             ).then_inc(s[f"h_loaded{piece}"], 16)

            def load_x(i):
                if has(i, 1):
                    sp.wait_ge(s["x_split"], i)
                sp.dma_start(x_in, io["x"][i]).then_inc(s["x_loaded"], 16)

            def store_prep(ky, P=P):
                sp.wait_ge(s["prep_step"], PREP_STEPS * (P * KY + ky + 1))
                sp.dma_start(mix_dram[P * KY + ky], prep_out[:]).then_inc(s["prep_stored"], 16)

            def load_prep(ky, P=P):
                for grp in range(4):
                    first = 0 if grp in (0, 3) else 1
                    for t in range(2):
                        sp.dma_start(prep_in[32 * grp:32 * grp + 32, t * 2 * KX * CH:(t + 1) * 2 * KX * CH],
                                     io["mix_w"][P, first ^ t, ky]).then_inc(s["prep_loaded"], 16)

            def next_mixed(i, P=P):
                sp.wait_ge(s["mixed_split"], (P - 1) * nq + i)
                load_mixed(i)

            def prologue(P=P):
                if P == 0:
                    load_x(0)
                else:
                    sp.wait_ge(s["spec_stored0"], 32 * KY * P)
                    sp.wait_ge(s["spec_stored1"], 32 * KY * P)
                    load_mixed(0)

            def steps(i, after, prep, P=P):
                if prep:
                    load_prep(i)
                if P > 0 and after == 2:
                    next_mixed(i + 2)
                if P == 0 and after == 2:
                    load_x(i + 2)
                for u in range(6):
                    if u < 4 and has(i) and P < LAYERS:
                        store_h(i, u)
                    if u >= 2 and after == 2 and P > 0:
                        load_h(i + 2, u - 2)
                if prep:
                    store_prep(i)

            def between(i, after):
                pass

            def steps_first(i, after, prep, P=P):
                if isinstance(i, int) and i == -1:
                    if P == 0:
                        load_x(1)
                    else:
                        next_mixed(1)
                        for piece in range(4):
                            load_h(1, piece)
                else:
                    steps(i, after, prep)

            def epilogue(P=P):
                if P < LAYERS:
                    for ky in range(preps, KY):
                        load_prep(ky)
                        store_prep(ky)
                    for piece in range(4):
                        sp.wait_ge(s[f"h_stored{piece}"], 16 * (P + 1) * nq)

            preps = min(KY, nq - 2) if P < LAYERS else 0
            pipeline(sp, P, steps_first, between, prologue, epilogue, preps)
        sp.wait_ge(s["tok_stored"], 32 * nq)

    def pe_program(pe):
        pe.wait_ge(s["consts_in"], N_CONST)
        nc.tensor.matmul(logit_ps[:, 0:LAYERS + 1], center[:], bias_in[:], start=True, stop=True
                         ).then_inc(s["bias_ps"], 1)
        pe.wait_ge(s["consts_ready"], CONST_STEPS)
        for P in range(LAYERS + 1):
            if P > 0:
                pe.wait_ge(s["fw_taken"], B_FILLS * P * nq)
                for ky in range(KY):
                    n = (P - 1) * KY + ky
                    pe.wait_ge(s[f"mix_loaded{ky % 4}"], 16 * (n // 4 + 1))
                    for f, ks in enumerate(MIX_SETS):
                        ps = (turn_ps + inv_ps)[f]
                        if n > 0:
                            pe.wait_ge(s["mix_act" if f % 2 == 0 else "mix_dve"], 2 * (n - 1) + f // 2 + 1)
                        for j, k in enumerate(ks):
                            mm = nc.tensor.matmul(ps[:, j * ni:(j + 1) * ni],
                                                  v_mix_w[ky % 4][:, k * 128:(k + 1) * 128],
                                                  spec_v[:, ky, k, :], start=True, stop=True)
                        mm.then_inc(s["mix_done"], 1)
                pe.wait_ge(s["mix_act"], 2 * P * KY)
                pe.wait_ge(s["mix_dve"], 2 * P * KY)

            def inverse_w(i, f, P=P):
                gd = (P - 1) * nq + i
                if f == 0:
                    pe.wait_ge(s["mixed_split"], gd + 1)
                    if P < LAYERS and has(i, 3):
                        pe.wait_ge(s["fw_taken"], B_FILLS * (P * nq + i - 2))
                if f >= 2:
                    pe.wait_ge(s["inv_half"], D_FILLS * gd + f - 1)
                mv = mixed[:].rearrange("p (e o m) -> p e o m", e=2, o=8)
                for j in range(2):
                    mm = product(inv_ps[f % 2][0:SK * QI, j * 256:(j + 1) * 256],
                                 lambda e: mv[:, e, 2 * f + j, :],
                                 lambda e: inv_w[:, e * 256:(e + 1) * 256])
                mm.then_inc(s["inv_half_ps"], 1)

            def add_var(g, t):
                pe.wait_ge(s["square_ready"], 8 * g + t + 1)
                if t == 0 and not (isinstance(g, int) and g == 0):
                    pe.wait_ge(s["parts_ready"], g)
                for j in range(4):
                    c = (t % SQ) * CHUNK + j * 128
                    o = j * 32 + t * WQ
                    mm = nc.tensor.matmul(var_ps[:, o:o + WQ], squares[:, c:c + 128], mean_sel[:],
                                          start=True, stop=True)
                mm.then_inc(s["var_added"], 1)

            def convolve(i, t, P=P):
                g = P * nq + i
                if t == 0 and P > 0:
                    pe.wait_ge(s["inv_half"], D_FILLS * (g - nq + 1))
                if P == 0 and t == 0:
                    pe.wait_ge(s["x_split"], g + 1)
                if P > 0 and t % 2 == 0:
                    pe.wait_ge(s[f"h_loaded{t // 2}"], 16 * (g - nq + 1))
                if t >= 2 or P > 0 or has(i, 1):
                    pe.wait_ge(s["dev_ready"], 8 * g + t - 1)
                if P == 0:
                    mm = product(conv_ps[t % 2][:],
                                 lambda e: fc0_w[:, (e * NCH + t) * 128:(e * NCH + t + 1) * 128],
                                 lambda e: x16[:, e * CHUNK:(e + 1) * CHUNK])
                else:
                    hv = half_inv[:].rearrange("p (e w o) -> p e w o", e=2, w=SIDE)
                    product(conv_ps[t % 2][:],
                            lambda e: conv_w[:, (e * LAYERS + P - 1) * 128:(e * LAYERS + P) * 128],
                            lambda e: h_in16[:, e * QCOLS + t * CHUNK:e * QCOLS + (t + 1) * CHUNK],
                            stop=False)
                    for j in range(2):
                        wj = 2 * t + j
                        mm = product(conv_ps[t % 2][:, j * 256:(j + 1) * 256],
                                     lambda e: hv[:, e, wj * WQ:(wj + 1) * WQ, :],
                                     lambda e: inv_y[:, e * 256:(e + 1) * 256],
                                     start=False, stop=(j == 1))
                mm.then_inc(s["conv_done"], 1)

            def spread(i, t, P=P):
                g = P * nq + i
                if t == 0:
                    pe.wait_ge(s["parts_ready"], g + 1)
                    if P == LAYERS and has(i, 1):
                        pe.wait_ge(s["logit_taken"], i)
                if t > 0 or P > 0 or has(i, 1):
                    pe.wait_ge(s["normed"], 8 * g + t)
                nc.tensor.matmul(spread_ps[:], spread_sel[:, t * 128:(t + 1) * 128], parts[:],
                                 start=True, stop=True).then_inc(s["spread_done"], 1)

            def turn_parts(i, P=P):
                pe.wait_ge(s["split_ready"], P * nq + i + 1)
                for j in range(4):
                    mm = nc.tensor.matmul(var_ps[0:96, j * 128:(j + 1) * 128],
                                          split[:, j * 96:(j + 1) * 96], ident_b[:], start=True, stop=True)
                mm.then_inc(s["parts_turned"], 1)

            def turn(i, f, P=P):
                g = P * nq + i
                pe.wait_ge(s["h_ready"], 8 * g + 2 * f + 2)
                if f == 0 and (P > 0 or has(i, 1)):
                    pe.wait_ge(s["fy_taken"], A_FILLS * g)
                for e, name, left in ((0, "turned_high", "turn_act"), (1, "turned_low", "turn_dve")):
                    if f > 0:
                        pe.wait_ge(s[left], T_FILLS * g + f)
                    ps = turn_ps[e][:].bitcast(F16)
                    for j in range(8):
                        c = e * QCOLS + 2 * f * CHUNK + j * 128
                        mm = nc.tensor.transpose(ps[:, j * 128:(j + 1) * 128],
                                                 h_next16[:, c:c + 128], ident16[:])
                    mm.then_inc(s[name], 1)

            def forward_y(i, f, P=P):
                g = P * nq + i
                if f == 0:
                    pe.wait_ge(s["turn_dve"], T_FILLS * (g + 1))
                    pe.wait_ge(s["turn_act"], T_FILLS * (g + 1))
                if f >= 2:
                    pe.wait_ge(s["fy_taken"], A_FILLS * g + f - 1)
                rv = rows16.rearrange("p (e a w c) -> p e a w c", e=2, a=2, w=SIDE)
                for j in range(8):
                    mm = product(turn_ps[f % 2][:, j * 2 * SK:(j + 1) * 2 * SK],
                                 lambda e: rv[:, e, :, :, 8 * f + j],
                                 lambda e: fwd_y[:, e * 2 * SK:(e + 1) * 2 * SK])
                mm.then_inc(s["fy_done"], 1)

            def forward_w(i, P=P):
                pe.wait_ge(s["fy_taken"], A_FILLS * (P * nq + i + 1))
                yv = spec_y[:].rearrange("p (e k m) -> p e k m", e=2, k=KX)
                for f, ks in enumerate(B_SETS):
                    for j, k in enumerate(ks):
                        mm = product(inv_ps[f][:, j * 2 * RK:(j + 1) * 2 * RK],
                                     lambda e: yv[:, e, k, :],
                                     lambda e: fwd_w[:, e * 2 * RK:(e + 1) * 2 * RK])
                    mm.then_inc(s["fw_done"], 1)

            def prologue(P=P):
                if P > 0:
                    inverse_w(0, 0)
                    inverse_w(0, 1)

            def steps(i, after, prep, P=P):
                g = P * nq + i
                for t in range(STEPS):
                    if t < NCH and has(i):
                        spread(i, t)
                    if t < 2 and P > 0 and after >= 1:
                        inverse_w(i + 1, 2 + t)
                    if t < A_FILLS and P < LAYERS and has(i, 1):
                        forward_y(i - 1, t)
                    if t >= LAG and after >= 1:
                        convolve(i + 1, t - LAG)
                        if t >= LAG + 2:
                            add_var(g + 1, t - LAG - 2)
                    if t == A_FILLS + 1 and P < LAYERS and has(i, 1):
                        forward_w(i - 1)
                    if t in TURN_AT and P < LAYERS and has(i):
                        turn(i, TURN_AT[t])
                if after >= 1:
                    add_var(g + 1, NCH - 2)
                    add_var(g + 1, NCH - 1)

            def between(i, after, P=P):
                if P > 0 and after == 2:
                    inverse_w(i + 2, 0)
                    inverse_w(i + 2, 1)
                if P == LAYERS and has(i):
                    head(i, after)
                elif after >= 1:
                    turn_parts(i + 1)

            def epilogue(P=P):
                if P < LAYERS:
                    for f in range(A_FILLS):
                        forward_y(nq - 1, f)
                    forward_w(nq - 1)

            def head(i, after):
                def fc1(u):
                    t, q = divmod(u, WQ)
                    if q == 0:
                        pe.wait_ge(s["h_ready"], 8 * (LAYERS * nq + i) + t + 1)
                    if u == 0 and has(i, 1):
                        pe.wait_ge(s["tok_ready"], i)
                    if u >= 2 or not (isinstance(i, int) and i == 0):
                        pe.wait_ge(s["fc1_act"], 32 * i + u - 1)
                    product(turn_ps[u % 2][:], lambda e: fc1_w[:, (e * WQ + q) * 128:(e * WQ + q + 1) * 128],
                            lambda e: h_next16[:, e * QCOLS + t * CHUNK:e * QCOLS + (t + 1) * CHUNK]
                            ).then_inc(s["fc1_done"], 1)

                def fc2(u):
                    pr = u // 2
                    pe.wait_ge(*low1_signal(i, u))
                    if u % 2 == 0 and (pr >= 2 or not (isinstance(i, int) and i == 0)):
                        pe.wait_ge(s["fc2_act"], 16 * i + pr - 1)
                    half = slice(64 * (u % 2), 64 * (u % 2) + 64)
                    product(inv_ps[pr % 2][half, :], lambda e: fc2_w[:, e * 64:(e + 1) * 64],
                            lambda e: hidden1[u % H1][e]).then_inc(s["fc2_done"], 1)

                def fc3(pr):
                    pe.wait_ge(s["low2"], 16 * i + pr + 1)
                    if pr == 0:
                        pe.wait_ge(s["normed"], 8 * (LAYERS * nq + i + 1))
                    product(logit_ps[0:32, :], lambda e: fc3_sel[:, (e * 16 + pr) * 32:(e * 16 + pr + 1) * 32],
                            lambda e: hidden2[pr % H2][e], start=(pr == 0), stop=(pr == 15)
                            ).then_inc(s["fc3_done"], 1)

                for u in range(HEAD_STEPS):
                    if u < 32:
                        fc1(u)
                    if 3 <= u < 35:
                        fc2(u - 3)
                    if u >= 8 and u % 2 == 0:
                        fc3((u - 8) // 2)
                    if u == ROOT_STEP and after >= 1:
                        turn_parts(i + 1)
                pe.wait_ge(s["logit_taken"], i + 1)
                for a in range(2):
                    for j in range(2):
                        c = j * 256 + a * 128
                        o = (a * 2 + j) * 128
                        mm = nc.tensor.transpose(turn_ps[0][:, o:o + 128], logits[:, c:c + 128], ident[:])
                mm.then_inc(s["tok_turned"], 1)

            pipeline(pe, P, steps, between, prologue, epilogue)

    def act_program(act):
        act.wait_ge(s["consts_ready"], CONST_STEPS)
        for P in range(LAYERS + 1):
            if P > 0:
                act.wait_ge(s["gelu_done"], 8 * P * nq)
                for ky in range(KY):
                    n = (P - 1) * KY + ky
                    stage = v_stage[ky % 2].rearrange("p (a k n) -> p k a n", a=nq, k=KX)
                    if ky >= 2:
                        act.wait_ge(s[f"spec_stored{ky % 2}"], 64 * (n // 2))
                    for f in (0, 2):
                        act.wait_ge(s["mix_done"], 4 * n + f + 1)
                        ks = MIX_SETS[f]
                        act.activation(stage[:, ks[0]:ks[-1] + 1],
                                       (turn_ps + inv_ps)[f][:, 0:len(ks) * ni].rearrange(
                                           "p (k a n) -> p k a n", k=len(ks), a=nq),
                                       ACT.Copy, scale=MIX_SCALE).then_inc(s["mix_act"], 1)

            def half_high(i, f, P=P):
                if f == 0:
                    act.wait_ge(s["conv_done"], 8 * (P * nq + i))
                act.wait_ge(s["inv_half_ps"], D_FILLS * ((P - 1) * nq + i) + f + 1)
                act.activation(half_view(0, f), inv_ps[f % 2][0:SK * QI, :].rearrange(
                    "p (e o w) -> p e o w", e=2, o=4), ACT.Copy).then_inc(s["inv_half_high"], 1)

            def square(g, t):
                act.wait_ge(s["dev_ready"], 8 * g + t + 1)
                if t >= SQ or not (isinstance(g, int) and g == 0):
                    act.wait_ge(s["var_added"], 8 * g + t + 1 - SQ)
                act.activation(squares[:, (t % SQ) * CHUNK:(t % SQ + 1) * CHUNK],
                               dev[:, t * CHUNK:(t + 1) * CHUNK], ACT.Square
                               ).then_inc(s["square_ready"], 1)

            def gelu_high(i, t, P=P):
                g = P * nq + i
                act.wait_ge(s["normed"], 8 * g + t + 1)
                chunk = dev[:, t * CHUNK:(t + 1) * CHUNK]
                act.activation(chunk, chunk, ACT.Gelu if 1 <= P < LAYERS else ACT.Identity,
                               bias=shift[:, P:P + 1], scale=gain[:, P:P + 1]
                               ).then_inc(s["gelu_done"], 1)
                if P == LAYERS and has(i, 1):
                    if t == 0:
                        act.wait_ge(s["fc1_done"], 32 * i)
                elif P > 0 or has(i, 1):
                    if t == 0:
                        act.wait_ge(s["turned_low"], T_FILLS * g)
                    if t % 2 == 0:
                        act.wait_ge(s[f"h_stored{t // 2}"], 16 * g)
                    if t == 0 and not has(i, 1):
                        act.wait_ge(s["mix_done"], 4 * P * KY)
                act.wait_ge(s["gelu_done"], 8 * g + t + 1)
                act.activation(h_next16[:, t * CHUNK:(t + 1) * CHUNK], chunk, ACT.Copy
                               ).then_inc(s["h_high"], 1)

            def turn_high(i, f, P=P):
                g = P * nq + i
                if f == 0 and (P > 0 or has(i, 1)):
                    act.wait_ge(s["fy_done"], A_FILLS * g)
                act.wait_ge(s["turned_high"], T_FILLS * g + f + 1)
                act.activation(rows_view(0, f), turn_ps[0][:].bitcast(F16).rearrange(
                    "p (w a c) -> p w a c", w=4, a=2), ACT.Copy).then_inc(s["turn_act"], 1)

            def spec_y_high(i, f, P=P):
                g = P * nq + i
                if f == 0 and (P > 0 or has(i, 1)):
                    act.wait_ge(s["fw_done"], B_FILLS * g)
                act.wait_ge(s["fy_done"], A_FILLS * g + f + 1)
                act.activation(spec_y_view(0, f), turn_ps[f % 2][:, 0:8 * 2 * SK].rearrange(
                    "p (c e k) -> p c e k", c=8, k=KX), ACT.Copy).then_inc(s["fy_high"], 1)

            def sign_prep(n, v):
                if v == 0:
                    act.wait_ge(s["prep_step"], PREP_STEPS * n + 7)
                    if not (isinstance(n, int) and n == 0):
                        act.wait_ge(s["prep_stored"], 16 * n)
                src = prep_in[:].rearrange("p (t e k o) -> p t e k o", t=2, e=2, k=KX)[:, (0, 1, 1, 0)[v]]
                outs = (prep_out[:].rearrange("p (k v o) -> p v k o", k=KX, v=4),
                        prep_tmp[:].rearrange("p (v k o) -> p v k o", v=4, k=KX))
                for e in range(2):
                    act.activation(outs[e][:, v], src[:, e], ACT.Copy, scale=sign[:, 2 * v + e:2 * v + e + 1]
                                   ).then_inc(s["prep_term" if e == 0 else "prep_signed"], 1)

            def prologue(P=P):
                if P > 0:
                    half_high(0, 0)
                    half_high(0, 1)

            def steps(i, after, prep, P=P):
                for t in range(STEPS):
                    if t < NCH and has(i):
                        gelu_high(i, t)
                    if t < 2 and P > 0 and after >= 1:
                        half_high(i + 1, 2 + t)
                    if t < A_FILLS and P < LAYERS and has(i, 1):
                        spec_y_high(i - 1, t)
                    if t >= LAG and after >= 1:
                        square(P * nq + i + 1, t - LAG)
                    if t in TURN_AT and P < LAYERS and has(i):
                        turn_high(i, TURN_AT[t])
                    if prep and t >= 5 and t < 9:
                        sign_prep(P * KY + i, t - 5)

            def between(i, after, P=P):
                if P > 0 and after == 2:
                    half_high(i + 2, 0)
                    half_high(i + 2, 1)
                if P == LAYERS and has(i):
                    head(i)

            def epilogue(P=P):
                if P < LAYERS:
                    for f in range(A_FILLS):
                        spec_y_high(nq - 1, f)
                    for ky in range(preps, KY):
                        for v in range(4):
                            sign_prep(P * KY + ky, v)

            def head(i):
                begin = isinstance(i, int) and i == 0

                def gelu1(u):
                    act.wait_ge(s["fc1_done"], 32 * i + u + 1)
                    if u >= H1 or not begin:
                        act.wait_ge(*low1_signal(i, u - H1))
                    act.activation(hidden1_full[u % H1], turn_ps[u % 2][:], ACT.Gelu, bias=fc1_b[:],
                                   scale=1 / W_SCALE).then_inc(s["fc1_act"], 1)

                def gelu2(pr):
                    act.wait_ge(s["fc2_done"], 32 * i + 2 * pr + 2)
                    if pr >= H2 or not begin:
                        act.wait_ge(s["low2"], 16 * i + pr + 1 - H2)
                    act.activation(hidden2_full[pr % H2], inv_ps[pr % 2][:], ACT.Gelu, bias=fc2_b[:],
                                   scale=1 / W_SCALE).then_inc(s["fc2_act"], 1)

                for u in range(HEAD_STEPS):
                    if u < 32:
                        gelu1(u)
                    if 5 <= u < 37 and u % 2 == 1:
                        gelu2((u - 5) // 2)

            preps = min(KY, nq - 2) if P < LAYERS else 0
            pipeline(act, P, steps, between, prologue, epilogue, preps)

    def dve_program(dve):
        dve.wait_ge(s["consts_in"], N_CONST)
        dve.tensor_copy(ident_b[:], ident[:]).then_inc(s["consts_ready"], 1)
        dve.tensor_copy(spread_sel[:], raw["spread_sel"]).then_inc(s["consts_ready"], 1)
        for n, w in enumerate((raw["conv_w"], raw["fc0_w"])):
            wv = w.rearrange("p (b o) -> p b o", o=CH)
            rows_, blocks = wv.shape[0], wv.shape[1]
            sums = col_sum[0:rows_, 0:blocks]
            if n > 0:
                dve.wait_ge(s["consts_ready"], 3)
            dve.tensor_reduce(sums, wv, AX.X, ALU.add).then_inc(s["fold_step"], 1)
            dve.wait_ge(s["fold_step"], 2 * n + 1)
            dve.tensor_scalar(sums, sums, 1.0 / CH, None, ALU.mult).then_inc(s["fold_step"], 1)
            dve.wait_ge(s["fold_step"], 2 * n + 2)
            dve.tensor_tensor(wv, wv, sums.unsqueeze(2).to_broadcast([rows_, blocks, CH]), ALU.subtract
                              ).then_inc(s["consts_ready"], 1)
        dve.wait_ge(s["consts_ready"], 4)
        for n, (w, name) in enumerate(((conv_w[:], "conv_w"), (fc1_w[:], "fc1_w"), (fc2_w[:], "fc2_w"),
                                       (fc3_sel[:], "fc3_sel"), (fc0_w, "fc0_w"))):
            half = w.shape[1] // 2
            dve.tensor_scalar(w[:, 0:half], raw[name], W_SCALE, None, ALU.mult
                              ).then_inc(s["consts_ready"], 1)
            dve.wait_ge(s["consts_ready"], 5 + 2 * n)
            dve.scalar_tensor_tensor(out=w[:, half:], in0=raw[name], scalar=W_SCALE, in1=w[:, 0:half],
                                     op0=ALU.mult, op1=ALU.subtract).then_inc(s["consts_ready"], 1)
            dve.wait_ge(s["consts_ready"], 6 + 2 * n)
        dve.wait_ge(s["bias_ps"], 1)
        dve.tensor_copy(bias[:], logit_ps[:, 0:LAYERS + 1]).then_inc(s["consts_ready"], 1)
        dve.wait_ge(s["consts_ready"], CONST_STEPS)
        for P in range(LAYERS + 1):
            if P > 0:
                dve.wait_ge(s["gelu_done"], 8 * P * nq)
                for ky in range(KY):
                    n = (P - 1) * KY + ky
                    stage = v_stage[ky % 2].rearrange("p (a k n) -> p k a n", a=nq, k=KX)
                    if ky >= 2:
                        dve.wait_ge(s[f"spec_stored{ky % 2}"], 64 * (n // 2))
                    for f in (1, 3):
                        dve.wait_ge(s["mix_done"], 4 * n + f + 1)
                        ks = MIX_SETS[f]
                        dve.tensor_scalar(stage[:, ks[0]:ks[-1] + 1],
                                          (turn_ps + inv_ps)[f][:, 0:len(ks) * ni].rearrange(
                                              "p (k a n) -> p k a n", k=len(ks), a=nq),
                                          MIX_SCALE, None, ALU.mult).then_inc(s["mix_dve"], 1)

            def inverse_root(g, start):
                st = s["rstd_step"]
                b = 15 * g

                def step(ins, k):
                    ins.then_inc(st, 1)
                    dve.wait_ge(st, b + k)

                dve.wait_ge(s["var_added"], 8 * (g + 1))
                step(dve.tensor_scalar(var_eps[:], var_ps[:, 0:128], EPS, None, ALU.add), 1)
                step(dve.tensor_scalar(seed[:], var_eps[:].bitcast(mybir.dt.int32), 1, None,
                                       ALU.logical_shift_right), 2)
                step(dve.tensor_scalar(rstd[:].bitcast(mybir.dt.int32), seed[:], -1.0, float(0x5F3759DF),
                                       ALU.mult, ALU.add), 3)
                for n in range(3):
                    step(dve.tensor_tensor(newton[:], rstd[:], rstd[:], ALU.mult), 4 + 3 * n)
                    step(dve.scalar_tensor_tensor(out=newton[:], in0=newton[:], scalar=-0.5,
                                                  in1=var_eps[:], op0=ALU.mult, op1=ALU.mult), 5 + 3 * n)
                    step(dve.scalar_tensor_tensor(out=rstd[:], in0=newton[:], scalar=1.5,
                                                  in1=rstd[:], op0=ALU.add, op1=ALU.mult), 6 + 3 * n)
                sv = split[:].rearrange("p (j a c) -> p a j c", j=4, a=3)
                rv = rstd[:].rearrange("p (j c) -> p j c", j=4)
                ev = rest[:].rearrange("p (j c) -> p j c", j=4)
                if not start:
                    dve.wait_ge(s["parts_turned"], g)
                step(dve.tensor_copy(sv[:, 0], rv), 13)
                step(dve.tensor_tensor(ev, rv, sv[:, 0], ALU.subtract), 14)
                step(dve.tensor_copy(sv[:, 1], ev), 15)
                dve.tensor_tensor(sv[:, 2], ev, sv[:, 1], ALU.subtract).then_inc(s["split_ready"], 1)

            def half_low(i, f, P=P):
                dve.wait_ge(s["inv_half_high"], D_FILLS * ((P - 1) * nq + i) + f + 1)
                dve.tensor_tensor(half_view(1, f), inv_ps[f % 2][0:SK * QI, :].rearrange(
                    "p (e o w) -> p e o w", e=2, o=4), half_view(0, f), ALU.subtract
                                  ).then_inc(s["inv_half"], 1)

            def deviation(i, t, P=P):
                g = P * nq + i
                dve.wait_ge(s["conv_done"], 8 * g + t + 1)
                if P > 0 or has(i, 1):
                    dve.wait_ge(s["h_ready"], 8 * g - 7 + t)
                dve.tensor_scalar(dev[:, t * CHUNK:(t + 1) * CHUNK], conv_ps[t % 2][:],
                                  1 / W_SCALE, bias[:, P:P + 1], ALU.mult, ALU.add
                                  ).then_inc(s["dev_ready"], 1)

            def normalize(i, t, P=P):
                dve.wait_ge(s["spread_done"], 8 * (P * nq + i) + t + 1)
                d = dev[:, t * CHUNK:(t + 1) * CHUNK]
                dve.tensor_tensor(d, d, spread_ps[:], ALU.mult).then_inc(s["normed"], 1)

            def turn_low(i, f, P=P):
                g = P * nq + i
                if f == 0 and (P > 0 or has(i, 1)):
                    dve.wait_ge(s["fy_done"], A_FILLS * g)
                dve.wait_ge(s["turned_low"], T_FILLS * g + f + 1)
                dve.tensor_copy(rows_view(1, f), turn_ps[1][:].bitcast(F16).rearrange(
                    "p (w a c) -> p w a c", w=4, a=2)).then_inc(s["turn_dve"], 1)

            def spec_y_low(i, f, P=P):
                dve.wait_ge(s["fy_high"], A_FILLS * (P * nq + i) + f + 1)
                dve.tensor_tensor(spec_y_view(1, f), turn_ps[f % 2][:, 0:8 * 2 * SK].rearrange(
                    "p (c e k) -> p c e k", c=8, k=KX), spec_y_view(0, f), ALU.subtract
                                  ).then_inc(s["fy_taken"], 1)

            def take_parts(i, P=P):
                g = P * nq + i
                dve.wait_ge(s["parts_turned"], g + 1)
                if P > 0 or has(i, 1):
                    dve.wait_ge(s["spread_done"], 8 * g)
                dve.tensor_copy(parts[:], var_ps[0:96, :]).then_inc(s["parts_ready"], 1)

            def take_spectra(i, P=P):
                sv = spec[:].rearrange("p (q k a m e) -> p k m q a e", q=KY, k=KX, a=nq, m=2)
                for f, ks in enumerate(B_SETS):
                    dve.wait_ge(s["fw_done"], B_FILLS * (P * nq + i) + f + 1)
                    pv = inv_ps[f][:, 0:len(ks) * 2 * RK].rearrange(
                        "p (k m r q) -> p k m r q", m=2, r=2, q=KY)
                    for e in range(2):
                        for r in range(2):
                            cp = dve.tensor_copy(
                                sv[64 * r:64 * r + 64, ks[0]:ks[-1] + 1, :, :, i, e],
                                pv[64 * e:64 * e + 64, :, :, r, :])
                    cp.then_inc(s["fw_taken"], 1)

            def prologue(P=P):
                if P > 0:
                    dve.wait_ge(s["spec_stored0"], 32 * KY * P)
                    dve.wait_ge(s["spec_stored1"], 32 * KY * P)
                    half_low(0, 0)
                    half_low(0, 1)

            def steps(i, after, prep, P=P):
                for t in range(STEPS):
                    if t < NCH and has(i):
                        normalize(i, t)
                    if 1 <= t < 3 and P > 0 and after >= 1:
                        half_low(i + 1, 1 + t)
                    if 1 <= t <= A_FILLS and P < LAYERS and has(i, 1):
                        spec_y_low(i - 1, t - 1)
                    if t >= LAG and after >= 1:
                        deviation(i + 1, t - LAG)
                    if t in TURN_AT and P < LAYERS and has(i):
                        turn_low(i, TURN_AT[t])
                    if t == A_FILLS + 2 and P < LAYERS and has(i, 1):
                        take_spectra(i - 1)

            def between(i, after, P=P):
                g = P * nq + i
                if after >= 1:
                    inverse_root(g + 1, P == 0 and not has(i))
                if P > 0 and after == 2:
                    half_low(i + 2, 0)
                    half_low(i + 2, 1)
                if P == LAYERS and has(i):
                    head(i, after)
                elif after >= 1:
                    take_parts(i + 1)

            def epilogue(P=P):
                if P < LAYERS:
                    for f in range(A_FILLS):
                        spec_y_low(nq - 1, f)
                    take_spectra(nq - 1)

            def head(i, after):
                begin = isinstance(i, int) and i == 0

                def high1(u):
                    dve.wait_ge(s["fc1_act"], 32 * i + u + 1)
                    if u >= H1 or not begin:
                        dve.wait_ge(s["fc2_done"], 32 * i + u + 1 - H1)
                    dve.tensor_copy(hidden1[u % H1][0], hidden1_full[u % H1]).then_inc(s["high1"], 1)
                    if u % H1 == H1 - 1:
                        dve.wait_ge(s["high1"], 32 * i + u + 1)
                        dve.tensor_tensor(hidden1[u % H1][1], hidden1_full[u % H1], hidden1[u % H1][0],
                                          ALU.subtract).then_inc(s["low1_dve"], 1)

                def high2(pr):
                    dve.wait_ge(s["fc2_act"], 16 * i + pr + 1)
                    if pr >= H2 or not begin:
                        dve.wait_ge(s["fc3_done"], 16 * i + pr + 1 - H2)
                    dve.tensor_copy(hidden2[pr % H2][0], hidden2_full[pr % H2]).then_inc(s["high2"], 1)
                    dve.wait_ge(s["high2"], 16 * i + pr + 1)
                    dve.tensor_tensor(hidden2[pr % H2][1], hidden2_full[pr % H2], hidden2[pr % H2][0],
                                      ALU.subtract).then_inc(s["low2"], 1)

                for u in range(HEAD_STEPS):
                    if u < 32:
                        high1(u)
                    if 6 <= u < 38 and u % 2 == 0:
                        high2((u - 6) // 2)
                    if u == ROOT_STEP and after >= 1:
                        take_parts(i + 1)
                dve.wait_ge(s["fc3_done"], 16 * (i + 1))
                if not (isinstance(i, int) and i == 0):
                    dve.wait_ge(s["tok_turned"], i)
                dve.tensor_scalar(logits[0:32, :], logit_ps[0:32, :], 1 / W_SCALE, fc3_b[:], ALU.mult, ALU.add
                                  ).then_inc(s["logit_taken"], 1)
                dve.wait_ge(s["tok_turned"], i + 1)
                if not (isinstance(i, int) and i == 0):
                    dve.wait_ge(s["tok_stored"], 32 * i)
                dve.tensor_copy(tok_rows.rearrange("p (a t j q) -> p a j t q", a=2, t=NCH, j=2),
                                turn_ps[0][:].rearrange("p (a j u) -> p a j u", a=2, j=2)[:, :, :, 0:32].rearrange(
                                    "p a j (t q) -> p a j t q", q=WQ)
                                ).then_inc(s["tok_ready"], 1)

            if P == LAYERS:
                dve.wait_ge(s["mix_done"], 4 * P * KY)
                dve.memset(logits, 0.0).then_inc(s["logits_zero"], 1)
                dve.wait_ge(s["logits_zero"], 1)
            pipeline(dve, P, steps, between, prologue, epilogue)

    def pool_program(pool):
        def step(ins, value):
            ins.then_inc(s["prep_step"], 1)
            pool.wait_ge(s["prep_step"], value)

        pool.wait_ge(s["consts_ready"], CONST_STEPS)
        def prep_piece(n, piece):
            first = isinstance(n, int) and n == 0
            b = PREP_STEPS * n
            v3 = prep_in[:].rearrange("p (m o) -> p m o", o=CH)
            fold = prep_fold[:].rearrange("p (m o) -> p m o", o=CH // 2)
            if piece == 0:
                pool.wait_ge(s["prep_loaded"], 128 * (n + 1))
                step(pool.tensor_tensor(fold, v3[:, :, 0:16], v3[:, :, 16:32], ALU.add), b + 1)
            elif piece == 1:
                for n_, w in enumerate((8, 4, 2, 1)):
                    step(pool.tensor_tensor(fold[:, :, 0:w], fold[:, :, 0:w], fold[:, :, w:2 * w], ALU.add),
                         b + 2 + n_)
                step(pool.tensor_tensor(fold[:, :, 0:1], fold[:, :, 0:1],
                                        sign[:, 8:9].unsqueeze(2).to_broadcast([128, 4 * KX, 1]),
                                        ALU.mult), b + 6)
            elif piece == 2:
                step(pool.tensor_tensor(v3, v3, fold[:, :, 0:1].to_broadcast([128, 4 * KX, CH]),
                                        ALU.subtract), b + 7)
            else:
                v = piece - 3
                pool.wait_ge(s["prep_signed"], 4 * n + v + 1)
                ov = prep_out[:].rearrange("p (k v o) -> p k v o", k=KX, v=4)
                tv = prep_tmp[:].rearrange("p (v k o) -> p v k o", v=4, k=KX)
                step(pool.tensor_tensor(ov[:, :, v, :], ov[:, :, v, :], tv[:, v], ALU.add), b + 8 + v)

        for P in range(LAYERS + 1):
            def split_mixed(i, P=P):
                gd = (P - 1) * nq + i
                pool.wait_ge(s["mixed_loaded"], 16 * (gd + 1))
                if P > 1 or not isinstance(i, int) or i > 0:
                    pool.wait_ge(s["inv_half_ps"], D_FILLS * gd)
                pool.tensor_tensor(mixed[:, 0:VCOLS], mixed_in[:], sign[0:96, 9:10].to_broadcast([96, VCOLS]),
                                   ALU.mult).then_inc(s["mixed_high"], 1)
                pool.wait_ge(s["mixed_high"], gd + 1)
                pool.tensor_tensor(mixed[:, VCOLS:], mixed_in[:], mixed[:, 0:VCOLS], ALU.subtract
                                   ).then_inc(s["mixed_split"], 1)

            def low_h(i, t, P=P):
                pool.wait_ge(s["h_high"], 8 * (P * nq + i) + t + 1)
                pool.tensor_tensor(h_next16[:, QCOLS + t * CHUNK:QCOLS + (t + 1) * CHUNK],
                                   dev[:, t * CHUNK:(t + 1) * CHUNK],
                                   h_next16[:, t * CHUNK:(t + 1) * CHUNK], ALU.subtract
                                   ).then_inc(s["h_ready"], 1)

            def head(i):
                for u in range(32):
                    if u % H1 < H1 - 1:
                        pool.wait_ge(s["high1"], 32 * i + u + 1)
                        pool.tensor_tensor(hidden1[u % H1][1], hidden1_full[u % H1], hidden1[u % H1][0],
                                           ALU.subtract).then_inc(s["low1"], 1)

            def store_tokens(i):
                pool.wait_ge(s["tok_ready"], i + 1)
                for e in range(2):
                    pool.dma_start(tok[i, e], tok_rows[64 * e:64 * e + 64, :].rearrange(
                        "p (a w) -> p a w", a=2)).then_inc(s["tok_stored"], 16)

            def split_x(i):
                pool.wait_ge(s["x_loaded"], 16 * (i + 1))
                if has(i, 1):
                    pool.wait_ge(s["conv_done"], 8 * i)
                pool.tensor_tensor(x16[:, 0:CHUNK], x_in, sign[0:XROWS, 9:10].to_broadcast([XROWS, CHUNK]),
                                   ALU.mult).then_inc(s["x_high"], 1)
                pool.wait_ge(s["x_high"], i + 1)
                pool.tensor_tensor(x16[:, CHUNK:2 * CHUNK], x_in, x16[:, 0:CHUNK], ALU.subtract
                                   ).then_inc(s["x_split"], 1)

            def prologue(P=P):
                if P == 0:
                    split_x(0)
                else:
                    split_mixed(0)
                    split_mixed(1)

            def steps(i, after, prep, P=P):
                if has(i):
                    for t in range(NCH):
                        low_h(i, t)
                        if prep and t != 3:
                            prep_piece(P * KY + i, t if t < 3 else t - 1)
                    if P > 0 and after == 2:
                        split_mixed(i + 2)
                if P == 0 and after == 2:
                    split_x(i + 2)

            def between(i, after, P=P):
                if P == LAYERS and has(i):
                    head(i)
                    store_tokens(i)

            def epilogue(P=P):
                if P < LAYERS:
                    for ky in range(preps, KY):
                        for piece in range(7):
                            prep_piece(P * KY + ky, piece)

            preps = min(KY, nq - 2) if P < LAYERS else 0
            pipeline(pool, P, steps, between, prologue, epilogue, preps)

    return s, sp_program, pe_program, act_program, dve_program, pool_program



D = 64
SEQ = SIDE + 1
HEADS, HD = 8, 8
WIN = 64
EXPERTS = 8
HID = 128
LHEADS, LHD, MEM = 4, 32, 4
KEYS = SEQ + MEM


def tail_constants():
    c = {}
    c["head_rows"] = np.kron(np.eye(HEADS), np.ones((HD, 1)))
    c["pair_mask"] = np.kron(np.eye(2), np.ones((WIN, HD))).reshape(2 * WIN, 1, 2 * HD) * np.ones((1, 4, 1))
    c["context_mask"] = np.kron(np.eye(LHEADS), np.ones((LHD, LHD))) * LHD ** -0.5
    c["mem_ident"] = np.broadcast_to(np.eye(MEM)[:, None, :], (MEM, 128, MEM))
    c["expert_no"] = np.broadcast_to(np.arange(EXPERTS), (128, EXPERTS))
    return {k: np.ascontiguousarray(np.asarray(v, np.float32).reshape(v.shape[0], -1)) for k, v in c.items()}


def token_transformer(nc, io, bank, sem, sb, tower_done, tokens, out):
    NIMG = tokens.shape[0] // SEQ
    NTOK = NIMG * SEQ
    NT = NTOK // 128
    XC = NT * D
    assert NT * 128 == NTOK and NIMG == 128

    h = sb("tok_h", [128, XC], F32)
    x = sb("tok_x", [128, XC], F32)
    area = [sb(f"area{n}", [128, NTOK + (NIMG * MEM if n == 0 else 0)], F32) for n in range(4)]
    y, y_last = area[3][:, 0:XC], area[0][:, 0:XC]
    stat = sb("stat", [128, 6 * NT], F32)
    seed = sb("tok_seed", [128, NT], mybir.dt.int32)
    small = sb("small", [128, 6 * NT * EXPERTS], F32)
    keys_ex = sb("keys_ex", [128, 2 * 512], F32)
    work = sb("work", [128, 2 * 512], F32)
    wide = sb("wide", [128, 2 * 512], F32)
    narrow = sb("narrow", [128, 4 * 128], F32)
    sums = sb("sums", [128, 2 * 32], F32)

    shapes = {k: io[k].shape for k in (
        "head_rows pair_mask context_mask mem_ident expert_no ident a_wq a_wk a_wv a_wproj a_bproj a_rel "
        "a_rel1 b_gamma b_beta b_wr b_br b_w1 b_b1 b_w2 b_b2 c_wq c_wk c_wv c_wout c_bout c_gout c_gpre "
        "d_w1 d_b1 d_wg d_bg d_wd d_bd").split()}
    groups = {"all": "ident expert_no", "a": "head_rows pair_mask a_wq a_wk a_wv a_wproj a_bproj a_rel a_rel1",
              "b": "b_gamma b_beta b_wr b_br b_w1 b_b1 b_w2 b_b2",
              "c": "context_mask c_wq c_wk c_wv c_wout c_bout c_gout c_gpre",
              "d": "d_w1 d_b1 d_wg d_bg d_wd d_bd"}
    groups = {g: v.split() for g, v in groups.items()}
    W = {}
    size = {g: sum(int(np.prod(shapes[k][1:])) for k in v) for g, v in groups.items()}
    w_all = sb("w_all", [128, size["all"]], F32)
    w_stage = sb("w_stage", [128, max(size[g] for g in "abcd")], F32)
    for g, v in groups.items():
        at = 0
        for k in v:
            n = int(np.prod(shapes[k][1:]))
            W[k] = (w_all if g == "all" else w_stage)[0:shapes[k][0], at:at + n]
            at += n
    ones_row = sb("ones_row", [1, 128], F32)
    ident = W["ident"]

    s = {n: sem("t_" + n) for n in (
        "in weights step x_ready ones turned turn_dve turn_act "
        "qk_ps qk_dve qk_act keys_ready scores_ps logits_ready probs_ready probs_turned probs_back v_ps v_ready "
        "mixed_ps mixed_norm mixed_turned mixed_back proj_ps proj_taken one_ps one_step one_prod one_p one_exp "
        "route_ps route_done hid_ps hid_act y_ps y_taken "
        "aug_ready kk_ps kk_max kk_exp kk_norm kk_turned kk_back vv_ps vv_back ctx_ps ctx_ready "
        "q_ps q_max q_exp q_ready q_turned q_back lin_ps lin_back w_ps w_taken "
        "stage_done out_done").split()}

    def t3(ap, n=D):
        return ap.rearrange("p (t d) -> p t d", d=n)

    hv, xv, yv = t3(h[:]), t3(x[:]), t3(y)
    wide_row = lambda ap, n: ap.unsqueeze(1).to_broadcast([128, n, ap.shape[1]])
    N_STAGE = {g: len(v) for g, v in groups.items()}
    w_count, at = {}, 0
    for g in ("all", "a", "b", "c", "d"):
        at += N_STAGE[g] + (1 if g == "c" else 0)
        w_count[g] = 16 * at
    TURNS = [("dve", "act")[f % 2] for f in range(-(-NT // 4))]

    def sp_program(sp):
        tower_done(sp)
        sp.dma_start(hv, tokens.rearrange("(t p) d -> p t d", p=128)).then_inc(s["in"], 16)
        for n, g in enumerate(("all", "a", "b", "c", "d")):
            if n >= 2:
                sp.wait_ge(s["stage_done"], n - 1)
            for k in groups[g]:
                sp.dma_start(W[k], io[k]).then_inc(s["weights"], 16)
            if g == "c":
                sp.wait_ge(s["aug_ready"], 1)
                sp.dma_start(area[0][64:64 + MEM, :].rearrange("p (b n) -> p b n", n=KEYS)[:, :, SEQ:],
                             io["mem_ident"].rearrange("p (b n) -> p b n", n=MEM)).then_inc(s["weights"], 16)
        sp.wait_ge(s["stage_done"], 4)
        sp.dma_start(out, hv).then_inc(s["out_done"], 16)
        sp.wait_ge(s["out_done"], 16)


    def turn_pe(pe, stage):
        pe.wait_ge(s["x_ready"], stage + 1)
        for f in range(len(TURNS)):
            n = stage * len(TURNS) + f
            if n >= 2:
                pe.wait_ge(s["turn_" + ("dve", "act")[f % 2]], prior(stage, f))
            for t in range(4 * f, min(4 * f + 4, NT)):
                mm = nc.tensor.transpose(bank[f % 2][0:D, (t % 4) * 128:(t % 4 + 1) * 128], xv[:, t, :], ident)
            mm.then_inc(s["turned"], 1)

    nd, na = TURNS.count("dve"), TURNS.count("act")

    def prior(stage, f):
        return stage * (nd if f % 2 == 0 else na) + f // 2

    def turn_back(eng, copy, stage, parity):
        for f in range(parity, len(TURNS), 2):
            eng.wait_ge(s["turned"], stage * len(TURNS) + f + 1)
            n = min(4, NT - 4 * f) * 128
            copy(area[1][0:D, f * 512:f * 512 + n], bank[f % 2][0:D, 0:n]).then_inc(
                s["turn_" + ("dve", "act")[parity]], 1)

    def turned(eng, stage):
        eng.wait_ge(s["turn_dve"], nd * (stage + 1))
        eng.wait_ge(s["turn_act"], na * (stage + 1))

    a_copy = lambda o, i: nc.scalar.activation(o, i, ACT.Copy)
    v_copy = lambda o, i: nc.vector.tensor_copy(o, i)

    NP = NIMG // 2
    xT = area[1]
    qT, kT, oT = area[2], area[3], area[0]
    xw = xT[0:D, :].rearrange("p (b n) -> p b n", n=SEQ)
    ow = oT[0:D, 0:NTOK].rearrange("p (b n) -> p b n", n=SEQ)
    CHUNKS = [(f * 4, min(4, NT - f * 4)) for f in range(len(TURNS))]
    NG = -(-NT // 8)
    KI = 4
    NK = NIMG // KI

    def pe_program(pe):
        pe.wait_ge(s["weights"], w_count["a"])
        turn_pe(pe, 0)
        turned(pe, 0)
        for n in range(2 * NIMG // 8):
            c, which = divmod(n, 2)
            if n >= 2:
                pe.wait_ge(s["qk_dve" if which == 0 else "qk_act"], c)
            nc.tensor.matmul(bank[2 + which][0:D, :], W["a_wq" if which == 0 else "a_wk"],
                             xw[:, 8 * c:8 * c + 8, 0:WIN], start=True, stop=True).then_inc(s["qk_ps"], 1)
        pe.wait_ge(s["qk_dve"], NIMG // 8)
        pe.wait_ge(s["qk_act"], NIMG // 8)

        def scores(n):
            pe.wait_ge(s["keys_ready"], 2 * n + 2)
            if n >= 2:
                pe.wait_ge(s["logits_ready"], 1 * (n - 1))
            for e in range(2):
                b = 2 * n + e
                mm = nc.tensor.matmul(bank[n % 2][64 * e:64 * e + 64, :], qT[0:D, b * WIN:(b + 1) * WIN],
                                      keys_ex[0:D, e * 512:(e + 1) * 512], start=True, stop=True)
            mm.then_inc(s["scores_ps"], 1)

        def values(n):
            if n >= 1:
                pe.wait_ge(s["v_ready"], n)
            for e in range(2):
                for half in range(2):
                    mm = nc.tensor.matmul(bank[4][64 * half:64 * half + 64, e * D:(e + 1) * D],
                                          xw[:, 2 * n + e, 0:WIN], W["a_wv"], start=True, stop=True)
            mm.then_inc(s["v_ps"], 1)

        def mix(n):
            pe.wait_ge(s["probs_ready"], n + 1)
            if n >= 1:
                pe.wait_ge(s["probs_back"], n)
            for hp in range(4):
                mm = nc.tensor.transpose(bank[5][:, hp * 128:(hp + 1) * 128],
                                         wide[:, (n % 2) * 512 + hp * 128:(n % 2) * 512 + (hp + 1) * 128], ident)
            mm.then_inc(s["probs_turned"], 1)

        def apply(n):
            pe.wait_ge(s["probs_back"], n + 1)
            pe.wait_ge(s["v_ready"], n + 1)
            if n >= 1:
                pe.wait_ge(s["mixed_norm"], n)
            for e in range(2):
                for hp in range(4):
                    mm = nc.tensor.matmul(bank[6][64 * e:64 * e + 64, hp * 16:(hp + 1) * 16],
                                          work[:, hp * 128 + 64 * e:hp * 128 + 64 * e + 64],
                                          narrow[:, e * D + hp * 16:e * D + (hp + 1) * 16],
                                          start=True, stop=True)
            mm.then_inc(s["mixed_ps"], 1)

        def turn_mixed(n):
            pe.wait_ge(s["mixed_norm"], n + 1)
            if n >= 1:
                pe.wait_ge(s["mixed_back"], n)
            nc.tensor.transpose(bank[7][0:D, 0:128], narrow[:, 2 * D + (n % 2) * D:2 * D + (n % 2 + 1) * D],
                                ident).then_inc(s["mixed_turned"], 1)

        for n in range(NP + 2):
            if n < NP:
                scores(n)
                values(n)
            if 1 <= n <= NP:
                mix(n - 1)
                apply(n - 1)
            if n >= 2:
                turn_mixed(n - 2)
        last = xw[:, :, WIN]
        nc.tensor.matmul(bank[2][0:D, 0:128], W["a_wq"], last, start=True, stop=True)
        nc.tensor.matmul(bank[2][0:D, 128:256], W["a_wk"], last, start=True, stop=True)
        nc.tensor.matmul(bank[2][:, 256:256 + D], last, W["a_wv"], start=True, stop=True).then_inc(s["one_ps"], 1)
        pe.wait_ge(s["one_prod"], 1)
        nc.tensor.matmul(bank[3][:, 0:HEADS], work[0:D, 256:384], W["head_rows"], start=True, stop=True
                         ).then_inc(s["one_ps"], 1)
        pe.wait_ge(s["one_p"], 1)
        nc.tensor.transpose(bank[3][0:D, 128:256], work[:, 384:384 + D], ident).then_inc(s["one_ps"], 1)
        pe.wait_ge(s["one_p"], 2)
        pe.wait_ge(s["mixed_back"], NP)
        for g in range(NG):
            if g >= 2:
                pe.wait_ge(s["proj_taken"], g - 1)
            for t in range(8 * g, min(8 * g + 8, NT)):
                mm = nc.tensor.matmul(bank[g % 2][:, (t % 8) * D:(t % 8 + 1) * D],
                                      oT[0:D, t * 128:(t + 1) * 128], W["a_wproj"], start=True, stop=True)
            mm.then_inc(s["proj_ps"], 1)
        pe.wait_ge(s["proj_taken"], NG)

        pe.wait_ge(s["weights"], w_count["b"])
        turn_pe(pe, 1)
        turned(pe, 1)
        for t in range(NT):
            mm = nc.tensor.matmul(bank[2 + t // 64][:, (t % 64) * 8:(t % 64 + 1) * 8],
                                  xT[0:D, t * 128:(t + 1) * 128], W["b_wr"], start=True, stop=True)
        mm.then_inc(s["route_ps"], 1)
        pe.wait_ge(s["route_done"], 1)
        hidden_b = [wide[:, 0:512], wide[:, 512:1024]]
        units = [(c, e) for c in range(len(CHUNKS)) for e in range(EXPERTS)]

        def hid_b(u):
            c, e = units[u]
            if u >= 2:
                pe.wait_ge(s["hid_act"], u - 1)
            n = CHUNKS[c][1] * 128
            nc.tensor.matmul(bank[u % 2][:, 0:n], W["b_w1"][:, e * HID:(e + 1) * HID],
                             xT[0:D, c * 512:c * 512 + n], start=True, stop=True).then_inc(s["hid_ps"], 1)

        def out_b(u):
            c, e = units[u]
            pe.wait_ge(s["hid_act"], u + 1)
            if e == 0:
                if c >= 1:
                    pe.wait_ge(s["y_taken"], sum(k for _, k in CHUNKS[:c]))
                for j in range(CHUNKS[c][1]):
                    nc.tensor.matmul(bank[2 + j][:], ones_row[:], W["b_b2"], start=True, stop=False)
            for j in range(CHUNKS[c][1]):
                mm = nc.tensor.matmul(bank[2 + j][:, e * D:(e + 1) * D], hidden_b[u % 2][:, j * 128:(j + 1) * 128],
                                      W["b_w2"][:, e * D:(e + 1) * D], start=False, stop=(e == EXPERTS - 1))
            mm.then_inc(s["y_ps"], 1)

        for u in range(len(units) + 1):
            if u < len(units):
                hid_b(u)
            if u >= 1:
                out_b(u - 1)
        pe.wait_ge(s["y_taken"], NT)

        pe.wait_ge(s["weights"], w_count["c"])
        turn_pe(pe, 2)
        turned(pe, 2)
        q_rows(pe)
        pe.wait_ge(s["q_back"], len(CHUNKS))
        pe.wait_ge(s["aug_ready"], 2)
        aug = area[0][0:D + MEM, :]

        def keys(n):
            if n >= 1:
                pe.wait_ge(s["kk_norm"], n)
            nc.tensor.matmul(bank[0][:, 0:KI * KEYS], W["c_wk"], aug[:, n * KI * KEYS:(n + 1) * KI * KEYS],
                             start=True, stop=True).then_inc(s["kk_ps"], 1)
            if n >= 1:
                pe.wait_ge(s["vv_back"], n)
            for i in range(KI):
                b = n * KI + i
                mm = nc.tensor.matmul(bank[1][0:KEYS, i * 128:(i + 1) * 128], aug[:, b * KEYS:(b + 1) * KEYS],
                                      W["c_wv"], start=True, stop=True)
            mm.then_inc(s["vv_ps"], 1)

        def turn_keys(n):
            pe.wait_ge(s["kk_exp"], n + 1)
            if n >= 1:
                pe.wait_ge(s["kk_back"], n)
            for i in range(KI):
                mm = nc.tensor.transpose(bank[2][0:KEYS, i * 128:(i + 1) * 128],
                                         keys_ex[:, (n % 2) * 512 + i * KEYS:(n % 2) * 512 + (i + 1) * KEYS],
                                         ident)
            mm.then_inc(s["kk_turned"], 1)

        def context(n):
            pe.wait_ge(s["kk_back"], n + 1)
            if n >= 1:
                pe.wait_ge(s["ctx_ready"], n)
            for i in range(KI):
                c = (n % 2) * 512 + i * 128
                mm = nc.tensor.matmul(bank[3][:, i * 128:(i + 1) * 128], wide[0:KEYS, c:c + 128],
                                      work[0:KEYS, c:c + 128], start=True, stop=True)
            mm.then_inc(s["ctx_ps"], 1)

        def linear(n):
            pe.wait_ge(s["ctx_ready"], n + 1)
            if n >= 1:
                pe.wait_ge(s["lin_back"], n)
            for i in range(KI):
                b = n * KI + i
                mm = nc.tensor.matmul(bank[4][:, i * SEQ:(i + 1) * SEQ], narrow[:, i * 128:(i + 1) * 128],
                                      area[2][:, b * SEQ:(b + 1) * SEQ], start=True, stop=True)
            mm.then_inc(s["lin_ps"], 1)

        for n in range(NK + 2):
            if n < NK:
                keys(n)
            if 1 <= n <= NK:
                turn_keys(n - 1)
                context(n - 1)
            if n >= 2:
                linear(n - 2)
        pe.wait_ge(s["lin_back"], NK)
        for g in range(NG):
            if g >= 2:
                pe.wait_ge(s["w_taken"], g - 1)
            for t in range(8 * g, min(8 * g + 8, NT)):
                mm = nc.tensor.matmul(bank[g % 2][:, (t % 8) * D:(t % 8 + 1) * D],
                                      area[1][:, t * 128:(t + 1) * 128], W["c_wout"], start=True, stop=True)
            mm.then_inc(s["w_ps"], 1)
        pe.wait_ge(s["w_taken"], NG)

        pe.wait_ge(s["weights"], w_count["d"])
        turn_pe(pe, 3)
        turned(pe, 3)
        base = len(units)
        for u in range(2 * len(CHUNKS)):
            c, half = divmod(u, 2)
            pe.wait_ge(s["hid_act"], base + u - 1)
            n = CHUNKS[c][1] * 128
            nc.tensor.matmul(bank[u % 2][:, 0:n], W["d_w1"][:, half * HID:(half + 1) * HID],
                             xT[0:D, c * 512:c * 512 + n], start=True, stop=True).then_inc(s["hid_ps"], 1)
        pe.wait_ge(s["hid_act"], base + 2 * len(CHUNKS))
        for t in range(NT):
            for half in range(2):
                mm = nc.tensor.matmul(bank[2 + t // 64][:, (t % 64) * 8:(t % 64 + 1) * 8],
                                      area[2 + half][:, t * 128:(t + 1) * 128],
                                      W["d_wg"][:, half * 8:(half + 1) * 8],
                                      start=(half == 0), stop=(half == 1))
        mm.then_inc(s["route_ps"], 1)
        pe.wait_ge(s["route_done"], 2)
        for t in range(NT):
            if t >= 4:
                pe.wait_ge(s["y_taken"], NT + t - 3)
            nc.tensor.matmul(bank[4 + t % 4][:], ones_row[:], W["d_bd"], start=True, stop=False)
            for half in range(2):
                mm = nc.tensor.matmul(bank[4 + t % 4][:], area[2 + half][:, t * 128:(t + 1) * 128],
                                      W["d_wd"][:, half * 512:(half + 1) * 512],
                                      start=False, stop=(half == 1))
            mm.then_inc(s["y_ps"], 1)

    def q_rows(pe):
        def q_ps(f):
            if f >= 1:
                pe.wait_ge(s["q_ready"], f)
            for t in range(CHUNKS[f][0], CHUNKS[f][0] + CHUNKS[f][1]):
                mm = nc.tensor.matmul(bank[2][:, (t % 4) * 128:(t % 4 + 1) * 128],
                                      xT[0:D, t * 128:(t + 1) * 128], W["c_wq"], start=True, stop=True)
            mm.then_inc(s["q_ps"], 1)

        def q_turn(f):
            pe.wait_ge(s["q_ready"], f + 1)
            if f >= 1:
                pe.wait_ge(s["q_back"], f)
            for j in range(CHUNKS[f][1]):
                c = (f % 2) * 512 + j * 128
                mm = nc.tensor.transpose(bank[3][:, j * 128:(j + 1) * 128], wide[:, c:c + 128], ident)
            mm.then_inc(s["q_turned"], 1)

        for f in range(len(CHUNKS) + 1):
            if f < len(CHUNKS):
                q_ps(f)
            if f >= 1:
                q_turn(f - 1)

    def act_program(act):
        turn_back(act, a_copy, 0, 1)
        for c in range(NIMG // 8):
            act.wait_ge(s["qk_ps"], 2 * c + 2)
            a_copy(kT[0:D, c * 512:(c + 1) * 512], bank[3][0:D, :]).then_inc(s["qk_act"], 1)
        for n in range(NP + 2):
            if n < NP:
                act.wait_ge(s["logits_ready"], n + 1)
                if n >= 2:
                    act.wait_ge(s["probs_turned"], n - 1)
                c = slice((n % 2) * 512, (n % 2 + 1) * 512)
                nc.scalar.activation(wide[:, c], wide[:, c], ACT.Exp).then_inc(s["probs_ready"], 1)
            if 1 <= n <= NP:
                act.wait_ge(s["probs_turned"], n)
                if n >= 2:
                    act.wait_ge(s["mixed_ps"], n - 1)
                a_copy(work[:, 0:512], bank[5][:]).then_inc(s["probs_back"], 1)
            if n >= 2:
                m = n - 2
                act.wait_ge(s["mixed_turned"], m + 1)
                a_copy(ow[:, 2 * m:2 * m + 2, 0:WIN], bank[7][0:D, 0:128].rearrange("p (e n) -> p e n", e=2)
                       ).then_inc(s["mixed_back"], 1)
        act.wait_ge(s["one_step"], 1)
        nc.scalar.activation(small[:, 128:208], small[:, 0:80], ACT.Exp).then_inc(s["one_exp"], 1)
        turn_back(act, a_copy, 1, 1)
        act.wait_ge(s["step"], STEP["route_exp0"])
        nc.scalar.activation(small[:, 0:NT], small[:, 0:NT], ACT.Exp).then_inc(s["route_exp"], 1)
        hidden_b = [wide[:, 0:512], wide[:, 512:1024]]
        nu = len(CHUNKS) * EXPERTS
        for u in range(nu):
            c, e = divmod(u, EXPERTS)
            act.wait_ge(s["hid_ps"], u + 1)
            if u >= 2:
                act.wait_ge(s["y_ps"], u - 1)
            n = CHUNKS[c][1] * 128
            nc.scalar.activation(hidden_b[u % 2][:, 0:n], bank[u % 2][:, 0:n], ACT.Gelu,
                                 bias=W["b_b1"][:, e:e + 1]).then_inc(s["hid_act"], 1)
        turn_back(act, a_copy, 2, 1)
        for f in range(len(CHUNKS) + 1):
            if f < len(CHUNKS):
                n = CHUNKS[f][1] * 128
                c = (f % 2) * 512
                act.wait_ge(s["q_max"], f + 1)
                nc.scalar.activation(wide[:, c:c + n], wide[:, c:c + n], ACT.Exp).then_inc(s["q_exp"], 1)
            if f >= 1:
                n = CHUNKS[f - 1][1] * 128
                act.wait_ge(s["q_turned"], f)
                a_copy(area[2][:, (f - 1) * 512:(f - 1) * 512 + n], bank[3][:, 0:n]).then_inc(s["q_back"], 1)
        for n in range(NK + 2):
            if n < NK:
                act.wait_ge(s["vv_ps"], n + 1)
                if n >= 2:
                    act.wait_ge(s["ctx_ps"], n - 1)
                a_copy(work[0:KEYS, (n % 2) * 512:(n % 2 + 1) * 512], bank[1][0:KEYS, :]
                       ).then_inc(s["vv_back"], 1)
                act.wait_ge(s["kk_norm"], n + 1)
                c = (n % 2) * 512
                nc.scalar.activation(keys_ex[:, c:c + KI * KEYS], keys_ex[:, c:c + KI * KEYS], ACT.Exp
                                     ).then_inc(s["kk_exp"], 1)
            if 1 <= n <= NK:
                act.wait_ge(s["kk_turned"], n)
                if n >= 3:
                    act.wait_ge(s["ctx_ps"], n - 2)
                c = ((n - 1) % 2) * 512
                a_copy(wide[0:KEYS, c:c + 512], bank[2][0:KEYS, :]).then_inc(s["kk_back"], 1)
            if n >= 2:
                m = n - 2
                act.wait_ge(s["lin_ps"], m + 1)
                a_copy(area[1][:, m * KI * SEQ:(m + 1) * KI * SEQ], bank[4][:, 0:KI * SEQ]
                       ).then_inc(s["lin_back"], 1)
        turn_back(act, a_copy, 3, 1)
        for u in range(2 * len(CHUNKS)):
            c, half = divmod(u, 2)
            act.wait_ge(s["hid_ps"], nu + u + 1)
            n = CHUNKS[c][1] * 128
            nc.scalar.activation(area[2 + half][:, c * 512:c * 512 + n], bank[u % 2][:, 0:n], ACT.Gelu,
                                 bias=W["d_b1"][:, half:half + 1]).then_inc(s["hid_act"], 1)
        act.wait_ge(s["step"], STEP["gate_exp"])
        nc.scalar.activation(small[:, 0:NT * 8], small[:, 0:NT * 8], ACT.Exp).then_inc(s["route_exp"], 1)

    STEP = {}
    s["route_exp"] = sem("t_route_exp")

    V = nc.vector
    st = [stat[:, n * NT:(n + 1) * NT] for n in range(6)]

    def dve_program(dve, dry=False):
        count = [0]

        def link(f):
            count[0] += 1
            if not dry:
                f().then_inc(s["step"], 1)
                dve.wait_ge(s["step"], count[0])

        def wait(name, value):
            if not dry:
                dve.wait_ge(s[name], value)

        def do(f, name=None):
            if not dry:
                ins = f()
                if name:
                    ins.then_inc(s[name], 1)

        def bc(ap, n=D):
            return ap.unsqueeze(2).to_broadcast([128, ap.shape[1], n])

        def inverse_root(v, r):
            link(lambda: V.tensor_scalar(seed[:], v.bitcast(mybir.dt.int32), 1, None, ALU.logical_shift_right))
            link(lambda: V.tensor_scalar(r.bitcast(mybir.dt.int32), seed[:], -1.0, float(0x5F3759DF),
                                         ALU.mult, ALU.add))
            for _ in range(3):
                link(lambda: V.tensor_tensor(st[4], r, r, ALU.mult))
                link(lambda: V.scalar_tensor_tensor(out=st[4], in0=st[4], scalar=-0.5, in1=v,
                                                    op0=ALU.mult, op1=ALU.mult))
                link(lambda: V.scalar_tensor_tensor(out=r, in0=st[4], scalar=1.5, in1=r,
                                                    op0=ALU.add, op1=ALU.mult))

        def layer_norm(dst, src, spare):
            link(lambda: V.tensor_reduce(st[0], src, AX.X, ALU.add))
            link(lambda: V.tensor_scalar(st[0], st[0], 1.0 / D, None, ALU.mult))
            link(lambda: V.tensor_tensor(dst, src, bc(st[0]), ALU.subtract))
            link(lambda: V.tensor_tensor(spare, dst, dst, ALU.mult))
            link(lambda: V.tensor_reduce(st[1], spare, AX.X, ALU.add))
            link(lambda: V.tensor_scalar(st[1], st[1], 1.0 / D, EPS, ALU.mult, ALU.add))
            inverse_root(st[1], st[2])
            link(lambda: V.tensor_tensor(dst, dst, bc(st[2]), ALU.mult))

        def rms_norm(dst, src, spare, gain):
            link(lambda: V.tensor_tensor(spare, src, src, ALU.mult))
            link(lambda: V.tensor_reduce(st[1], spare, AX.X, ALU.add))
            link(lambda: V.tensor_scalar(st[1], st[1], 1e-24, None, ALU.max))
            inverse_root(st[1], st[2])
            link(lambda: V.tensor_scalar(st[2], st[2], float(D) ** 0.5, None, ALU.mult))
            link(lambda: V.tensor_tensor(dst, src, bc(st[2]), ALU.mult))
            link(lambda: V.tensor_tensor(dst, dst, wide_row(gain, NT), ALU.mult))

        wait("in", 16)
        do(lambda: V.memset(ones_row[:], 1.0), "ones")
        layer_norm(xv, hv, yv)
        do(lambda: V.engine_nop(), "x_ready")
        if not dry:
            turn_back(dve, v_copy, 0, 0)
        for c in range(NIMG // 8):
            wait("qk_ps", 2 * c + 1)
            do(lambda: v_copy(qT[0:D, c * 512:(c + 1) * 512], bank[2][0:D, :]), "qk_dve")
        wait("qk_act", NIMG // 8)
        wait("weights", w_count["a"])
        rel = W["a_rel"].unsqueeze(1).to_broadcast([128, HEADS, WIN])
        hr = W["head_rows"].unsqueeze(2).to_broadcast([D, HEADS, WIN])

        def keys(n):
            if n >= 1:
                wait("scores_ps", n)
            for e in range(2):
                b = 2 * n + e
                kb = kT[0:D, b * WIN:(b + 1) * WIN].unsqueeze(1).to_broadcast([D, HEADS, WIN])
                do(lambda: V.tensor_tensor(keys_ex[0:D, e * 512:(e + 1) * 512].rearrange(
                    "p (h k) -> p h k", h=HEADS), kb, hr, ALU.mult), "keys_ready")

        def soft(n):
            L = wide[:, (n % 2) * 512:(n % 2 + 1) * 512].rearrange("p (h k) -> p h k", h=HEADS)
            m = sums[:, (n % 2) * 32:(n % 2) * 32 + 8]
            wait("scores_ps", n + 1)
            if n >= 2:
                wait("probs_turned", n - 1)
            link(lambda: V.scalar_tensor_tensor(out=L, in0=bank[n % 2][:].rearrange("p (h k) -> p h k", h=HEADS),
                                                scalar=HD ** -0.5, in1=rel, op0=ALU.mult, op1=ALU.add))
            link(lambda: V.tensor_reduce(m, L, AX.X, ALU.max))
            do(lambda: V.tensor_tensor(L, L, bc(m, WIN), ALU.subtract), "logits_ready")

        def norm(n):
            L = wide[:, (n % 2) * 512:(n % 2 + 1) * 512].rearrange("p (h k) -> p h k", h=HEADS)
            z = sums[:, (n % 2) * 32 + 8:(n % 2) * 32 + 16]
            wait("v_ps", n + 1)
            if n >= 1:
                wait("mixed_ps", n)
            do(lambda: V.tensor_tensor(narrow[:, 0:2 * D].rearrange("p (e c) -> p e c", e=2),
                                       bank[4][:, 0:2 * D].rearrange("p (e c) -> p e c", e=2),
                                       W["pair_mask"].unsqueeze(1).to_broadcast([128, 2, D]), ALU.mult),
               "v_ready")
            wait("probs_ready", n + 1)
            link(lambda: V.tensor_reduce(z, L, AX.X, ALU.add))
            link(lambda: V.reciprocal(z, z))
            wait("mixed_ps", n + 1)
            if n >= 2:
                wait("mixed_turned", n - 1)
            o = narrow[:, 2 * D + (n % 2) * D:2 * D + (n % 2 + 1) * D]
            do(lambda: V.tensor_tensor(o.rearrange("p (h d) -> p h d", h=HEADS),
                                       bank[6][:, 0:D].rearrange("p (h d) -> p h d", h=HEADS),
                                       bc(z, HD), ALU.mult), "mixed_norm")

        for n in range(NP + 1):
            if n < NP:
                keys(n)
                soft(n)
            if n >= 1:
                norm(n - 1)
        wait("one_ps", 1)
        wait("probs_back", NP)
        link(lambda: V.tensor_copy(work[0:D, 0:128], bank[2][0:D, 0:128]))
        do(lambda: V.tensor_tensor(work[0:D, 256:384], work[0:D, 0:128], bank[2][0:D, 128:256], ALU.mult),
           "one_prod")
        lg, zk, mx, zmax = small[:, 0:8], small[:, 8:72], small[:, 72:80], small[:, 96:97]
        link(lambda: V.tensor_reduce(zmax, W["a_rel1"][:, 1:64], AX.X, ALU.max))
        link(lambda: V.tensor_tensor(zk, W["a_rel1"], zmax.to_broadcast([128, 64]), ALU.subtract))
        wait("one_ps", 2)
        link(lambda: V.tensor_scalar(lg, bank[3][:, 0:HEADS], HD ** -0.5, W["a_rel1"][:, 0:1],
                                     ALU.mult, ALU.add))
        link(lambda: V.tensor_tensor(mx, lg, zmax.to_broadcast([128, 8]), ALU.max))
        link(lambda: V.tensor_tensor(lg, lg, mx, ALU.subtract))
        link(lambda: V.tensor_tensor(mx, zmax.to_broadcast([128, 8]), mx, ALU.subtract))
        do(lambda: V.engine_nop(), "one_step")
        wait("one_exp", 1)
        p, ez, em, zs = small[:, 128:136], small[:, 137:200], small[:, 200:208], small[:, 208:209]
        z8 = small[:, 216:224]
        link(lambda: V.tensor_reduce(zs, ez, AX.X, ALU.add))
        link(lambda: V.tensor_scalar(z8, em, zs, None, ALU.mult))
        link(lambda: V.tensor_tensor(z8, z8, p, ALU.add))
        link(lambda: V.reciprocal(z8, z8))
        link(lambda: V.tensor_tensor(z8, z8, p, ALU.mult))
        do(lambda: V.tensor_tensor(work[:, 384:384 + D].rearrange("p (h d) -> p h d", h=HEADS),
                                   bank[2][:, 256:256 + D].rearrange("p (h d) -> p h d", h=HEADS),
                                   bc(z8, HD), ALU.mult), "one_p")
        wait("one_ps", 3)
        do(lambda: V.tensor_copy(ow[:, :, WIN], bank[3][0:D, 128:256]), "one_p")

        def add_rows(g, bias, target, done, ps):
            n = min(8, NT - 8 * g)
            r = target[:, 8 * g:8 * g + n]
            wait(ps, g + 1)
            link(lambda: V.tensor_tensor(r, r, t3(bank[g % 2][:, 0:n * D]), ALU.add))
            do(lambda: V.tensor_tensor(r, r, wide_row(bias, n), ALU.add), done)

        for g in range(NG):
            add_rows(g, W["a_bproj"], hv, "proj_taken", "proj_ps")
        wait("proj_taken", NG)
        do(lambda: V.engine_nop(), "stage_done")

        layer_norm(xv, hv, yv)
        layer_norm(xv, xv, yv)
        wait("weights", w_count["b"])
        link(lambda: V.tensor_tensor(xv, xv, wide_row(W["b_gamma"], NT), ALU.mult))
        link(lambda: V.tensor_tensor(xv, xv, wide_row(W["b_beta"], NT), ALU.add))
        do(lambda: V.engine_nop(), "x_ready")
        if not dry:
            turn_back(dve, v_copy, 1, 0)
        NE = NT * EXPERTS
        L, one1, one2, tmp, wgt = [small[:, n * NE:(n + 1) * NE].rearrange("p (t e) -> p t e", e=EXPERTS)
                                   for n in range(5)]
        flat = lambda v: v.rearrange("p t e -> p (t e)")
        en = wide_row(W["expert_no"], NT)

        def first_max(oh, values, m):
            link(lambda: V.tensor_reduce(m, values, AX.X, ALU.max))
            link(lambda: V.tensor_tensor(tmp, values, bc(m, EXPERTS), ALU.is_equal))
            link(lambda: V.tensor_scalar(oh, en, -float(EXPERTS), None, ALU.add))
            link(lambda: V.tensor_tensor(tmp, tmp, oh, ALU.mult))
            link(lambda: V.tensor_reduce(st[3], tmp, AX.X, ALU.min))
            link(lambda: V.tensor_tensor(oh, oh, bc(st[3], EXPERTS), ALU.is_equal))

        def route_in(bias):
            for a, b, ps in ((0, 64, bank[2]), (64, NT, bank[3])):
                link(lambda: V.tensor_tensor(L[:, a:b], t3(ps[:, 0:(b - a) * 8], 8),
                                             wide_row(bias, b - a), ALU.add))

        wait("route_ps", 1)
        route_in(W["b_br"])
        first_max(one1, L, st[0])
        link(lambda: V.scalar_tensor_tensor(out=L, in0=one1, scalar=-3.0e38, in1=L, op0=ALU.mult, op1=ALU.add))
        first_max(one2, L, st[1])
        link(lambda: V.tensor_tensor(small[:, 0:NT], st[1], st[0], ALU.subtract))
        STEP["route_exp0"] = count[0]
        wait("route_exp", 1)
        link(lambda: V.tensor_scalar(st[0], small[:, 0:NT], 1.0, None, ALU.add))
        link(lambda: V.reciprocal(st[0], st[0]))
        link(lambda: V.tensor_tensor(st[1], small[:, 0:NT], st[0], ALU.mult))
        link(lambda: V.tensor_tensor(wgt, one1, bc(st[0], EXPERTS), ALU.mult))
        link(lambda: V.tensor_tensor(tmp, one2, bc(st[1], EXPERTS), ALU.mult))
        link(lambda: V.tensor_tensor(wgt, wgt, tmp, ALU.add))
        do(lambda: V.engine_nop(), "route_done")

        def combine(t, ps, taken, yv=yv):
            w = work[:, (t % 2) * 512:(t % 2 + 1) * 512]
            do(lambda: V.tensor_tensor(t3(w), t3(ps[:]), bc(wgt[:, t], D), ALU.mult), "y_taken")
            wait("y_taken", taken)
            do(lambda: V.tensor_reduce(yv[:, t], w.rearrange("p (e d) -> p d e", e=EXPERTS), AX.X, ALU.add),
               None if t < NT - 1 else "y_sum")

        for c, (t0, k) in enumerate(CHUNKS):
            wait("y_ps", EXPERTS * (c + 1))
            for j in range(k):
                combine(t0 + j, bank[2 + j], t0 + j + 1)
        wait("y_sum", 1)
        link(lambda: V.tensor_tensor(h[:], h[:], y, ALU.add))
        do(lambda: V.engine_nop(), "stage_done")

        layer_norm(yv, hv, xv)
        wait("weights", w_count["c"] - 16)
        do(lambda: V.memset(area[0][0:D + MEM, :], 0.0), "aug_ready")
        rms_norm(xv, yv, t3(area[2][:, 0:XC]), W["c_gpre"])
        do(lambda: V.engine_nop(), "x_ready")
        if not dry:
            turn_back(dve, v_copy, 2, 0)
            turned(dve, 2)
        wait("weights", w_count["c"])
        do(lambda: V.tensor_copy(area[0][0:D, :].rearrange("p (b n) -> p b n", n=KEYS)[:, :, 0:SEQ],
                                 xw), "aug_ready")
        for f, (t0, k) in enumerate(CHUNKS):
            n = k * 128
            qv = wide[:, (f % 2) * 512:(f % 2) * 512 + n].rearrange("p (g d) -> p g d", d=LHD)
            m = sums[:, 0:4 * k]
            wait("q_ps", f + 1)
            link(lambda: V.tensor_reduce(m, bank[2][:, 0:n].rearrange("p (g d) -> p g d", d=LHD), AX.X, ALU.max))
            if f >= 2:
                wait("q_turned", f - 1)
            do(lambda: V.tensor_tensor(qv, bank[2][:, 0:n].rearrange("p (g d) -> p g d", d=LHD), bc(m, LHD),
                                       ALU.subtract), "q_max")
            wait("q_exp", f + 1)
            link(lambda: V.tensor_reduce(m, qv, AX.X, ALU.add))
            link(lambda: V.reciprocal(m, m))
            do(lambda: V.tensor_tensor(qv, qv, bc(m, LHD), ALU.mult), "q_ready")

        def key_max(n):
            kv = bank[0][:, 0:KI * KEYS].rearrange("p (i n) -> p i n", i=KI)
            dst = keys_ex[:, (n % 2) * 512:(n % 2) * 512 + KI * KEYS].rearrange("p (i n) -> p i n", i=KI)
            m = sums[:, (n % 2) * 32:(n % 2) * 32 + KI]
            wait("kk_ps", n + 1)
            link(lambda: V.tensor_reduce(m, kv, AX.X, ALU.max))
            if n >= 2:
                wait("kk_turned", n - 1)
            do(lambda: V.tensor_tensor(dst, kv, bc(m, KEYS), ALU.subtract), "kk_norm")

        def contexts(n):
            src = keys_ex[:, (n % 2) * 512:(n % 2) * 512 + KI * KEYS].rearrange("p (i n) -> p i n", i=KI)
            z = sums[:, (n % 2) * 32 + 8:(n % 2) * 32 + 8 + KI]
            wait("kk_exp", n + 1)
            link(lambda: V.tensor_reduce(z, src, AX.X, ALU.add))
            link(lambda: V.reciprocal(z, z))
            wait("ctx_ps", n + 1)
            if n >= 1:
                wait("lin_ps", n)
            for i in range(KI):
                do(lambda: V.scalar_tensor_tensor(out=narrow[:, i * 128:(i + 1) * 128],
                                                  in0=bank[3][:, i * 128:(i + 1) * 128], scalar=z[:, i:i + 1],
                                                  in1=W["context_mask"], op0=ALU.mult, op1=ALU.mult),
                   "ctx_ready" if i == KI - 1 else None)

        for n in range(NK + 1):
            if n < NK:
                key_max(n)
            if n >= 1:
                contexts(n - 1)
        wait("lin_ps", NK)
        for g in range(NG):
            n = min(8, NT - 8 * g)
            wait("w_ps", g + 1)
            do(lambda: V.tensor_tensor(xv[:, 8 * g:8 * g + n], t3(bank[g % 2][:, 0:n * D]),
                                       wide_row(W["c_bout"], n), ALU.add), "w_taken")
        wait("w_taken", NG)
        link(lambda: V.tensor_tensor(h[:], h[:], y, ALU.add))
        rms_norm(xv, xv, yv, W["c_gout"])
        link(lambda: V.tensor_tensor(h[:], h[:], x[:], ALU.add))
        do(lambda: V.engine_nop(), "stage_done")

        layer_norm(xv, hv, t3(y_last))
        do(lambda: V.engine_nop(), "x_ready")
        if not dry:
            turn_back(dve, v_copy, 3, 0)
        wait("weights", w_count["d"])
        wait("route_ps", 2)
        route_in(W["d_bg"])
        link(lambda: V.tensor_reduce(st[0], L, AX.X, ALU.max))
        link(lambda: V.tensor_tensor(L, L, bc(st[0], EXPERTS), ALU.subtract))
        STEP["gate_exp"] = count[0]
        wait("route_exp", 2)
        link(lambda: V.tensor_reduce(st[0], L, AX.X, ALU.add))
        link(lambda: V.reciprocal(st[0], st[0]))
        link(lambda: V.tensor_tensor(L, L, bc(st[0], EXPERTS), ALU.mult))
        first_max(one1, L, st[1])
        link(lambda: V.tensor_tensor(wgt, L, one1, ALU.mult))
        do(lambda: V.engine_nop(), "route_done")
        for t in range(NT):
            wait("y_ps", EXPERTS * len(CHUNKS) + t + 1)
            combine(t, bank[4 + t % 4], NT + t + 1, t3(y_last))
        wait("y_sum", 2)
        link(lambda: V.tensor_tensor(h[:], h[:], y_last, ALU.add))
        do(lambda: V.engine_nop(), "stage_done")

    s["y_sum"] = sem("t_y_sum")
    dve_program(None, dry=True)

    def pool_program(pool):
        pass

    return sp_program, pe_program, act_program, dve_program, pool_program

def lay_out(inp, nq):
    f = {k: np.asarray(v) for k, v in inp.items()}
    io = dict(constants())
    x = f['x'][:nq*QI]
    x = x.reshape(nq, QI, SIDE, WJ, WQ, 3)
    io['x'] = np.ascontiguousarray(x.transpose(0, 4, 5, 3, 1, 2).reshape(nq, 12, NCH, CHUNK)
                                   .transpose(0, 2, 1, 3).reshape(nq, XROWS, CHUNK))
    def blockdiag(w, n):
        z = np.zeros((n, w.shape[0], n, w.shape[1]), w.dtype)
        for q in range(n): z[q, :, q] = w
        return z.reshape(n * w.shape[0], n * w.shape[1])
    fc0 = np.zeros((NCH, 12, NCH, 128), np.float32)
    for t in range(NCH):
        fc0[t, :, t] = blockdiag(f['L0_tok_fc0_w'], WQ)
    io['fc0_w'] = fc0.reshape(XROWS, NCH * 128)
    io['conv_w'] = np.concatenate([blockdiag(f['L0_tok_conv_w'][l].T, WQ) for l in range(LAYERS)], 1)
    col = lambda first, rest: np.ascontiguousarray(np.tile(np.concatenate([first[None], rest]), (1, WQ)).T)
    io['bias_in'] = col(f['L0_tok_fc0_b'], f['L0_tok_conv_b'])
    io['gain'] = col(f['L0_tok_ln0_g'], f['L0_tok_ln_g'])
    io['shift'] = col(f['L0_tok_ln0_b'], f['L0_tok_ln_b'])
    io['fc1_w'] = blockdiag(f['L0_tok_fc1_w'], WQ)
    io['fc1_b'] = f['L0_tok_fc1_b'][:, None]
    io['fc2_w'] = f['L0_tok_fc2_w']
    io['fc2_b'] = np.tile(f['L0_tok_fc2_b'], 2)[:, None]
    z = np.zeros((2, 64, 16, 32), np.float32)
    for pr in range(16):
        for e in range(2):
            z[e, :, pr, 2 * pr + e] = f['L0_tok_fc3_w'][:, 0]
    io['fc3_sel'] = z.reshape(128, 512)
    io['fc3_b'] = np.broadcast_to(f['L0_tok_fc3_b'][:, None], (32, 1))
    mw = np.zeros((LAYERS, 2, KY, CH, 2, KX, CH), np.float32)
    for kind, (a, b) in enumerate((('w1r', 'w2r'), ('w1i', 'w2i'))):
        wp, wm = f['L0_tok_' + a], f['L0_tok_' + b]
        mw[:, kind, :, :, 0, :12] = wp.transpose(0, 4, 1, 3, 2)
        mw[:, kind, :, :, 1, 1:] = wm[:, :, :, ::-1].transpose(0, 4, 1, 3, 2)
    io['mix_w'] = mw.reshape(LAYERS, 2, KY, CH, 2 * KX * CH)
    return {k: np.ascontiguousarray(v) for k, v in io.items()}


def lay_out_tail(inp):
    f = {k: np.asarray(v) for k, v in inp.items()}
    io = dict(tail_constants())
    over = lambda v: np.broadcast_to(v.reshape(1, -1), (128, v.size))
    w = f["L0_attn_w_qkv"].T
    io["a_wq"], io["a_wk"], io["a_wv"] = w[:, 0:64], w[:, 64:128], w[:, 128:192]
    io["a_wproj"] = f["L0_attn_w_proj"].T
    io["a_bproj"] = over(f["L0_attn_b_proj"])
    pos = np.arange(WIN)
    io["a_rel"] = np.tile(f["L0_attn_rel_bias"][pos[None, :] - pos[:, None] + WIN - 1], (2, 1))
    io["a_rel1"] = over(f["L0_attn_rel_bias"][WIN - 1:])
    io["b_gamma"], io["b_beta"] = over(f["L0_ffn_gamma"]), over(f["L0_ffn_beta"])
    io["b_wr"], io["b_br"] = f["L0_ffn_Wr"], over(f["L0_ffn_br"])
    io["b_w1"] = f["L0_ffn_W1"].transpose(1, 0, 2).reshape(D, -1)
    io["b_b1"] = f["L0_ffn_b1"].T
    io["b_w2"] = f["L0_ffn_W2"].transpose(1, 0, 2).reshape(HID, -1)
    io["b_b2"] = f["L0_ffn_b2"].reshape(1, -1)
    w, mem = f["L1_attn_w_qkv"], f["L1_attn_mem_kv"]
    io["c_wq"] = w[:, 0:128]
    io["c_wk"] = np.concatenate([w[:, 128:256], mem[0].reshape(128, MEM).T])
    io["c_wv"] = np.concatenate([w[:, 256:384], mem[1].reshape(128, MEM).T])
    io["c_wout"], io["c_bout"] = f["L1_attn_w_out"], over(f["L1_attn_b_out"])
    io["c_gout"], io["c_gpre"] = over(f["L1_attn_g_out"]), over(f["L1_attn_g_pre"])
    io["d_w1"] = f["L1_ffn_W1"]
    io["d_b1"] = f["L1_ffn_b1"].reshape(2, HID).T
    halves = lambda v: v.reshape(2, HID, -1).transpose(1, 0, 2).reshape(HID, -1)
    io["d_wg"], io["d_bg"] = halves(f["L1_ffn_Wg"]), over(f["L1_ffn_bg"])
    io["d_wd"] = halves(f["L1_ffn_Wd"].transpose(1, 0, 2))
    io["d_bd"] = f["L1_ffn_bd"].reshape(1, -1)
    io["cls"] = f["cls_tok"].reshape(1, -1)
    return {k: np.ascontiguousarray(v) for k, v in io.items()}


def build(nc, io, out, nq=32):
    with ExitStack() as ctx:
        bank = [ctx.enter_context(nc.psum_tensor(f"bank{n}", [128, CHUNK], F32)) for n in range(8)]

        def sem(name):
            return ctx.enter_context(nc.semaphore(name))

        tokens = nc.dram_tensor("tokens", [nq * QI * SEQ, D], F32, kind="Internal").ap()
        grid = tokens.rearrange("(q a e n) w -> q e n a w", a=2, e=2, n=SEQ)[:, :, 1:]
        with ExitStack() as first:
            tower = token_tower(
                nc, io, nq, bank, sem, lambda n, sh, dt: first.enter_context(nc.sbuf_tensor(n, sh, dt)),
                lambda n, sh, dt: nc.dram_tensor(n, sh, dt, kind="Internal").ap(), grid)
        ts = tower[0]

        def tower_done(sp):
            sp.dma_start(tokens.rearrange("(b n) w -> n b w", n=SEQ)[0],
                         io["cls"].to_broadcast([nq * QI, D])).then_inc(ts["cls_stored"], 16)
            sp.wait_ge(ts["cls_stored"], 16)
            sp.wait_ge(ts["tok_stored"], 32 * nq)

        rest = token_transformer(
            nc, io, bank, sem, lambda n, sh, dt: ctx.enter_context(nc.sbuf_tensor(n, sh, dt)), tower_done,
            tokens, out.rearrange("b n d -> (b n) d").rearrange("(t p) d -> p t d", p=128))
        block = ctx.enter_context(nc.Block())

        @block.sync
        def _(sp):
            tower[1](sp)
            rest[0](sp)

        @block.tensor
        def _(pe):
            tower[2](pe)
            rest[1](pe)

        @block.scalar
        def _(act):
            tower[3](act)
            rest[2](act)

        @block.vector
        def _(dve):
            tower[4](dve)
            rest[3](dve)

        @block.gpsimd
        def _(pool):
            tower[5](pool)


def kernel(**inputs):
    import concourse.bacc as bacc
    from concourse.bass_utils import run_bass_kernel_spmd

    nc = bacc.Bacc("TRN2", target_bir_lowering=False, num_devices=1)
    arrays = {f"in_{k}": v for k, v in {**lay_out(inputs, 32), **lay_out_tail(inputs)}.items()}
    io = {k[3:]: nc.dram_tensor(k, v.shape, mybir.dt.from_np(v.dtype), kind="ExternalInput").ap()
          for k, v in arrays.items()}
    out = nc.dram_tensor("out", (128, SEQ, D), F32, kind="ExternalOutput").ap()
    build(nc, io, out)
    return run_bass_kernel_spmd(nc, [arrays], core_ids=[0]).results[0]["out"]
```
